# Optimizing a Trainium2 kernel written in Bass

```python
import numpy as np
import jax
import jax.numpy as jnp

def _softmax(x, axis=-1):
    return jax.nn.softmax(x, axis=axis)

def _gelu(x):
    return jax.nn.gelu(x, approximate=True)

def _silu(x):
    return jax.nn.silu(x)

def _sigmoid(x):
    return jax.nn.sigmoid(x)

def _layernorm(x, axis=-1, eps=1e-05):
    m = jnp.mean(x, axis=axis, keepdims=True)
    v = jnp.var(x, axis=axis, keepdims=True)
    return (x - m) / jnp.sqrt(v + eps)

def _scatter_add(tgt, idx, src, axis=0):
    return tgt.at[idx].add(src)

def _segment_sum(src, seg, n):
    return jax.ops.segment_sum(src, seg, n)
kernel_name = 'mk_gnn_preln_d2_gnn_r32_5655b1'

def setup_inputs(seed: int=0):
    np.random.seed(seed)
    _w = jnp.asarray

    def _rec_inputs():
        import jax
        import jax.numpy as jnp
        _gk = jax.random.key(seed)
        x = -0.0003713 + 1 * jax.random.normal(jax.random.fold_in(_gk, 1), (50000, 256), jnp.float32)
        _s = jax.random.randint(jax.random.fold_in(_gk, 2), (12500,), 0, 50000, jnp.int32)
        _d = jax.random.randint(jax.random.fold_in(_gk, 3), (12500,), 0, 50000, jnp.int32)
        _loop = jnp.arange(50000, dtype=jnp.int32)
        src = jnp.concatenate([_s, _d, _loop])
        dst = jnp.concatenate([_d, _s, _loop])
        _o = jnp.argsort(dst, stable=True)
        src = src[_o]
        dst = dst[_o]
        return (x, src, dst)
    x, src, dst = _rec_inputs()

    def _L0_gnn_setup():
        import jax, jax.numpy as jnp
        import numpy as np
        N = 50000
        E = 25000
        DIM = 256
        H = 8
        D = DIM // H
        key = jax.random.key(seed)
        ks = jax.random.split(key, 12)
        s = 1.0 / np.sqrt(DIM)
        return {'x': jax.random.normal(ks[0], (N, DIM), dtype=jnp.float32), 'Wq': jax.random.normal(ks[1], (DIM, DIM), dtype=jnp.float32) * s, 'bq': jax.random.normal(ks[2], (DIM,), dtype=jnp.float32) * 0.01, 'Wk': jax.random.normal(ks[3], (DIM, DIM), dtype=jnp.float32) * s, 'bk': jax.random.normal(ks[4], (DIM,), dtype=jnp.float32) * 0.01, 'Wv': jax.random.normal(ks[5], (DIM, DIM), dtype=jnp.float32) * s, 'bv': jax.random.normal(ks[6], (DIM,), dtype=jnp.float32) * 0.01, 'Wo': jax.random.normal(ks[7], (DIM, DIM), dtype=jnp.float32) * s, 'bo': jax.random.normal(ks[8], (DIM,), dtype=jnp.float32) * 0.01, 'src': jax.random.randint(ks[9], (E,), 0, N, dtype=jnp.int32), 'dst': jax.random.randint(ks[10], (E,), 0, N, dtype=jnp.int32)}
    _L0_gnn_all = _L0_gnn_setup()
    _L0_gnn_in = {k: v for k, v in _L0_gnn_all.items() if k in ('Wq', 'bq', 'Wk', 'bk', 'Wv', 'bv', 'Wo', 'bo')}
    del _L0_gnn_all

    def _L1_gnn_setup():
        import jax, jax.numpy as jnp
        import numpy as np
        N, E, D, L = (50000, 50000, 256, 3)
        EPS = 1e-05
        key = jax.random.key(seed)
        ks = jax.random.split(key, 10)
        x = jax.random.normal(ks[0], (N, D), dtype=jnp.float32)
        edge_index = jax.random.randint(ks[1], (2, E), 0, N, dtype=jnp.int32)
        mask_embed = jax.random.normal(ks[2], (D,), dtype=jnp.float32)
        s = 1.0 / np.sqrt(D)
        Wl = jax.random.normal(ks[3], (L, D, D), dtype=jnp.float32) * s
        Wr = jax.random.normal(ks[4], (L, D, D), dtype=jnp.float32) * s
        b = jax.random.normal(ks[5], (L, D), dtype=jnp.float32) * 0.01
        gamma = 1.0 + 0.1 * jax.random.normal(ks[6], (L, D), dtype=jnp.float32)
        beta = 0.1 * jax.random.normal(ks[7], (L, D), dtype=jnp.float32)
        rmean = 0.1 * jax.random.normal(ks[8], (L, D), dtype=jnp.float32)
        rvar = 0.5 + jax.random.uniform(ks[9], (L, D), dtype=jnp.float32)
        return {'x': x, 'edge_index': edge_index, 'mask_embed': mask_embed, 'Wl': Wl, 'Wr': Wr, 'b': b, 'gamma': gamma, 'beta': beta, 'rmean': rmean, 'rvar': rvar}
    _L1_gnn_all = _L1_gnn_setup()
    _L1_gnn_in = {k: v for k, v in _L1_gnn_all.items() if k in ('mask_embed', 'Wl', 'Wr', 'b', 'gamma', 'beta', 'rmean', 'rvar')}
    del _L1_gnn_all
    return {'x': x, 'src': src, 'dst': dst, 'L0_gnn_Wq': _L0_gnn_in['Wq'], 'L0_gnn_bq': _L0_gnn_in['bq'], 'L0_gnn_Wk': _L0_gnn_in['Wk'], 'L0_gnn_bk': _L0_gnn_in['bk'], 'L0_gnn_Wv': _L0_gnn_in['Wv'], 'L0_gnn_bv': _L0_gnn_in['bv'], 'L0_gnn_Wo': _L0_gnn_in['Wo'], 'L0_gnn_bo': _L0_gnn_in['bo'], 'L1_gnn_mask_embed': _L1_gnn_in['mask_embed'], 'L1_gnn_Wl': _L1_gnn_in['Wl'], 'L1_gnn_Wr': _L1_gnn_in['Wr'], 'L1_gnn_b': _L1_gnn_in['b'], 'L1_gnn_gamma': _L1_gnn_in['gamma'], 'L1_gnn_beta': _L1_gnn_in['beta'], 'L1_gnn_rmean': _L1_gnn_in['rmean'], 'L1_gnn_rvar': _L1_gnn_in['rvar']}

def reference(x, src, dst, L0_gnn_Wq, L0_gnn_bq, L0_gnn_Wk, L0_gnn_bk, L0_gnn_Wv, L0_gnn_bv, L0_gnn_Wo, L0_gnn_bo, L1_gnn_mask_embed, L1_gnn_Wl, L1_gnn_Wr, L1_gnn_b, L1_gnn_gamma, L1_gnn_beta, L1_gnn_rmean, L1_gnn_rvar):
    import jax
    import jax.numpy as jnp

    def _L0_gnn_ref(x, Wq, bq, Wk, bk, Wv, bv, Wo, bo, src, dst):
        import jax, jax.numpy as jnp
        import numpy as np
        N = 50000
        E = 25000
        DIM = 256
        H = 8
        D = DIM // H
        q = (x @ Wq.T + bq).reshape(N, H, D)
        k = (x @ Wk.T + bk).reshape(N, H, D)
        v = (x @ Wv.T + bv).reshape(N, H, D)
        scores = jnp.einsum('ehd,ehd->eh', q[src], k[dst]) / jnp.sqrt(jnp.float32(D))
        smax = jax.ops.segment_max(scores, dst, num_segments=N)
        e = jnp.exp(scores - smax[dst])
        ssum = jax.ops.segment_sum(e, dst, num_segments=N)
        probs = e / ssum[dst]
        out = jax.ops.segment_sum(v[src] * probs[:, :, None], dst, num_segments=N)
        out = out.reshape(N, DIM)
        return out @ Wo.T + bo

    def _L1_gnn_ref(x, edge_index, mask_embed, Wl, Wr, b, gamma, beta, rmean, rvar):
        import jax, jax.numpy as jnp
        import numpy as np
        N, E, D, L = (50000, 50000, 256, 3)
        EPS = 1e-05
        src, dst = (edge_index[0], edge_index[1])
        h = x.at[0].set(mask_embed)
        deg = jax.ops.segment_sum(jnp.ones((src.shape[0],), h.dtype), dst, num_segments=N)
        deg = jnp.maximum(deg, 1.0)[:, None]
        for i in range(L):
            agg = jax.ops.segment_sum(h[src], dst, num_segments=N) / deg
            z = agg @ Wl[i] + b[i] + h @ Wr[i]
            z = (z - rmean[i]) * jax.lax.rsqrt(rvar[i] + EPS) * gamma[i] + beta[i]
            if i != L - 1:
                z = jax.nn.relu(z)
            z = z + h
            h = z
        return h
    edge_index = jnp.stack([src, dst])
    h = jnp.maximum(_layernorm(x, axis=-1), 0.0)
    x = x + _L0_gnn_ref(h, L0_gnn_Wq, L0_gnn_bq, L0_gnn_Wk, L0_gnn_bk, L0_gnn_Wv, L0_gnn_bv, L0_gnn_Wo, L0_gnn_bo, src, dst)
    h = jnp.maximum(_layernorm(x, axis=-1), 0.0)
    x = x + _L1_gnn_ref(h, edge_index, L1_gnn_mask_embed, L1_gnn_Wl, L1_gnn_Wr, L1_gnn_b, L1_gnn_gamma, L1_gnn_beta, L1_gnn_rmean, L1_gnn_rvar)
    return x

_drawn_inputs = setup_inputs


def setup_inputs(seed=0):
    import zlib

    import numpy as np

    out = dict(_drawn_inputs(seed))
    spreads = {}
    factors = {'L0_gnn_bq': 64.0,
     'L0_gnn_bk': 64.0,
     'L0_gnn_bv': 8.0,
     'L0_gnn_bo': 8.0,
     'L1_gnn_mask_embed': 8.0,
     'L1_gnn_b': 8.0}
    for name, (base, spread) in spreads.items():
        noise = np.random.default_rng([zlib.crc32(name.encode()), seed]).standard_normal(out[name].shape)
        drawn = base * np.exp(spread * noise) if base else spread * noise
        out[name] = jnp.asarray(drawn.astype(out[name].dtype))
    for name, factor in factors.items():
        out[name] = (out[name] * factor).astype(out[name].dtype)
    return out
```

```python
from contextlib import ExitStack

import concourse.bass as bass
from concourse import mybir

F32 = mybir.dt.float32
F32R = mybir.dt.float32r
I32 = mybir.dt.int32
ALU = mybir.AluOpType
ACT = mybir.ActivationFunctionType
AX = mybir.AxisListType

P = 128
QT = 4
BODY = 2 * QT
SKIP = 1 << 20
NEG = 1.0e30
EPS = 1e-5


class Plan:

    def __init__(self, n, e, d, heads):
        self.N, self.E, self.D, self.H = n, e, d, heads
        self.hd = d // heads
        self.C = d // P
        self.turns = -(-n // (P * BODY))
        self.NT = self.turns * BODY
        self.NP = self.NT * P
        self.QR = QT * P
        self.last_rows = n - (self.turns - 1) * BODY * P - self.QR
        assert 0 < self.last_rows <= self.QR
        self.EC = -(-e // P)
        self.EB = -(-self.EC // 16) * 16
        self.e_tail = e - (P - 1) * self.EC
        assert 0 < self.e_tail <= self.EC


def quad_rows(t, base, cols=None):
    v = t[bass.ds(base, QT * P), :] if cols is None else t[bass.ds(base, QT * P), cols[0]:cols[1]]
    return v.rearrange("(t p) d -> p t d", p=P)


def ragged(table, base, rows, tile):
    full, rest = rows // P, rows % P
    out = []
    if rest:
        out.append((table[base + full * P:base + rows, :], tile[0:rest, full, :]))
    if full:
        out.append((table[base:base + full * P, :].rearrange("(t p) d -> p t d", p=P), tile[:, 0:full, :]))
    return out


def constants(nc, ctx, pl):
    c = {}
    for name, shape, dt in (("ident", [P, P], F32), ("ones", [P, P], F32), ("iota", [P, P], F32),
                            ("eps", [P, 1], F32), ("links", [P, pl.NT, 2], I32), ("dloc", [P, pl.NT], F32),
                            ("deg", [P, pl.NT], F32), ("inv_deg", [P, pl.NT], F32)):
        c[name] = ctx.enter_context(nc.sbuf_tensor(name, shape, dt))
    return c


def edge_tables(nc, pl, con, src, dst, link_dram, idx_out, pay_out):
    EC, NT = pl.EC, pl.NT
    with ExitStack() as ctx:
        def sb(n, s, d=F32):
            return ctx.enter_context(nc.sbuf_tensor(n, s, d))

        def sem(n):
            return ctx.enter_context(nc.semaphore(n))
        dst_i, src_i = sb("dst_i", [P, EC + 2], I32), sb("src_i", [P, EC], I32)
        tb_i, e_i = sb("tb_i", [P, EC + 2], I32), sb("e_i", [P, EC], I32)
        iota_i = sb("iota_i", [P, P], I32)
        d, s, tb, e = sb("d_f", [P, EC + 2]), sb("s_f", [P, EC]), sb("tb_f", [P, EC + 2]), sb("e_f", [P, EC])
        first, start, slot = sb("first", [P, EC]), sb("start", [P, EC]), sb("slot", [P, EC])
        loop, link, tmp = sb("loop", [P, EC]), sb("link", [P, EC]), sb("tmp", [P, EC])
        row_in, row, carry = sb("row_in", [1, P]), sb("row", [1, P + 1]), sb("carry", [P, 1])
        empty = sb("empty", [P, NT, 2], I32)
        ps_row = ctx.enter_context(nc.psum_tensor("ps_row", [P, 512], F32))
        ps_col = ctx.enter_context(nc.psum_tensor("ps_col", [P, 512], F32))
        padded, edges_in, pool_ready, step = sem("padded"), sem("edges_in"), sem("pool_ready"), sem("step")
        row_up, row_back, row_ready, empty_out, ident_clear = (
            sem("row_up"), sem("row_back"), sem("row_ready"), sem("empty_out"), sem("ident_clear"))
        start_ready = sem("start_ready")
        block = ctx.enter_context(nc.Block())

        @block.sync
        def _(sp):
            sp.wait_ge(padded, 1)
            flat = lambda a, n: a.rearrange("(p c) -> p c", c=n)
            sp.dma_start(dst_i[0:1, 1:EC + 2], flat(dst[0:EC + 1], EC + 1)).then_inc(edges_in, 16)
            mid = dst[EC - 1:EC - 1 + (P - 2) * EC]
            sp.dma_start(dst_i[1:P - 1, 0:EC], flat(mid, EC)).then_inc(edges_in, 16)
            with nc.allow_non_contiguous_dma("the two neighbours past a partition's edges"):
                tail = dst[2 * EC - 1:2 * EC - 1 + (P - 3) * EC].rearrange("(p c) -> p c", c=EC)
                sp.dma_start(dst_i[1:P - 2, EC:EC + 2], tail[:, 0:2]).then_inc(edges_in, 16)
                at = (P - 1) * EC - 1
                sp.dma_start(dst_i[P - 2:P - 1, EC:EC + 2], flat(dst[at:at + 2], 2)).then_inc(edges_in, 16)
            sp.dma_start(dst_i[P - 1:P, 0:pl.e_tail + 1],
                         flat(dst[(P - 1) * EC - 1:pl.E], pl.e_tail + 1)).then_inc(edges_in, 16)
            sp.dma_start(src_i[0:P - 1, :], flat(src[0:(P - 1) * EC], EC)).then_inc(edges_in, 16)
            sp.dma_start(src_i[P - 1:P, 0:pl.e_tail],
                         flat(src[(P - 1) * EC:pl.E], pl.e_tail)).then_inc(edges_in, 16)
            sp.wait_ge(padded, 2)
            sp.dma_start(link_dram.rearrange("(p t) w -> p (t w)", p=P),
                         empty[:].rearrange("p t w -> p (t w)")).then_inc(empty_out, 16)
            sp.wait_ge(empty_out, 16)

        @block.gpsimd
        def _(pool):
            nc.gpsimd.iota(iota_i[:], pattern=[[1, P]], base=0, channel_multiplier=0)
            nc.gpsimd.iota(e_i[:], pattern=[[1, EC]], base=0, channel_multiplier=EC).then_inc(pool_ready, 1)
            nc.gpsimd.memset(con["ones"][:], 1.0)
            nc.gpsimd.memset(con["eps"][:], EPS)
            nc.gpsimd.memset(con["ident"][:], 0.0).then_inc(ident_clear, 1)
            pool.wait_ge(ident_clear, 1)
            nc.gpsimd.affine_select(out=con["ident"][:], in_=con["ident"][:], compare_op=ALU.not_equal, fill=1.0,
                                    base=0, pattern=[[-1, P]], channel_multiplier=1).then_inc(pool_ready, 1)

        @block.tensor
        def _(pe):
            pe.wait_ge(pool_ready, 2)
            pe.wait_ge(start_ready, 1)
            nc.tensor.transpose(ps_row[0:1, 0:P], start[:, EC - 1:EC], con["ident"][:]).then_inc(row_up, 1)
            pe.wait_ge(row_ready, 1)
            nc.tensor.matmul(ps_col[:, 0:1], row[0:1, 0:P], con["ones"][0:1, 0:1],
                             start=True, stop=True).then_inc(row_back, 1)

        @block.vector
        def _(dve):
            n = [0]

            def then(ins):
                n[0] += 1
                ins.then_inc(step, 1)
                dve.wait_ge(step, n[0])
            V = nc.vector
            V.memset(dst_i[:], pl.NP)
            then(V.memset(src_i[:], 0))
            V.memset(dst_i[0:1, 0:1], -1).then_inc(padded, 1)
            V.memset(empty[:, :, 0], SKIP)
            V.memset(empty[:, :, 1], -1).then_inc(padded, 1)
            V.memset(idx_out[:], SKIP)
            V.memset(pay_out[:], 0)
            V.memset(row[:], 0.0)
            dve.wait_ge(pool_ready, 1)
            V.tensor_copy(con["iota"][:], iota_i[:])
            V.tensor_copy(e[:], e_i[:])
            dve.wait_ge(edges_in, 7 * 16)
            V.tensor_copy(d[:], dst_i[:])
            V.tensor_copy(s[:], src_i[:])
            then(V.tensor_scalar(tb_i[:], dst_i[:], 7, 7, ALU.arith_shift_right, ALU.logical_shift_left))
            then(V.tensor_copy(tb[:], tb_i[:]))
            own, prev, nxt = slice(1, EC + 1), slice(0, EC), slice(2, EC + 2)
            then(V.tensor_tensor(first[:], tb[:, own], tb[:, prev], ALU.not_equal))
            then(V.tensor_tensor(first[:], first[:], e[:], ALU.mult))
            V.tensor_tensor_scan(start[:], first[:], first[:], 0.0, ALU.max, ALU.max).then_inc(start_ready, 1)
            dve.wait_ge(row_up, 1)
            then(V.tensor_copy(row_in[:], ps_row[0:1, 0:P]))
            V.tensor_tensor_scan(row[0:1, 1:P + 1], row_in[:], row_in[:], 0.0,
                                 ALU.max, ALU.max).then_inc(row_ready, 1)
            dve.wait_ge(row_back, 1)
            then(V.tensor_copy(carry[:], ps_col[:, 0:1]))
            then(V.tensor_scalar(start[:], start[:], carry[:, 0:1], None, ALU.max))
            then(V.tensor_tensor(slot[:], e[:], d[:, own], ALU.subtract))
            then(V.tensor_tensor(slot[:], slot[:], start[:], ALU.subtract))
            then(V.tensor_tensor(slot[:], slot[:], tb[:, own], ALU.add))
            then(V.tensor_tensor(loop[:], d[:, own], d[:, nxt], ALU.not_equal))
            then(V.tensor_tensor(tmp[:], d[:, own], s[:], ALU.is_equal))
            then(V.tensor_tensor(loop[:], loop[:], tmp[:], ALU.mult))
            then(V.tensor_scalar(link[:], e[:], float(pl.E), None, ALU.is_lt))
            then(V.tensor_tensor(link[:], link[:], loop[:], ALU.subtract))
            then(V.tensor_scalar(tmp[:], tb[:, own], 1.0 / P, float(SKIP), ALU.mult, ALU.add))
            then(V.scalar_tensor_tensor(out=tmp[:], in0=slot[:], scalar=float(NT), in1=tmp[:],
                                        op0=ALU.mult, op1=ALU.add))
            then(V.scalar_tensor_tensor(out=idx_out[:, 0:EC], in0=link[:], scalar=-float(SKIP), in1=tmp[:],
                                        op0=ALU.mult, op1=ALU.add))
            V.tensor_copy(pay_out[:, 0:EC, 0], src_i[:])
            then(V.tensor_tensor(pay_out[:, 0:EC, 1], d[:, own], tb[:, own], ALU.subtract))


def project(nc, pl, con, x, weights, biases, qv_dram, ks_dram, link_dram, idx, pay):
    D, C, H, hd = pl.D, pl.C, pl.H, pl.hd
    KW = D + H
    with ExitStack() as ctx:
        def sb(n, s, d=F32):
            return ctx.enter_context(nc.sbuf_tensor("proj_" + n, s, d))

        def ps(n):
            return ctx.enter_context(nc.psum_tensor("proj_" + n, [P, 512], F32))

        def sem(n):
            return ctx.enter_context(nc.semaphore("proj_" + n))
        wraw = sb("wraw", [P, 3 * C, D])
        wT = sb("wT", [P, C, 3 * D])
        bias = sb("bias", [P, 3 * D])
        xq = [sb(f"xq{u}", [P, QT, D]) for u in range(2)]
        st, mv = sb("st", [P, 2, QT, 6]), sb("mv", [P, 2, QT, 2])
        sd, rstd, nmr = sb("sd", [P, 2, QT]), sb("rstd", [P, 2, QT]), sb("nmr", [P, 2, QT])
        h = sb("h", [P, 2, D])
        hT = sb("hT", [P, 2, D])
        prod = sb("prod", [P, D])
        qv = [sb(f"qv{u}", [P, QT, 2 * D]) for u in range(2)]
        ks = [sb(f"ks{u}", [P, QT, KW]) for u in range(2)]
        sidx, spay = sb("sidx", [P, 2, 8], I32), sb("spay", [P, 2, 16], I32)
        psT, psQK, psV = [ps(f"psT{b}") for b in range(2)], [ps(f"psQK{b}") for b in range(2)], [ps(f"psV{b}") for b in range(2)]
        w_in, w_up, w_ready, x_clear = sem("w_in"), sem("w_up"), sem("w_ready"), sem("x_clear")
        tail_in = sem("tail_in")
        x_in = [sem(f"x_in{u}") for u in range(2)]
        qv_out = [sem(f"qv_out{u}") for u in range(2)]
        h_free_of_x = sem("x_read")
        stats, var, std, rs, norm = sem("stats"), sem("var"), sem("std"), sem("rs"), sem("norm")
        h_ready, hT_up, hT_ready, qkv_up, qkv_read, ks_step = (sem("h_ready"), sem("hT_up"), sem("hT_ready"),
                                                      sem("qkv_up"), sem("qkv_read"), sem("ks_step"))
        prod_ready = sem("prod_ready")
        qv_ready = sem("qv_ready")
        passed = sem("passed")
        staged, scattered = sem("staged"), [sem(f"scattered{b}") for b in range(2)]
        block = ctx.enter_context(nc.Block())
        last = pl.turns - 1

        @block.sync
        def _(sp):
            for m, w in enumerate(weights):
                for c in range(C):
                    sp.dma_start(wraw[:, m * C + c, :], w[c * P:(c + 1) * P, :]).then_inc(w_in, 16)
            for m, b in enumerate(biases):
                sp.dma_start(bias[:, m * D:(m + 1) * D],
                             b.rearrange("(o d) -> o d", o=1).to_broadcast([P, D])).then_inc(w_in, 16)
            sp.wait_ge(x_clear, 1)

            def load(i, u):
                sp.wait_ge(h_free_of_x, 2 * i + u + 1)
                sp.dma_start(xq[u][:], quad_rows(x, i * (BODY * P) + u * pl.QR)).then_inc(x_in[u], 16)

            def store(i, u):
                sp.wait_ge(qv_ready, 2 * i + u + 1)
                at = i * (BODY * P) + u * pl.QR
                sp.dma_start(quad_rows(qv_dram, at), qv[u][:]).then_inc(qv_out[u], 16)
                sp.dma_start(quad_rows(ks_dram, at), ks[u][:]).then_inc(qv_out[u], 16)
            sp.sem_inc(qv_out[0], 32)
            sp.sem_inc(qv_out[1], 32)
            load(0, 0)
            with sp.Fori(0, last) as i:
                load(i, 1)
                store(i, 0)
                load(i + 1, 0)
                store(i, 1)
            sp.wait_ge(h_free_of_x, 2 * last + 2)
            parts = ragged(x, last * BODY * P + pl.QR, pl.last_rows, xq[1])
            for dram, tile in parts[:-1]:
                sp.dma_start(tile, dram).then_inc(tail_in, 16)
            if len(parts) > 1:
                sp.wait_ge(tail_in, 16)
            sp.dma_start(parts[-1][1], parts[-1][0]).then_inc(x_in[1], 16)
            store(last, 0)
            store(last, 1)
            for u in range(2):
                sp.wait_ge(qv_out[u], 32 * (pl.turns + 1))

        @block.gpsimd
        def _(pool):
            bound = pool.to_reg(P * pl.NT - 1)

            def scatter(i, b, first):
                if not first:
                    pool.wait_ge(scattered[b], i * 128)
                nc.gpsimd.tensor_copy(sidx[:, b, :], idx[:, bass.ds(i * 16 + b * 8, 8)])
                nc.gpsimd.tensor_copy(spay[:, b, :],
                                      pay[:].rearrange("p e w -> p (e w)")[:, bass.ds(i * 32 + b * 16, 16)]
                                      ).then_inc(staged, 1)
                pool.wait_ge(staged, i * 2 + b + 1)
                pool.sem_inc(passed, 1)
                for c in range(8):
                    nc.gpsimd.indirect_dma_start(
                        out=link_dram[:, :], out_offset=bass.IndirectOffsetOnAxis(ap=sidx[:, b, c:c + 1], axis=0),
                        in_=spay[:, b, 2 * c:2 * c + 2], in_offset=None,
                        bounds_check=bound, oob_is_err=False).then_inc(scattered[b], 16)
            scatter(0, 0, True)
            scatter(0, 1, True)
            with pool.Fori(1, pl.EB // 16) as i:
                scatter(i, 0, False)
                scatter(i, 1, False)
            for b in range(2):
                pool.wait_ge(scattered[b], 128 * (pl.EB // 16))

        def tiles(body):
            return [body(k) for k in range(BODY)]

        @block.tensor
        def _(pe):
            pe.wait_ge(w_in, 16 * 3 * (C + 1))
            for m in range(3):
                for c in range(C):
                    for r in range(C):
                        n = (m * C + c) * C + r
                        if n >= 2:
                            pe.wait_ge(w_ready, n - 1)
                        nc.tensor.transpose(psT[n % 2][:, 0:P], wraw[:, m * C + c, r * P:(r + 1) * P],
                                            con["ident"][:]).then_inc(w_up, 1)
            pe.wait_ge(w_ready, 3 * C * C)
            pe.sem_inc(hT_up, 2)

            def up(n, b):
                pe.wait_ge(h_ready, n + 1)
                pe.wait_ge(hT_ready, n + 1)
                for c in range(C):
                    ins = nc.tensor.transpose(psT[b][:, c * P:(c + 1) * P], h[:, b, c * P:(c + 1) * P], con["ident"][:])
                ins.then_inc(hT_up, 1)

            def products(n, b):
                pe.wait_ge(hT_ready, n + 3)
                pe.wait_ge(qkv_read, n + 1)
                for c in range(C):
                    nc.tensor.matmul(psQK[b][:, :], hT[:, b, c * P:(c + 1) * P], wT[:, c, 0:2 * D],
                                     start=(c == 0), stop=(c == C - 1))
                for c in range(C):
                    ins = nc.tensor.matmul(psV[b][:, 0:D], hT[:, b, c * P:(c + 1) * P], wT[:, c, 2 * D:3 * D],
                                           start=(c == 0), stop=(c == C - 1))
                ins.then_inc(qkv_up, 1)
            up(0, 0)

            def turn(i, end):
                for k in range(BODY):
                    n = i * BODY + k
                    if not (end and k == BODY - 1):
                        up(n + 1, (k + 1) % 2)
                    products(n, k % 2)
            with pe.Fori(0, last) as i:
                turn(i, False)
            turn(last, True)

        @block.scalar
        def _(act):
            n = 0
            for m in range(3):
                for c in range(C):
                    for r in range(C):
                        act.wait_ge(w_up, n + 1)
                        nc.scalar.copy(wT[:, r, m * D + c * P:m * D + (c + 1) * P], psT[n % 2][:, 0:P]).then_inc(w_ready, 1)
                        n += 1
            act.sem_inc(hT_ready, 2)
            act.sem_inc(h_free_of_x, 2)

            def deviation(i, u):
                act.wait_ge(var, 2 * i + u + 1)
                nc.scalar.activation(sd[:, u, :], mv[:, u, :, 1], ACT.Sqrt, bias=con["eps"][:, 0:1]).then_inc(std, 1)

            def normalize(i, k):
                u, t, n = k // QT, k % QT, i * BODY + k
                if t == 0:
                    act.wait_ge(norm, 2 * i + u + 1)
                act.wait_ge(hT_up, n + 1)
                ins = nc.scalar.activation(h[:, k % 2, :], xq[u][:, t, :], ACT.Relu,
                                           bias=nmr[:, u, t:t + 1], scale=rstd[:, u, t:t + 1])
                ins.then_inc(h_ready, 1)
                if t == QT - 1:
                    act.wait_ge(h_ready, n + 1)
                    act.sem_inc(h_free_of_x, 1)

            def keep(i, k):
                n = i * BODY + k
                act.wait_ge(hT_up, n + 3)
                act.wait_ge(qkv_up, n + 1)
                nc.scalar.copy(hT[:, k % 2, :], psT[k % 2][:, 0:D]).then_inc(hT_ready, 1)
            deviation(0, 0)

            def turn(i, end):
                for k in range(BODY):
                    normalize(i, k)
                    if k == 1:
                        deviation(i, 1)
                    if k == QT + 1 and not end:
                        deviation(i + 1, 0)
                    keep(i, k)
            with act.Fori(0, last) as i:
                turn(i, False)
            turn(last, True)

        @block.vector
        def _(dve):
            V = nc.vector
            V.memset(xq[1][:], 0.0).then_inc(x_clear, 1)
            dve.sem_inc(qkv_read, 2)
            dve.wait_ge(w_in, 16 * 3 * (C + 1))
            dve.sem_inc(qkv_up, 2)

            def statistics(i, u):
                q = 2 * i + u
                dve.wait_ge(x_in[u], i * 16 + 16)
                for t in range(QT):
                    ins = V.bn_stats(st[:, u, t, :], xq[u][:, t, :])
                ins.then_inc(stats, 1)
                dve.wait_ge(stats, q + 1)
                dve.sem_inc(passed, 1)
                for t in range(QT):
                    ins = V.bn_aggr(mv[:, u, t, :], st[:, u, t, :])
                ins.then_inc(var, 1)

            def shift(i, u):
                q = 2 * i + u
                dve.wait_ge(std, q + 1)
                V.reciprocal(rstd[:, u, :], sd[:, u, :]).then_inc(rs, 1)
                dve.wait_ge(rs, q + 1)
                V.scalar_tensor_tensor(out=nmr[:, u, :], in0=mv[:, u, :, 0], scalar=-1.0, in1=rstd[:, u, :],
                                       op0=ALU.mult, op1=ALU.mult).then_inc(norm, 1)

            def collect(i, k):
                u, t, n, b = k // QT, k % QT, i * BODY + k, k % 2
                dve.wait_ge(qkv_up, n + 3)
                if t == 0:
                    dve.wait_ge(qv_out[u], i * 32 + 32)
                V.tensor_tensor(qv[u][:, t, 0:D], psQK[b][:, 0:D], bias[:, 0:D], ALU.add)
                V.tensor_tensor(ks[u][:, t, 0:D], psQK[b][:, D:2 * D], bias[:, D:2 * D], ALU.add).then_inc(ks_step, 1)
                V.tensor_tensor(qv[u][:, t, D:2 * D], psV[b][:, 0:D], bias[:, 2 * D:3 * D], ALU.add).then_inc(qkv_read, 1)
                dve.wait_ge(ks_step, n + 1)
                V.tensor_tensor(prod[:], qv[u][:, t, 0:D], ks[u][:, t, 0:D], ALU.mult).then_inc(prod_ready, 1)
                dve.wait_ge(prod_ready, n + 1)
                ins = V.tensor_reduce(ks[u][:, t, D:KW], prod[:].rearrange("p (h d) -> p h d", h=H), AX.X, ALU.add)
                if t == QT - 1:
                    ins.then_inc(qv_ready, 1)
            statistics(0, 0)
            shift(0, 0)

            def turn(i, end):
                for k in range(BODY):
                    if k == 0:
                        statistics(i, 1)
                    if k == QT and not end:
                        statistics(i + 1, 0)
                    collect(i, k)
                    if k == 1:
                        shift(i, 1)
                    if k == QT + 1 and not end:
                        shift(i + 1, 0)
            with dve.Fori(0, last) as i:
                turn(i, False)
            turn(last, True)


def attend(nc, pl, con, x, w_out, b_out, qv_dram, ks_dram, link_dram, mask_embed, x1_dram, h_dram):
    D, C, H, hd, NT = pl.D, pl.C, pl.H, pl.hd, pl.NT
    KW, QH = D + H, QT * H
    SCALE = float(hd) ** -0.5
    with ExitStack() as ctx:
        def sb(n, s, d=F32):
            return ctx.enter_context(nc.sbuf_tensor("att_" + n, s, d))

        def ps(n):
            return ctx.enter_context(nc.psum_tensor("att_" + n, [P, 512], F32))

        def sem(n):
            return ctx.enter_context(nc.semaphore("att_" + n))
        wraw, wT, bias = sb("wo_raw", [P, C, D]), sb("woT", [P, C, D]), sb("bo", [P, D])
        rows = [sb(f"rows{u}", [P, QT, 2 * D]) for u in range(2)]
        ks = [sb(f"ksn{u}", [P, QT, KW]) for u in range(2)]
        xs = [sb(f"xs{u}", [P, QT, D]) for u in range(2)]
        vs = [sb(f"vs{u}", [P, QT, D]) for u in range(2)]
        hot = [sb(f"hot{u}", [P, QT, P]) for u in range(2)]
        lidx, ldst = sb("lidx", [P, 2, QT], I32), sb("ldst", [P, 2, QT])
        hotT = sb("hotT", [P, 2, P])
        prod, pv = sb("prod", [P, 2, D]), sb("pv", [P, 2, D])
        slot_sc = sb("slot_sc", [P, 3, QT, H])
        tsc = sb("tsc", [QH, 3, P])
        same, cut = sb("same", [QH, P + 1]), sb("cut", [QH, P + 1])
        top, fwd, bwd = sb("top", [QH, P]), sb("fwd", [QH, P]), sb("bwd", [QH, P])
        dif, ex, tot = sb("dif", [QH, 2, P]), sb("ex", [QH, 2, P]), sb("tot", [QH, P])
        tp = sb("tp", [QH, 3, P])
        pr = sb("pr", [P, QT, H])
        fin = sb("fin", [P, QT, 2 * H + 1])
        own = sb("own", [P, QT, 2 * H + 1])
        pself = sb("pself", [P, QT, H])
        vself = sb("vself", [P, QT, D])
        o, oT = sb("o", [P, 2, D]), sb("oT", [P, 2, D])
        x1 = [sb(f"x1_{u}", [P, QT, D]) for u in range(2)]
        ho = [sb(f"ho{u}", [P, QT, D]) for u in range(2)]
        st, mv = sb("st2", [P, QT, 6]), sb("mv2", [P, QT, 2])
        sd, rstd, nmr = sb("sd2", [P, QT]), sb("rstd2", [P, QT]), sb("nmr2", [P, QT])
        ps_hot, ps_k = ps("ps_hot"), [ps("ps_k0"), ps("ps_k1")]
        ps_sm, ps_g, ps_o, ps_p = ps("ps_sm"), [ps("ps_g0"), ps("ps_g1")], ps("ps_oT"), ps("ps_p")

        setup_in, bufs_clear, w_up, w_ready = sem("setup_in"), sem("bufs_clear"), sem("w_up"), sem("w_ready")
        table_ready, staged = sem("table_ready"), sem("staged")
        rows_in = [sem(f"rows_in{u}") for u in range(2)]
        ks_in, xs_in, vs_in = ([sem(f"{n}{u}") for u in range(2)] for n in ("ks_in", "xs_in", "vs_in"))
        hot_ready, hot_up, hotT_ready = sem("hot_ready"), sem("hot_up"), sem("hotT_ready")
        k_up, prod_ready, k_read = sem("k_up"), sem("prod_ready"), sem("k_read")
        score_ready, sc_up, tsc_ready = sem("score_ready"), sem("sc_up"), sem("tsc_ready")
        dif_ready, ex_ready, tp_ready, tp_up, pr_ready = (sem("dif_ready"), sem("ex_ready"), sem("tp_ready"),
                                                          sem("tp_up"), sem("pr_ready"))
        own_up, own_ready, pself_ready, vself_ready = (sem("own_up"), sem("own_ready"), sem("pself_ready"),
                                                       sem("vself_ready"))
        pv_ready, g_up, o_ready, o_up, oT_ready, p_up, x1_tile = (
            sem("pv_ready"), sem("g_up"), sem("o_ready"), sem("o_up"), sem("oT_ready"), sem("p_up"), sem("x1_tile"))
        soft, own_read = sem("soft"), sem("own_read")
        var, std, norm, h_ready = sem("var"), sem("std"), sem("norm"), sem("h_ready")
        vstep = sem("vstep")
        x1_out = [sem(f"x1_out{u}") for u in range(2)]
        h_out = [sem(f"h_out{u}") for u in range(2)]
        mask_out = sem("mask_out")
        passed = sem("passed")
        block = ctx.enter_context(nc.Block())
        last = pl.turns - 1

        @block.sync
        def _(sp):
            for c in range(C):
                sp.dma_start(wraw[:, c, :], w_out[c * P:(c + 1) * P, :]).then_inc(setup_in, 16)
            sp.dma_start(bias[:], b_out.rearrange("(o d) -> o d", o=1).to_broadcast([P, D])).then_inc(setup_in, 16)
            sp.dma_start(con["links"][:], link_dram.rearrange("(p t) w -> p t w", p=P)).then_inc(setup_in, 16)
            sp.wait_ge(bufs_clear, 1)
            for u in range(2):
                sp.sem_inc(x1_out[u], 16)
                sp.sem_inc(h_out[u], 16)

            def load(i, u):
                q = 2 * i + u
                at = i * (BODY * P) + u * pl.QR
                sp.wait_ge(k_read, q * QT + QT)
                sp.dma_start(ks[u][:], quad_rows(ks_dram, at)).then_inc(ks_in[u], 16)
                sp.wait_ge(vself_ready, q + 1)
                sp.dma_start(vs[u][:], quad_rows(qv_dram, at, (D, 2 * D))).then_inc(vs_in[u], 16)
                sp.wait_ge(x1_tile, q * QT + QT)

            def load_x(i, u):
                sp.dma_start(xs[u][:], quad_rows(x, i * (BODY * P) + u * pl.QR)).then_inc(xs_in[u], 16)

            def store(i, u):
                q = 2 * i + u
                at = i * (BODY * P) + u * pl.QR
                sp.wait_ge(h_ready, q + 2)
                sp.dma_start(quad_rows(x1_dram, at), x1[u][:]).then_inc(x1_out[u], 16)
                sp.dma_start(quad_rows(h_dram, at), ho[u][:]).then_inc(h_out[u], 16)
            load(0, 0)
            load_x(0, 0)
            with sp.Fori(0, last) as i:
                load(i, 1)
                load_x(i, 1)
                store(i, 0)
                load(i + 1, 0)
                load_x(i + 1, 0)
                store(i, 1)
            load(last, 1)
            parts = ragged(x, last * BODY * P + pl.QR, pl.last_rows, xs[1])
            for dram, tile in parts[:-1]:
                sp.dma_start(tile, dram).then_inc(mask_out, 16)
            if len(parts) > 1:
                sp.wait_ge(mask_out, 16)
            sp.dma_start(parts[-1][1], parts[-1][0]).then_inc(xs_in[1], 16)
            store(last, 0)
            store(last, 1)
            for u in range(2):
                sp.wait_ge(x1_out[u], 16 * (pl.turns + 1))
                sp.wait_ge(h_out[u], 16 * (pl.turns + 1))
            sp.dma_start(h_dram[0:1, :], mask_embed.rearrange("(o d) -> o d", o=1)).then_inc(mask_out, 16)
            sp.wait_ge(mask_out, 16 * len(parts))

        @block.gpsimd
        def _(pool):
            for u in range(2):
                nc.gpsimd.memset(rows[u][:], 0.0)
            nc.gpsimd.memset(xs[1][:], 0.0).then_inc(bufs_clear, 1)
            pool.wait_ge(setup_in, 16 * (C + 2))
            nc.gpsimd.tensor_copy(con["dloc"][:], con["links"][:, :, 1]).then_inc(table_ready, 1)
            pool.wait_ge(table_ready, 1)
            pool.wait_ge(bufs_clear, 1)
            pool.sem_inc(vself_ready, 2)
            bound = pool.to_reg(pl.NP - 1)

            def fetch(i, u):
                q = 2 * i + u
                pool.wait_ge(g_up, q * QT + QT)
                nc.gpsimd.tensor_copy(lidx[:, u, :], con["links"][:, bass.ds(i * BODY + u * QT, QT), 0])
                nc.gpsimd.tensor_copy(ldst[:, u, :], con["dloc"][:, bass.ds(i * BODY + u * QT, QT)]).then_inc(staged, 1)
                pool.wait_ge(staged, q + 1)
                pool.sem_inc(passed, 1)
                for t in range(QT):
                    nc.gpsimd.indirect_dma_start(
                        out=rows[u][:, t, :], out_offset=None, in_=qv_dram[:, :],
                        in_offset=bass.IndirectOffsetOnAxis(ap=lidx[:, u, t:t + 1], axis=0),
                        bounds_check=bound, oob_is_err=False).then_inc(rows_in[u], 16)
                for t in range(QT):
                    ins = nc.gpsimd.tensor_scalar(hot[u][:, t, :], con["iota"][:], ldst[:, u, t:t + 1], None, ALU.is_equal)
                ins.then_inc(hot_ready, 1)

            def weigh_own(i, u):
                q = 2 * i + u
                pool.wait_ge(vs_in[u], i * 16 + 16)
                pool.wait_ge(o_ready, q * QT + 2)
                pool.wait_ge(pself_ready, q + 1)
                nc.gpsimd.tensor_tensor(vself[:].rearrange("p t (h d) -> p (t h) d", h=H),
                                        vs[u][:].rearrange("p t (h d) -> p (t h) d", h=H),
                                        pself[:].rearrange("p t h -> p (t h)").to_broadcast([P, QH, hd]),
                                        ALU.mult).then_inc(vself_ready, 1)
            fetch(0, 0)

            def turn(i, end):
                fetch(i, 1)
                weigh_own(i, 0)
                if not end:
                    fetch(i + 1, 0)
                weigh_own(i, 1)
            with pool.Fori(0, last) as i:
                turn(i, False)
            turn(last, True)

        @block.tensor
        def _(pe):
            pe.wait_ge(setup_in, 16 * (C + 2))
            for n in range(C * C):
                c, r = n // C, n % C
                if n:
                    pe.wait_ge(w_ready, n)
                nc.tensor.transpose(ps_hot[:, 0:P], wraw[:, c, r * P:(r + 1) * P], con["ident"][:]).then_inc(w_up, 1)
            pe.wait_ge(w_ready, C * C)
            pe.sem_inc(g_up, 2 * QT)

            def expand(i, u):
                q = 2 * i + u
                pe.wait_ge(hot_ready, q + 1)
                pe.wait_ge(ks_in[u], i * 16 + 16)
                for t in range(QT):
                    n = q * QT + t
                    pe.wait_ge(hotT_ready, n + 1)
                    nc.tensor.transpose(ps_hot[:, 0:P], hot[u][:, t, :], con["ident"][:]).then_inc(hot_up, 1)
                    pe.wait_ge(hotT_ready, n + 2)
                    pe.wait_ge(k_read, n + 7)
                    nc.tensor.matmul(ps_k[t % 2][:, 0:KW], hotT[:, t % 2, :], ks[u][:, t, :],
                                     start=True, stop=True).then_inc(k_up, 1)

            def turn_scores(i, u):
                q = 2 * i + u
                pe.wait_ge(score_ready, q + 1)
                pe.wait_ge(own_ready, q + 1)
                for a in range(3):
                    ins = nc.tensor.transpose(ps_sm[0:QH, a * P:(a + 1) * P],
                                              slot_sc[:, a, :, :].rearrange("p t h -> p (t h)"), con["ident"][:])
                ins.then_inc(sc_up, 1)
                pe.wait_ge(tp_ready, q + 1)
                pe.sem_inc(passed, 1)
                for a in range(3):
                    ins = nc.tensor.transpose(ps_sm[:, a * QH:(a + 1) * QH], tp[:, a, :], con["ident"][0:QH, 0:QH])
                ins.then_inc(tp_up, 1)

            def own_shares(i, u):
                q = 2 * i + u
                pe.wait_ge(pr_ready, q + 1)
                for t in range(QT):
                    ins = nc.tensor.matmul(ps_sm[:, t * 32:t * 32 + 2 * H + 1], hot[u][:, t, :], fin[:, t, :],
                                           start=True, stop=True)
                ins.then_inc(own_up, 1)

            def gather_up(i, u):
                q = 2 * i + u
                for t in range(QT):
                    n = q * QT + t
                    pe.wait_ge(pv_ready, n + 1)
                    pe.wait_ge(o_ready, n + 1)
                    nc.tensor.matmul(ps_g[t % 2][:, 0:D], hot[u][:, t, :], pv[:, t % 2, :],
                                     start=True, stop=True).then_inc(g_up, 1)
                    if t:
                        project_out(n - 1, t - 1)
                project_out(q * QT + QT - 1, QT - 1)

            def project_out(n, t):
                pe.wait_ge(o_ready, n + 3)
                pe.wait_ge(oT_ready, n + 1)
                for c in range(C):
                    ins = nc.tensor.transpose(ps_o[:, c * P:(c + 1) * P], o[:, t % 2, c * P:(c + 1) * P], con["ident"][:])
                ins.then_inc(o_up, 1)
                pe.wait_ge(oT_ready, n + 2)
                pe.wait_ge(x1_tile, n + 8)
                for c in range(C):
                    ins = nc.tensor.matmul(ps_p[:, 0:D], oT[:, t % 2, c * P:(c + 1) * P], wT[:, c, :],
                                           start=(c == 0), stop=(c == C - 1))
                ins.then_inc(p_up, 1)
            expand(0, 0)

            def turn(i, end):
                turn_scores(i, 0)
                expand(i, 1)
                own_shares(i, 0)
                gather_up(i, 0)
                turn_scores(i, 1)
                if not end:
                    expand(i + 1, 0)
                own_shares(i, 1)
                gather_up(i, 1)
            with pe.Fori(0, last) as i:
                turn(i, False)
            turn(last, True)

        @block.scalar
        def _(act):
            for n in range(C * C):
                c, r = n // C, n % C
                act.wait_ge(w_up, n + 1)
                nc.scalar.copy(wT[:, r, c * P:(c + 1) * P], ps_hot[:, 0:P]).then_inc(w_ready, 1)
            act.sem_inc(hotT_ready, 1)
            act.sem_inc(oT_ready, 1)
            act.sem_inc(h_ready, 1)

            def keep_hot(i, u):
                q = 2 * i + u
                for t in range(QT):
                    n = q * QT + t
                    act.wait_ge(hot_up, n + 1)
                    act.wait_ge(k_up, n + 1)
                    nc.scalar.copy(hotT[:, t % 2, :], ps_hot[:, 0:P]).then_inc(hotT_ready, 1)

            def exponent(i, u):
                act.wait_ge(dif_ready, 2 * i + u + 1)
                nc.scalar.activation(ex[:], dif[:], ACT.Exp, scale=SCALE).then_inc(ex_ready, 1)

            def keep_o(i, u):
                q = 2 * i + u
                for t in range(QT):
                    n = q * QT + t
                    act.wait_ge(o_up, n + 1)
                    act.wait_ge(p_up, n + 1)
                    nc.scalar.copy(oT[:, t % 2, :], ps_o[:, 0:D]).then_inc(oT_ready, 1)

            def normalize(i, u):
                q = 2 * i + u
                act.wait_ge(var, q + 1)
                nc.scalar.activation(sd[:], mv[:, :, 1], ACT.Sqrt, bias=con["eps"][:, 0:1]).then_inc(std, 1)
                act.wait_ge(norm, q + 1)
                act.wait_ge(h_out[u], i * 16 + 16)
                for t in range(QT):
                    ins = nc.scalar.activation(ho[u][:, t, :], x1[u][:, t, :], ACT.Relu,
                                               bias=nmr[:, t:t + 1], scale=rstd[:, t:t + 1])
                ins.then_inc(h_ready, 1)
            keep_hot(0, 0)

            def turn(i, end):
                exponent(i, 0)
                keep_hot(i, 1)
                keep_o(i, 0)
                normalize(i, 0)
                exponent(i, 1)
                if not end:
                    keep_hot(i + 1, 0)
                keep_o(i, 1)
                normalize(i, 1)
            with act.Fori(0, last) as i:
                turn(i, False)
            turn(last, True)

        @block.vector
        def _(dve):
            V = nc.vector
            dve.wait_ge(setup_in, 16 * (C + 2))
            V.memset(same[:, 0:1], 0.0)
            V.memset(same[:, P:P + 1], 0.0)
            V.memset(fin[:], 1.0).then_inc(vstep, 1)
            dve.sem_inc(k_read, 2 * QT)
            dve.sem_inc(k_up, 2)
            dve.sem_inc(own_ready, 1)
            dve.sem_inc(o_ready, 2)
            dve.sem_inc(p_up, 2)
            dve.sem_inc(x1_tile, 2 * QT)
            dve.wait_ge(vstep, 1)

            def scores(i, u):
                q = 2 * i + u
                dve.wait_ge(rows_in[u], i * (16 * QT) + 16 * QT)
                dve.wait_ge(staged, q + 1)
                dve.wait_ge(sc_up, q + 1)
                V.tensor_copy(slot_sc[:, 2, :, :], ldst[:, u, :].to_broadcast([P, QT, H]))
                for t in range(QT):
                    n = q * QT + t
                    dve.wait_ge(k_up, n + 3)
                    V.tensor_tensor(prod[:, t % 2, :], rows[u][:, t, 0:D], ps_k[t % 2][:, 0:D], ALU.mult).then_inc(prod_ready, 1)
                    V.tensor_copy(slot_sc[:, 1, t, :], ps_k[t % 2][:, D:KW]).then_inc(k_read, 1)
                    dve.wait_ge(prod_ready, n + 1)
                    ins = V.tensor_reduce(slot_sc[:, 0, t, :], prod[:, t % 2, :].rearrange("p (h d) -> p h d", h=H),
                                          AX.X, ALU.add)
                ins.then_inc(score_ready, 1)

            def softmax(i, u):
                q = 2 * i + u
                step = [0]
                STEPS = 11

                def then(ins):
                    step[0] += 1
                    ins.then_inc(soft, 1)
                    dve.wait_ge(soft, q * STEPS + step[0])
                dve.wait_ge(sc_up, q + 2)
                then(V.tensor_copy(tsc[:], ps_sm[0:QH, 0:3 * P].rearrange("p (a s) -> p a s", a=3)))
                V.tensor_tensor(top[:], tsc[:, 0, :], tsc[:, 1, :], ALU.max)
                then(V.tensor_tensor(same[:, 1:P], tsc[:, 2, 1:P], tsc[:, 2, 0:P - 1], ALU.is_equal))
                then(V.tensor_scalar(cut[:], same[:], -1.0, NEG, ALU.add, ALU.mult))
                V.tensor_tensor_scan(fwd[:], cut[:, 0:P], top[:], 0.0, ALU.add, ALU.max)
                then(V.tensor_tensor_scan(bwd[:, ::-1], cut[:, 1:P + 1][:, ::-1], top[:, ::-1], 0.0, ALU.add, ALU.max))
                then(V.tensor_tensor(fwd[:], fwd[:], bwd[:], ALU.max))
                V.tensor_tensor(dif[:, 0, :], tsc[:, 0, :], fwd[:], ALU.subtract)
                V.tensor_tensor(dif[:, 1, :], tsc[:, 1, :], fwd[:], ALU.subtract).then_inc(dif_ready, 1)
                dve.wait_ge(ex_ready, q + 1)
                V.tensor_tensor_scan(fwd[:], same[:, 0:P], ex[:, 0, :], 0.0, ALU.mult, ALU.add)
                V.tensor_tensor_scan(bwd[:, ::-1], same[:, 1:P + 1][:, ::-1], ex[:, 0, ::-1], 0.0, ALU.mult, ALU.add)
                then(V.tensor_tensor(tot[:], ex[:, 1, :], ex[:, 0, :], ALU.subtract))
                then(V.tensor_tensor(fwd[:], fwd[:], bwd[:], ALU.add))
                then(V.tensor_tensor(tot[:], tot[:], fwd[:], ALU.add))
                then(V.reciprocal(tot[:], tot[:]))
                V.tensor_scalar(tp[:, 2, :], same[:, 1:P + 1], -1.0, 1.0, ALU.mult, ALU.add)
                then(V.tensor_tensor(bwd[:], ex[:, 1, :], tot[:], ALU.mult))
                V.tensor_tensor(tp[:, 0, :], ex[:, 0, :], tot[:], ALU.mult)
                V.tensor_tensor(tp[:, 1, :], bwd[:], tp[:, 2, :], ALU.mult).then_inc(tp_ready, 1)
                dve.wait_ge(tp_up, q + 1)
                then(V.tensor_copy(pr[:].rearrange("p t h -> p (t h)"), ps_sm[:, 0:QH]))
                V.tensor_copy(fin[:, :, 0:H], ps_sm[:, QH:2 * QH].rearrange("p (t h) -> p t h", h=H))
                V.tensor_copy(fin[:, :, H:2 * H],
                              ps_sm[:, 2 * QH:3 * QH].rearrange("p (t h) -> p t h", h=H)).then_inc(pr_ready, 1)
                assert step[0] == STEPS, step

            def settle(i, u):
                q = 2 * i + u
                dve.wait_ge(own_up, q + 1)
                V.tensor_copy(own[:], ps_sm[:, 0:QT * 32].rearrange("p (t w) -> p t w", t=QT)[:, :, 0:2 * H + 1]
                              ).then_inc(own_read, 1)
                dve.wait_ge(own_read, q + 1)
                V.tensor_tensor(pself[:], own[:, :, 0:H], own[:, :, H:2 * H], ALU.subtract).then_inc(own_ready, 1)
                V.tensor_scalar(con["deg"][:, bass.ds(i * BODY + u * QT, QT)], own[:, :, 2 * H], 1.0, None, ALU.add)
                dve.wait_ge(own_ready, q + 2)
                V.tensor_scalar(pself[:], pself[:], 1.0, None, ALU.add).then_inc(pself_ready, 1)

            def combine(i, u):
                q = 2 * i + u

                def weigh(t):
                    n = q * QT + t
                    dve.wait_ge(g_up, n + 7)
                    V.tensor_tensor(pv[:, t % 2, :].rearrange("p (h d) -> p h d", h=H),
                                    rows[u][:, t, D:2 * D].rearrange("p (h d) -> p h d", h=H),
                                    pr[:, t, :].to_broadcast([P, H, hd]), ALU.mult).then_inc(pv_ready, 1)

                def finish(t):
                    n = q * QT + t
                    dve.wait_ge(p_up, n + 3)
                    V.tensor_tensor(x1[u][:, t, :], xs[u][:, t, :], ps_p[:, 0:D], ALU.add).then_inc(x1_tile, 1)
                dve.wait_ge(xs_in[u], i * 16 + 16)
                dve.wait_ge(x1_out[u], i * 16 + 16)
                for t in range(QT):
                    V.tensor_tensor(xs[u][:, t, :], xs[u][:, t, :], bias[:], ALU.add)
                weigh(0)
                for t in range(QT):
                    n = q * QT + t
                    if t < QT - 1:
                        weigh(t + 1)
                    if t == 0:
                        dve.wait_ge(vself_ready, q + 3)
                    dve.wait_ge(g_up, n + 9)
                    if t >= 2:
                        dve.wait_ge(o_up, q * QT + t - 1)
                    V.tensor_tensor(o[:, t % 2, :], ps_g[t % 2][:, 0:D], vself[:, t, :], ALU.add).then_inc(o_ready, 1)
                    if t:
                        finish(t - 1)
                finish(QT - 1)
                dve.wait_ge(x1_tile, q * QT + 3 * QT)
                for t in range(QT):
                    ins = V.bn_stats(st[:, t, :], x1[u][:, t, :])
                ins.then_inc(vstep, 1)
                dve.wait_ge(vstep, q * 3 + 2)
                dve.sem_inc(passed, 1)
                for t in range(QT):
                    ins = V.bn_aggr(mv[:, t, :], st[:, t, :])
                ins.then_inc(var, 1)
                dve.wait_ge(std, q + 1)
                dve.wait_ge(h_ready, q + 1)
                V.reciprocal(rstd[:], sd[:]).then_inc(vstep, 1)
                dve.wait_ge(vstep, q * 3 + 3)
                V.scalar_tensor_tensor(out=nmr[:], in0=mv[:, :, 0], scalar=-1.0, in1=rstd[:],
                                       op0=ALU.mult, op1=ALU.mult).then_inc(norm, 1)
                dve.sem_inc(vstep, 1)
            dve.sem_inc(sc_up, 1)
            scores(0, 0)

            def turn(i, end):
                softmax(i, 0)
                scores(i, 1)
                settle(i, 0)
                combine(i, 0)
                softmax(i, 1)
                if not end:
                    scores(i + 1, 0)
                settle(i, 1)
                combine(i, 1)
            with dve.Fori(0, last) as i:
                turn(i, False)
            turn(last, True)
            dve.wait_ge(own_ready, 2 * pl.turns + 1)
            V.reciprocal(con["inv_deg"][:], con["deg"][:])


def clear_signals(nc, signals):
    with nc.Block() as block:
        @block.gpsimd
        def _(pool):
            for s in signals:
                pool.sem_clear(s)


def aggregate(nc, pl, con, signals, layer, wl, wr, b, gamma, beta, rmean, rvar, h_in, h_next, x1_dram, out):
    D, C, NT = pl.D, pl.C, pl.NT
    final = out is not None
    with ExitStack() as ctx:
        def name(n):
            return f"{n}_l{layer}"

        def sb(n, s, d=F32):
            return ctx.enter_context(nc.sbuf_tensor(name(n), s, d))

        def ps(n):
            return ctx.enter_context(nc.psum_tensor(name(n), [P, 512], F32))

        def sem(n):
            if n.startswith("rows_in"):
                return nc.alloc_semaphore(f"agg_{name(n)}")
            if n not in signals:
                signals[n] = nc.alloc_semaphore("agg_" + n)
            return signals[n]
        wls, wrs = sb("wl", [P, C, D]), sb("wr", [P, C, D])
        par = sb("par", [P, 5, D])
        g, bias = sb("g", [P, D]), sb("bias", [P, D])
        hs = [sb(f"hs{u}", [P, QT, D]) for u in range(2)]
        xs = [sb(f"xs{u}", [P, QT, D]) for u in range(2)]
        rows = [sb(f"rows{u}", [P, QT, D]) for u in range(2)]
        hot = [sb(f"hot{u}", [P, QT, P]) for u in range(2)]
        res = [sb(f"res{u}", [P, QT, D]) for u in range(2)]
        lidx, ldst, ideg = sb("lidx", [P, 2, QT], I32), sb("ldst", [P, 2, QT]), sb("ideg", [P, 2, QT])
        hT, aT, z = sb("hT", [P, 2, D]), sb("aT", [P, 2, D]), sb("z", [P, 2, D])
        ps_h, ps_a, ps_z = [[ps(f"{n}{v}") for v in range(2)] for n in ("ps_h", "ps_a", "ps_z")]
        par_in, std_ready, fold, weights_ready = sem("par_in"), sem("std_ready"), sem("fold"), sem("weights_ready")
        bufs_clear, staged, hot_ready = sem("bufs_clear"), sem("staged"), sem("hot_ready")
        passed = sem("passed")
        hs_in, xs_in, rows_in, res_out = ([sem(f"{n}{u}") for u in range(2)] for n in ("hs_in", "xs_in", "rows_in", "res_out"))
        h_up, a_up, hT_ready, aT_ready, z_up, z_read, z_step, tile_done, ideg_ready, tail_io = (
            sem("h_up"), sem("a_up"), sem("hT_ready"), sem("aT_ready"), sem("z_up"), sem("z_read"), sem("z_step"),
            sem("tile_done"), sem("ideg_ready"), sem("tail_io"))
        block = ctx.enter_context(nc.Block())
        last = pl.turns - 1

        @block.sync
        def _(sp):
            for c in range(C):
                sp.dma_start(wls[:, c, :], wl[c * P:(c + 1) * P, :]).then_inc(par_in, 16)
                sp.dma_start(wrs[:, c, :], wr[c * P:(c + 1) * P, :]).then_inc(par_in, 16)
            for j, v in enumerate((b, gamma, beta, rmean, rvar)):
                sp.dma_start(par[:, j, :], v.to_broadcast([P, D])).then_inc(par_in, 16)
            for u in range(2):
                sp.sem_inc(res_out[u], 16)

            def load(i, u):
                sp.wait_ge(tile_done, (2 * i + u) * QT + QT)
                at = i * (BODY * P) + u * pl.QR
                sp.dma_start(hs[u][:], quad_rows(h_in, at)).then_inc(hs_in[u], 16)
                if final:
                    sp.dma_start(xs[u][:], quad_rows(x1_dram, at)).then_inc(xs_in[u], 16)

            def store(i, u):
                sp.wait_ge(tile_done, (2 * i + u) * QT + 3 * QT)
                sp.dma_start(quad_rows(out if final else h_next, i * (BODY * P) + u * pl.QR),
                             res[u][:]).then_inc(res_out[u], 16)
            load(0, 0)
            with sp.Fori(0, last) as i:
                load(i, 1)
                store(i, 0)
                load(i + 1, 0)
                store(i, 1)
            load(last, 1)
            store(last, 0)
            if final:
                sp.wait_ge(tile_done, (2 * last + 1) * QT + 3 * QT)
                parts = ragged(out, last * BODY * P + pl.QR, pl.last_rows, res[1])
                for dram, tile in parts:
                    sp.dma_start(dram, tile).then_inc(tail_io, 16)
                sp.wait_ge(tail_io, 16 * len(parts))
            else:
                store(last, 1)
            sp.wait_ge(res_out[0], 16 * (pl.turns + 1))
            sp.wait_ge(res_out[1], 16 * (pl.turns + (0 if final else 1)))

        @block.gpsimd
        def _(pool):
            for u in range(2):
                ins = nc.gpsimd.memset(rows[u][:], 0.0)
            ins.then_inc(bufs_clear, 1)
            pool.wait_ge(bufs_clear, 1)
            bound = pool.to_reg(pl.NP - 1)

            def fetch(i, u):
                q = 2 * i + u
                pool.wait_ge(a_up, q * QT + QT)
                nc.gpsimd.tensor_copy(lidx[:, u, :], con["links"][:, bass.ds(i * BODY + u * QT, QT), 0])
                nc.gpsimd.tensor_copy(ldst[:, u, :], con["dloc"][:, bass.ds(i * BODY + u * QT, QT)]).then_inc(staged, 1)
                pool.wait_ge(staged, q + 1)
                pool.sem_inc(passed, 1)
                for t in range(QT):
                    nc.gpsimd.indirect_dma_start(
                        out=rows[u][:, t, :], out_offset=None, in_=h_in[:, :],
                        in_offset=bass.IndirectOffsetOnAxis(ap=lidx[:, u, t:t + 1], axis=0),
                        bounds_check=bound, oob_is_err=False).then_inc(rows_in[u], 16)
                for t in range(QT):
                    ins = nc.gpsimd.tensor_scalar(hot[u][:, t, :], con["iota"][:], ldst[:, u, t:t + 1], None, ALU.is_equal)
                ins.then_inc(hot_ready, 1)
            with pool.Fori(0, pl.turns) as i:
                fetch(i, 0)
                fetch(i, 1)

        @block.tensor
        def _(pe):
            pe.wait_ge(weights_ready, 1)
            pe.sem_inc(a_up, 2 * QT)

            def up(i, k):
                u, t, bb, n, q = k // QT, k % QT, k % 2, i * BODY + k, 2 * i + k // QT
                if t == 0:
                    pe.wait_ge(hs_in[u], i * 16 + 16)
                    pe.wait_ge(rows_in[u], i * (16 * QT) + 16 * QT)
                    pe.wait_ge(hot_ready, q + 1)
                pe.wait_ge(hT_ready, n + 1)
                for c in range(C):
                    ins = nc.tensor.transpose(ps_h[bb][:, c * P:(c + 1) * P], hs[u][:, t, c * P:(c + 1) * P], con["ident"][:])
                ins.then_inc(h_up, 1)
                pe.wait_ge(aT_ready, n + 1)
                for c in range(C):
                    ins = nc.tensor.matmul(ps_a[bb][:, c * P:(c + 1) * P], rows[u][:, t, c * P:(c + 1) * P],
                                           hot[u][:, t, :], start=True, stop=True)
                ins.then_inc(a_up, 1)

            def dense(i, k):
                n, bb = i * BODY + k, k % 2
                pe.wait_ge(hT_ready, n + 3)
                pe.wait_ge(z_read, n + 1)
                for c in range(C):
                    nc.tensor.matmul(ps_z[bb][:, D:2 * D], hT[:, bb, c * P:(c + 1) * P], wrs[:, c, :],
                                     start=(c == 0), stop=(c == C - 1))
                pe.wait_ge(aT_ready, n + 3)
                for c in range(C):
                    ins = nc.tensor.matmul(ps_z[bb][:, 0:D], aT[:, bb, c * P:(c + 1) * P], wls[:, c, :],
                                           start=(c == 0), stop=(c == C - 1))
                ins.then_inc(z_up, 1)
            up(0, 0)

            def turn(i, end):
                for k in range(BODY):
                    if k < BODY - 1:
                        up(i, k + 1)
                    elif not end:
                        up(i + 1, 0)
                    dense(i, k)
            with pe.Fori(0, last) as i:
                turn(i, False)
            turn(last, True)

        @block.scalar
        def _(act):
            act.wait_ge(par_in, 16 * (2 * C + 5))
            nc.scalar.activation(g[:], par[:, 4, :], ACT.Sqrt, bias=con["eps"][:, 0:1]).then_inc(std_ready, 1)
            act.sem_inc(hT_ready, 2)

            def keep(n, bb):
                act.wait_ge(h_up, n + 1)
                act.wait_ge(z_up, n + 1)
                nc.scalar.copy(hT[:, bb, :], ps_h[bb][:, 0:D]).then_inc(hT_ready, 1)
            with act.Fori(0, pl.turns) as i:
                for k in range(BODY):
                    keep(i * BODY + k, k % 2)

        @block.vector
        def _(dve):
            V = nc.vector
            dve.wait_ge(par_in, 16 * (2 * C + 5))
            dve.wait_ge(std_ready, 1)
            V.tensor_tensor(bias[:], par[:, 0, :], par[:, 3, :], ALU.subtract)
            V.reciprocal(g[:], g[:]).then_inc(fold, 1)
            dve.wait_ge(fold, 1)
            V.tensor_tensor(g[:], g[:], par[:, 1, :], ALU.mult).then_inc(fold, 1)
            dve.wait_ge(fold, 2)
            V.tensor_tensor(bias[:], bias[:], g[:], ALU.mult).then_inc(fold, 1)
            for w in (wls, wrs):
                for c in range(C):
                    V.tensor_tensor(w[:, c, :], w[:, c, :], g[:], ALU.mult)
            dve.wait_ge(fold, 3)
            V.tensor_tensor(bias[:], bias[:], par[:, 2, :], ALU.add).then_inc(weights_ready, 1)
            dve.wait_ge(weights_ready, 1)
            dve.sem_inc(aT_ready, 2)
            dve.sem_inc(z_up, 2)
            dve.sem_inc(z_read, 2)
            dve.sem_inc(tile_done, 2 * QT)

            def add_own(i, k):
                n, bb = i * BODY + k, k % 2
                dve.wait_ge(a_up, n + 9)
                dve.wait_ge(hT_ready, n + 3)
                dve.wait_ge(z_up, n + 1)
                V.tensor_tensor(aT[:, bb, :], hT[:, bb, :], ps_a[bb][:, 0:D], ALU.add).then_inc(aT_ready, 1)

            def close(i, k):
                u, t, bb, n, q = k // QT, k % QT, k % 2, i * BODY + k, 2 * i + k // QT
                if t == 0:
                    V.tensor_copy(ideg[:, u, :], con["inv_deg"][:, bass.ds(i * BODY + u * QT, QT)]).then_inc(ideg_ready, 1)
                    dve.wait_ge(ideg_ready, q + 1)
                    dve.wait_ge(res_out[u], i * 16 + 16)
                    if final:
                        dve.wait_ge(xs_in[u], i * 16 + 16)
                dve.wait_ge(z_up, n + 3)
                V.scalar_tensor_tensor(out=z[:, bb, :], in0=ps_z[bb][:, 0:D], scalar=ideg[:, u, t:t + 1], in1=bias[:],
                                       op0=ALU.mult, op1=ALU.add).then_inc(z_step, 1)
                dve.wait_ge(z_step, 2 * n + 1)
                V.tensor_tensor(z[:, bb, :], z[:, bb, :], ps_z[bb][:, D:2 * D], ALU.add).then_inc(z_read, 1)
                dve.wait_ge(z_read, n + 3)
                if final:
                    V.tensor_tensor(z[:, bb, :], z[:, bb, :], hs[u][:, t, :], ALU.add).then_inc(z_step, 1)
                    dve.wait_ge(z_step, 2 * n + 2)
                    V.tensor_tensor(res[u][:, t, :], z[:, bb, :], xs[u][:, t, :], ALU.add).then_inc(tile_done, 1)
                else:
                    V.scalar_tensor_tensor(out=res[u][:, t, :], in0=z[:, bb, :], scalar=0.0, in1=hs[u][:, t, :],
                                           op0=ALU.max, op1=ALU.add).then_inc(tile_done, 1)
                    dve.sem_inc(z_step, 1)
            add_own(0, 0)

            def turn(i, end):
                for k in range(BODY):
                    if k < BODY - 1:
                        add_own(i, k + 1)
                    elif not end:
                        add_own(i + 1, 0)
                    close(i, k)
            with dve.Fori(0, last) as i:
                turn(i, False)
            turn(last, True)


def program(nc, x, src, dst, Wq, bq, Wk, bk, Wv, bv, Wo, bo, mask_embed, Wl, Wr, b, gamma, beta, rmean, rvar, out):
    N, D = x.shape
    pl = Plan(N, src.shape[0], D, 8)
    KW = D + pl.H
    qv = nc.dram_tensor("qv_rows", (pl.NP, 2 * D), F32, kind="Internal").ap()
    ks = nc.dram_tensor("k_rows", (pl.NP, KW), F32, kind="Internal").ap()
    links = nc.dram_tensor("link_table", (P * pl.NT, 2), I32, kind="Internal").ap()
    x1 = nc.dram_tensor("x1_rows", (pl.NP, D), F32, kind="Internal").ap()
    hbuf = [nc.dram_tensor(f"h_rows{j}", (pl.NP, D), F32, kind="Internal").ap() for j in range(2)]
    with ExitStack() as ctx:
        con = constants(nc, ctx, pl)
        with ExitStack() as edges:
            idx = edges.enter_context(nc.sbuf_tensor("edge_rows", [P, pl.EB], I32))
            pay = edges.enter_context(nc.sbuf_tensor("edge_pay", [P, pl.EB, 2], I32))
            edge_tables(nc, pl, con, src, dst, links, idx, pay)
            project(nc, pl, con, x, (Wq, Wk, Wv), (bq, bk, bv), qv, ks, links, idx, pay)
        attend(nc, pl, con, x, Wo, bo, qv, ks, links, mask_embed, x1, hbuf[0])
        L = Wl.shape[0]
        signals = {}
        for l in range(L):
            vec = [v[l:l + 1, :] for v in (b, gamma, beta, rmean, rvar)]
            if l:
                clear_signals(nc, list(signals.values()))
            aggregate(nc, pl, con, signals, l, Wl[l], Wr[l], *vec, hbuf[l % 2], hbuf[(l + 1) % 2], x1,
                      out if l == L - 1 else None)


INPUTS = ['x', 'src', 'dst', 'L0_gnn_Wq', 'L0_gnn_bq', 'L0_gnn_Wk', 'L0_gnn_bk', 'L0_gnn_Wv', 'L0_gnn_bv',
          'L0_gnn_Wo', 'L0_gnn_bo', 'L1_gnn_mask_embed', 'L1_gnn_Wl', 'L1_gnn_Wr', 'L1_gnn_b', 'L1_gnn_gamma',
          'L1_gnn_beta', 'L1_gnn_rmean', 'L1_gnn_rvar']


def kernel(**inputs):
    import concourse.bacc as bacc
    import numpy as np
    from concourse.bass_utils import run_bass_kernel_spmd

    nc = bacc.Bacc("TRN2", target_bir_lowering=False, num_devices=1)
    arrays, args = {}, []
    for name in INPUTS:
        a = np.ascontiguousarray(inputs[name])
        arrays[f"in_{name}"] = a
        args.append(nc.dram_tensor(f"in_{name}", a.shape, mybir.dt.from_np(a.dtype), kind="ExternalInput").ap())
    out = nc.dram_tensor("out_x", inputs["x"].shape, F32, kind="ExternalOutput").ap()
    program(nc, *args, out)
    r = run_bass_kernel_spmd(nc, [arrays], core_ids=[0])
    return r.results[0]["out_x"]
```

```python
from contextlib import ExitStack

import concourse.bass as bass
from concourse import mybir

F32 = mybir.dt.float32
F32R = mybir.dt.float32r
I32 = mybir.dt.int32
ALU = mybir.AluOpType
ACT = mybir.ActivationFunctionType
AX = mybir.AxisListType

P = 128
QT = 4
BODY = 2 * QT
SKIP = 1 << 20
NEG = 1.0e30
EPS = 1e-5


class Plan:

    def __init__(self, n, e, d, heads):
        self.N, self.E, self.D, self.H = n, e, d, heads
        self.hd = d // heads
        self.C = d // P
        self.turns = -(-n // (P * BODY))
        self.NT = self.turns * BODY
        self.NP = self.NT * P
        self.QR = QT * P
        self.last_rows = n - (self.turns - 1) * BODY * P - self.QR
        assert 0 < self.last_rows <= self.QR
        self.EC = -(-e // P)
        self.EB = -(-self.EC // 16) * 16
        self.e_tail = e - (P - 1) * self.EC
        assert 0 < self.e_tail <= self.EC


def quad_rows(t, base, cols=None):
    v = t[bass.ds(base, QT * P), :] if cols is None else t[bass.ds(base, QT * P), cols[0]:cols[1]]
    return v.rearrange("(t p) d -> p t d", p=P)


def ragged(table, base, rows, tile):
    full, rest = rows // P, rows % P
    out = []
    if rest:
        out.append((table[base + full * P:base + rows, :], tile[0:rest, full, :]))
    if full:
        out.append((table[base:base + full * P, :].rearrange("(t p) d -> p t d", p=P), tile[:, 0:full, :]))
    return out


def constants(nc, ctx, pl):
    c = {}
    for name, shape, dt in (("ident", [P, P], F32), ("ones", [P, P], F32), ("iota", [P, P], F32),
                            ("eps", [P, 1], F32), ("links", [P, pl.NT, 2], I32), ("dloc", [P, pl.NT], F32),
                            ("flag", [1, 1], I32), ("edge_src", [P, pl.EC], I32), ("edge_dst", [P, pl.EC], I32),
                            ("deg", [P, pl.NT], F32), ("inv_deg", [P, pl.NT], F32)):
        c[name] = ctx.enter_context(nc.sbuf_tensor(name, shape, dt))
    return c


def where(attach, con, regular):
    def wrap(body):
        @attach
        def _(eng):
            flag = eng.value_load(con["flag"][0:1, 0:1], min_val=0, max_val=1)
            with eng.If(flag > 0 if regular else flag < 1):
                body(eng)
    return wrap


def edge_tables(nc, pl, con, src, dst, link_dram, idx_out, pay_out):
    EC, NT = pl.EC, pl.NT
    with ExitStack() as ctx:
        def sb(n, s, d=F32):
            return ctx.enter_context(nc.sbuf_tensor(n, s, d))

        def sem(n):
            return ctx.enter_context(nc.semaphore(n))
        dst_i, src_i = sb("dst_i", [P, EC + 2], I32), sb("src_i", [P, EC], I32)
        tb_i, e_i = sb("tb_i", [P, EC + 2], I32), sb("e_i", [P, EC], I32)
        iota_i = sb("iota_i", [P, P], I32)
        d, s, tb, e = sb("d_f", [P, EC + 2]), sb("s_f", [P, EC]), sb("tb_f", [P, EC + 2]), sb("e_f", [P, EC])
        first, start, slot = sb("first", [P, EC]), sb("start", [P, EC]), sb("slot", [P, EC])
        loop, link, tmp = sb("loop", [P, EC]), sb("link", [P, EC]), sb("tmp", [P, EC])
        row_in, row, carry = sb("row_in", [1, P]), sb("row", [1, P + 1]), sb("carry", [P, 1])
        sums, total, bad = sb("sums", [P, 3]), sb("total", [1, 3]), sb("bad", [1, 1])
        empty = sb("empty", [P, NT, 2], I32)
        ps_row = ctx.enter_context(nc.psum_tensor("ps_row", [P, 512], F32))
        ps_col = ctx.enter_context(nc.psum_tensor("ps_col", [P, 512], F32))
        padded, edges_in, pool_ready, step = sem("padded"), sem("edges_in"), sem("pool_ready"), sem("step")
        row_up, row_back, row_ready, empty_out, ident_clear = (
            sem("row_up"), sem("row_back"), sem("row_ready"), sem("empty_out"), sem("ident_clear"))
        start_ready, sums_ready, sums_up = sem("start_ready"), sem("sums_ready"), sem("sums_up")
        block = ctx.enter_context(nc.Block())

        @block.sync
        def _(sp):
            sp.wait_ge(padded, 1)
            flat = lambda a, n: a.rearrange("(p c) -> p c", c=n)
            sp.dma_start(dst_i[0:1, 1:EC + 2], flat(dst[0:EC + 1], EC + 1)).then_inc(edges_in, 16)
            mid = dst[EC - 1:EC - 1 + (P - 2) * EC]
            sp.dma_start(dst_i[1:P - 1, 0:EC], flat(mid, EC)).then_inc(edges_in, 16)
            with nc.allow_non_contiguous_dma("the two neighbours past a partition's edges"):
                tail = dst[2 * EC - 1:2 * EC - 1 + (P - 3) * EC].rearrange("(p c) -> p c", c=EC)
                sp.dma_start(dst_i[1:P - 2, EC:EC + 2], tail[:, 0:2]).then_inc(edges_in, 16)
                at = (P - 1) * EC - 1
                sp.dma_start(dst_i[P - 2:P - 1, EC:EC + 2], flat(dst[at:at + 2], 2)).then_inc(edges_in, 16)
            sp.dma_start(dst_i[P - 1:P, 0:pl.e_tail + 1],
                         flat(dst[(P - 1) * EC - 1:pl.E], pl.e_tail + 1)).then_inc(edges_in, 16)
            sp.dma_start(src_i[0:P - 1, :], flat(src[0:(P - 1) * EC], EC)).then_inc(edges_in, 16)
            sp.dma_start(src_i[P - 1:P, 0:pl.e_tail],
                         flat(src[(P - 1) * EC:pl.E], pl.e_tail)).then_inc(edges_in, 16)
            sp.wait_ge(padded, 2)
            sp.dma_start(link_dram.rearrange("(p t) w -> p (t w)", p=P),
                         empty[:].rearrange("p t w -> p (t w)")).then_inc(empty_out, 16)
            sp.wait_ge(empty_out, 16)

        @block.gpsimd
        def _(pool):
            nc.gpsimd.iota(iota_i[:], pattern=[[1, P]], base=0, channel_multiplier=0)
            nc.gpsimd.iota(e_i[:], pattern=[[1, EC]], base=0, channel_multiplier=EC).then_inc(pool_ready, 1)
            nc.gpsimd.memset(con["ones"][:], 1.0)
            nc.gpsimd.memset(con["eps"][:], EPS)
            nc.gpsimd.memset(con["ident"][:], 0.0).then_inc(ident_clear, 1)
            pool.wait_ge(ident_clear, 1)
            nc.gpsimd.affine_select(out=con["ident"][:], in_=con["ident"][:], compare_op=ALU.not_equal, fill=1.0,
                                    base=0, pattern=[[-1, P]], channel_multiplier=1).then_inc(pool_ready, 1)

        @block.tensor
        def _(pe):
            pe.wait_ge(pool_ready, 2)
            pe.wait_ge(start_ready, 1)
            nc.tensor.transpose(ps_row[0:1, 0:P], start[:, EC - 1:EC], con["ident"][:]).then_inc(row_up, 1)
            pe.wait_ge(row_ready, 1)
            nc.tensor.matmul(ps_col[:, 0:1], row[0:1, 0:P], con["ones"][0:1, 0:1],
                             start=True, stop=True).then_inc(row_back, 1)
            pe.wait_ge(sums_ready, 1)
            nc.tensor.matmul(ps_row[0:1, 0:3], con["ones"][:, 0:1], sums[:], start=True, stop=True).then_inc(sums_up, 1)

        @block.vector
        def _(dve):
            n = [0]

            def then(ins):
                n[0] += 1
                ins.then_inc(step, 1)
                dve.wait_ge(step, n[0])
            V = nc.vector
            V.memset(dst_i[:], pl.NP)
            then(V.memset(src_i[:], 0))
            V.memset(dst_i[0:1, 0:1], -1).then_inc(padded, 1)
            V.memset(empty[:, :, 0], SKIP)
            V.memset(empty[:, :, 1], -1).then_inc(padded, 1)
            V.memset(idx_out[:], SKIP)
            V.memset(pay_out[:], 0)
            V.memset(row[:], 0.0)
            dve.wait_ge(pool_ready, 1)
            V.tensor_copy(con["iota"][:], iota_i[:])
            V.tensor_copy(e[:], e_i[:])
            dve.wait_ge(edges_in, 7 * 16)
            V.tensor_copy(d[:], dst_i[:])
            V.tensor_copy(s[:], src_i[:])
            then(V.tensor_scalar(tb_i[:], dst_i[:], 7, 7, ALU.arith_shift_right, ALU.logical_shift_left))
            then(V.tensor_copy(tb[:], tb_i[:]))
            own, prev, nxt = slice(1, EC + 1), slice(0, EC), slice(2, EC + 2)
            then(V.tensor_tensor(first[:], tb[:, own], tb[:, prev], ALU.not_equal))
            then(V.tensor_tensor(first[:], first[:], e[:], ALU.mult))
            V.tensor_tensor_scan(start[:], first[:], first[:], 0.0, ALU.max, ALU.max).then_inc(start_ready, 1)
            dve.wait_ge(row_up, 1)
            then(V.tensor_copy(row_in[:], ps_row[0:1, 0:P]))
            V.tensor_tensor_scan(row[0:1, 1:P + 1], row_in[:], row_in[:], 0.0,
                                 ALU.max, ALU.max).then_inc(row_ready, 1)
            dve.wait_ge(row_back, 1)
            then(V.tensor_copy(carry[:], ps_col[:, 0:1]))
            then(V.tensor_scalar(start[:], start[:], carry[:, 0:1], None, ALU.max))
            then(V.tensor_tensor(slot[:], e[:], d[:, own], ALU.subtract))
            then(V.tensor_tensor(slot[:], slot[:], start[:], ALU.subtract))
            then(V.tensor_tensor(slot[:], slot[:], tb[:, own], ALU.add))
            then(V.tensor_tensor(loop[:], d[:, own], d[:, nxt], ALU.not_equal))
            then(V.tensor_tensor(tmp[:], d[:, own], s[:], ALU.is_equal))
            then(V.tensor_tensor(loop[:], loop[:], tmp[:], ALU.mult))
            then(V.tensor_scalar(link[:], e[:], float(pl.E), None, ALU.is_lt))
            then(V.tensor_tensor(link[:], link[:], loop[:], ALU.subtract))
            then(V.tensor_scalar(tmp[:], tb[:, own], 1.0 / P, float(SKIP), ALU.mult, ALU.add))
            then(V.scalar_tensor_tensor(out=tmp[:], in0=slot[:], scalar=float(NT), in1=tmp[:],
                                        op0=ALU.mult, op1=ALU.add))
            then(V.scalar_tensor_tensor(out=idx_out[:, 0:EC], in0=link[:], scalar=-float(SKIP), in1=tmp[:],
                                        op0=ALU.mult, op1=ALU.add))
            V.tensor_copy(pay_out[:, 0:EC, 0], src_i[:])
            V.tensor_copy(con["edge_src"][:], src_i[:])
            V.tensor_copy(con["edge_dst"][:], dst_i[:, own])
            then(V.tensor_tensor(pay_out[:, 0:EC, 1], d[:, own], tb[:, own], ALU.subtract))
            then(V.tensor_tensor(tmp[:], d[:, own], d[:, prev], ALU.is_lt))
            then(V.tensor_reduce(sums[:, 0:1], tmp[:], AX.X, ALU.add))
            then(V.tensor_scalar(tmp[:], slot[:], P - 0.5, None, ALU.is_gt))
            then(V.tensor_tensor(tmp[:], tmp[:], link[:], ALU.mult))
            then(V.tensor_reduce(sums[:, 1:2], tmp[:], AX.X, ALU.add))
            V.tensor_reduce(sums[:, 2:3], loop[:], AX.X, ALU.add).then_inc(sums_ready, 1)
            dve.wait_ge(sums_up, 1)
            then(V.tensor_copy(total[:], ps_row[0:1, 0:3]))
            then(V.tensor_scalar(total[0:1, 2:3], total[0:1, 2:3], float(pl.N), None, ALU.not_equal))
            then(V.tensor_reduce(bad[:], total[:], AX.X, ALU.add))
            then(V.tensor_scalar(con["flag"][:], bad[:], 0.5, None, ALU.is_lt))


def project(nc, pl, con, x, weights, biases, qv_dram, ks_dram, link_dram, idx, pay):
    D, C, H, hd = pl.D, pl.C, pl.H, pl.hd
    KW = D + H
    with ExitStack() as ctx:
        def sb(n, s, d=F32):
            return ctx.enter_context(nc.sbuf_tensor("proj_" + n, s, d))

        def ps(n):
            return ctx.enter_context(nc.psum_tensor("proj_" + n, [P, 512], F32))

        def sem(n):
            return ctx.enter_context(nc.semaphore("proj_" + n))
        wraw = sb("wraw", [P, 3 * C, D])
        wT = sb("wT", [P, C, 3 * D])
        bias = sb("bias", [P, 3 * D])
        xq = [sb(f"xq{u}", [P, QT, D]) for u in range(2)]
        st, mv = sb("st", [P, 2, QT, 6]), sb("mv", [P, 2, QT, 2])
        sd, rstd, nmr = sb("sd", [P, 2, QT]), sb("rstd", [P, 2, QT]), sb("nmr", [P, 2, QT])
        h = sb("h", [P, 2, D])
        hT = sb("hT", [P, 2, D])
        prod = sb("prod", [P, D])
        qv = [sb(f"qv{u}", [P, QT, 2 * D]) for u in range(2)]
        ks = [sb(f"ks{u}", [P, QT, KW]) for u in range(2)]
        sidx, spay = sb("sidx", [P, 2, 8], I32), sb("spay", [P, 2, 16], I32)
        psT, psQK, psV = [ps(f"psT{b}") for b in range(2)], [ps(f"psQK{b}") for b in range(2)], [ps(f"psV{b}") for b in range(2)]
        w_in, w_up, w_ready, x_clear = sem("w_in"), sem("w_up"), sem("w_ready"), sem("x_clear")
        tail_in = sem("tail_in")
        x_in = [sem(f"x_in{u}") for u in range(2)]
        qv_out = [sem(f"qv_out{u}") for u in range(2)]
        h_free_of_x = sem("x_read")
        stats, var, std, rs, norm = sem("stats"), sem("var"), sem("std"), sem("rs"), sem("norm")
        h_ready, hT_up, hT_ready, qkv_up, qkv_read, ks_step = (sem("h_ready"), sem("hT_up"), sem("hT_ready"),
                                                      sem("qkv_up"), sem("qkv_read"), sem("ks_step"))
        prod_ready = sem("prod_ready")
        qv_ready = sem("qv_ready")
        passed = sem("passed")
        staged, scattered = sem("staged"), [sem(f"scattered{b}") for b in range(2)]
        block = ctx.enter_context(nc.Block())
        last = pl.turns - 1

        @block.sync
        def _(sp):
            for m, w in enumerate(weights):
                for c in range(C):
                    sp.dma_start(wraw[:, m * C + c, :], w[c * P:(c + 1) * P, :]).then_inc(w_in, 16)
            for m, b in enumerate(biases):
                sp.dma_start(bias[:, m * D:(m + 1) * D],
                             b.rearrange("(o d) -> o d", o=1).to_broadcast([P, D])).then_inc(w_in, 16)
            sp.wait_ge(x_clear, 1)

            def load(i, u):
                sp.wait_ge(h_free_of_x, 2 * i + u + 1)
                sp.dma_start(xq[u][:], quad_rows(x, i * (BODY * P) + u * pl.QR)).then_inc(x_in[u], 16)

            def store(i, u):
                sp.wait_ge(qv_ready, 2 * i + u + 1)
                at = i * (BODY * P) + u * pl.QR
                sp.dma_start(quad_rows(qv_dram, at), qv[u][:]).then_inc(qv_out[u], 16)
                sp.dma_start(quad_rows(ks_dram, at), ks[u][:]).then_inc(qv_out[u], 16)
            sp.sem_inc(qv_out[0], 32)
            sp.sem_inc(qv_out[1], 32)
            load(0, 0)
            load(0, 1)
            with sp.Fori(0, last - 1) as i:
                load(i + 1, 0)
                store(i, 0)
                load(i + 1, 1)
                store(i, 1)
            load(last, 0)
            store(last - 1, 0)
            sp.wait_ge(h_free_of_x, 2 * last + 2)
            parts = ragged(x, last * BODY * P + pl.QR, pl.last_rows, xq[1])
            for dram, tile in parts[:-1]:
                sp.dma_start(tile, dram).then_inc(tail_in, 16)
            if len(parts) > 1:
                sp.wait_ge(tail_in, 16)
            sp.dma_start(parts[-1][1], parts[-1][0]).then_inc(x_in[1], 16)
            store(last - 1, 1)
            store(last, 0)
            store(last, 1)
            for u in range(2):
                sp.wait_ge(qv_out[u], 32 * (pl.turns + 1))

        @where(block.gpsimd, con, True)
        def _(pool):
            bound = pool.to_reg(P * pl.NT - 1)

            def scatter(i, b, first):
                if not first:
                    pool.wait_ge(scattered[b], i * 128)
                nc.gpsimd.tensor_copy(sidx[:, b, :], idx[:, bass.ds(i * 16 + b * 8, 8)])
                nc.gpsimd.tensor_copy(spay[:, b, :],
                                      pay[:].rearrange("p e w -> p (e w)")[:, bass.ds(i * 32 + b * 16, 16)]
                                      ).then_inc(staged, 1)
                pool.wait_ge(staged, i * 2 + b + 1)
                pool.sem_inc(passed, 1)
                for c in range(8):
                    nc.gpsimd.indirect_dma_start(
                        out=link_dram[:, :], out_offset=bass.IndirectOffsetOnAxis(ap=sidx[:, b, c:c + 1], axis=0),
                        in_=spay[:, b, 2 * c:2 * c + 2], in_offset=None,
                        bounds_check=bound, oob_is_err=False).then_inc(scattered[b], 16)
            scatter(0, 0, True)
            scatter(0, 1, True)
            with pool.Fori(1, pl.EB // 16) as i:
                scatter(i, 0, False)
                scatter(i, 1, False)
            for b in range(2):
                pool.wait_ge(scattered[b], 128 * (pl.EB // 16))

        def tiles(body):
            return [body(k) for k in range(BODY)]

        @block.tensor
        def _(pe):
            pe.wait_ge(w_in, 16 * 3 * (C + 1))
            for m in range(3):
                for c in range(C):
                    for r in range(C):
                        n = (m * C + c) * C + r
                        if n >= 2:
                            pe.wait_ge(w_ready, n - 1)
                        nc.tensor.transpose(psT[n % 2][:, 0:P], wraw[:, m * C + c, r * P:(r + 1) * P],
                                            con["ident"][:]).then_inc(w_up, 1)
            pe.wait_ge(w_ready, 3 * C * C)
            pe.sem_inc(hT_up, 2)

            def up(n, b):
                pe.wait_ge(h_ready, n + 1)
                pe.wait_ge(hT_ready, n + 1)
                for c in range(C):
                    ins = nc.tensor.transpose(psT[b][:, c * P:(c + 1) * P], h[:, b, c * P:(c + 1) * P], con["ident"][:])
                ins.then_inc(hT_up, 1)

            def products(n, b):
                pe.wait_ge(hT_ready, n + 3)
                pe.wait_ge(qkv_read, n + 1)
                for c in range(C):
                    nc.tensor.matmul(psQK[b][:, :], hT[:, b, c * P:(c + 1) * P], wT[:, c, 0:2 * D],
                                     start=(c == 0), stop=(c == C - 1))
                for c in range(C):
                    ins = nc.tensor.matmul(psV[b][:, 0:D], hT[:, b, c * P:(c + 1) * P], wT[:, c, 2 * D:3 * D],
                                           start=(c == 0), stop=(c == C - 1))
                ins.then_inc(qkv_up, 1)
            up(0, 0)

            def turn(i, end):
                for k in range(BODY):
                    n = i * BODY + k
                    if not (end and k == BODY - 1):
                        up(n + 1, (k + 1) % 2)
                    products(n, k % 2)
            with pe.Fori(0, last) as i:
                turn(i, False)
            turn(last, True)

        @block.scalar
        def _(act):
            n = 0
            for m in range(3):
                for c in range(C):
                    for r in range(C):
                        act.wait_ge(w_up, n + 1)
                        nc.scalar.copy(wT[:, r, m * D + c * P:m * D + (c + 1) * P], psT[n % 2][:, 0:P]).then_inc(w_ready, 1)
                        n += 1
            act.sem_inc(hT_ready, 2)
            act.sem_inc(h_free_of_x, 2)

            def deviation(i, u):
                act.wait_ge(var, 2 * i + u + 1)
                nc.scalar.activation(sd[:, u, :], mv[:, u, :, 1], ACT.Sqrt, bias=con["eps"][:, 0:1]).then_inc(std, 1)

            def normalize(i, k):
                u, t, n = k // QT, k % QT, i * BODY + k
                if t == 0:
                    act.wait_ge(norm, 2 * i + u + 1)
                act.wait_ge(hT_up, n + 1)
                ins = nc.scalar.activation(h[:, k % 2, :], xq[u][:, t, :], ACT.Relu,
                                           bias=nmr[:, u, t:t + 1], scale=rstd[:, u, t:t + 1])
                ins.then_inc(h_ready, 1)
                if t == QT - 1:
                    act.wait_ge(h_ready, n + 1)
                    act.sem_inc(h_free_of_x, 1)

            def keep(i, k):
                n = i * BODY + k
                act.wait_ge(hT_up, n + 3)
                act.wait_ge(qkv_up, n + 1)
                nc.scalar.copy(hT[:, k % 2, :], psT[k % 2][:, 0:D]).then_inc(hT_ready, 1)
            deviation(0, 0)

            def turn(i, end):
                for k in range(BODY):
                    normalize(i, k)
                    if k == 1:
                        deviation(i, 1)
                    if k == QT + 1 and not end:
                        deviation(i + 1, 0)
                    keep(i, k)
            with act.Fori(0, last) as i:
                turn(i, False)
            turn(last, True)

        @block.vector
        def _(dve):
            V = nc.vector
            V.memset(xq[1][:], 0.0).then_inc(x_clear, 1)
            dve.sem_inc(qkv_read, 2)
            dve.wait_ge(w_in, 16 * 3 * (C + 1))
            dve.sem_inc(qkv_up, 2)

            def statistics(i, u):
                q = 2 * i + u
                dve.wait_ge(x_in[u], i * 16 + 16)
                for t in range(QT):
                    ins = V.bn_stats(st[:, u, t, :], xq[u][:, t, :])
                ins.then_inc(stats, 1)
                dve.wait_ge(stats, q + 1)
                dve.sem_inc(passed, 1)
                for t in range(QT):
                    ins = V.bn_aggr(mv[:, u, t, :], st[:, u, t, :])
                ins.then_inc(var, 1)

            def shift(i, u):
                q = 2 * i + u
                dve.wait_ge(std, q + 1)
                V.reciprocal(rstd[:, u, :], sd[:, u, :]).then_inc(rs, 1)
                dve.wait_ge(rs, q + 1)
                V.scalar_tensor_tensor(out=nmr[:, u, :], in0=mv[:, u, :, 0], scalar=-1.0, in1=rstd[:, u, :],
                                       op0=ALU.mult, op1=ALU.mult).then_inc(norm, 1)

            def collect(i, k):
                u, t, n, b = k // QT, k % QT, i * BODY + k, k % 2
                dve.wait_ge(qkv_up, n + 3)
                if t == 0:
                    dve.wait_ge(qv_out[u], i * 32 + 32)
                V.tensor_tensor(qv[u][:, t, 0:D], psQK[b][:, 0:D], bias[:, 0:D], ALU.add)
                V.tensor_tensor(ks[u][:, t, 0:D], psQK[b][:, D:2 * D], bias[:, D:2 * D], ALU.add).then_inc(ks_step, 1)
                V.tensor_tensor(qv[u][:, t, D:2 * D], psV[b][:, 0:D], bias[:, 2 * D:3 * D], ALU.add).then_inc(qkv_read, 1)
                dve.wait_ge(ks_step, n + 1)
                V.tensor_tensor(prod[:], qv[u][:, t, 0:D], ks[u][:, t, 0:D], ALU.mult).then_inc(prod_ready, 1)
                dve.wait_ge(prod_ready, n + 1)
                ins = V.tensor_reduce(ks[u][:, t, D:KW], prod[:].rearrange("p (h d) -> p h d", h=H), AX.X, ALU.add)
                if t == QT - 1:
                    ins.then_inc(qv_ready, 1)
            statistics(0, 0)
            shift(0, 0)

            def turn(i, end):
                for k in range(BODY):
                    if k == 0:
                        statistics(i, 1)
                    if k == QT and not end:
                        statistics(i + 1, 0)
                    collect(i, k)
                    if k == 1:
                        shift(i, 1)
                    if k == QT + 1 and not end:
                        shift(i + 1, 0)
            with dve.Fori(0, last) as i:
                turn(i, False)
            turn(last, True)


def attend(nc, pl, con, x, w_out, b_out, qv_dram, ks_dram, link_dram, mask_embed, x1_dram, h_dram):
    D, C, H, hd, NT = pl.D, pl.C, pl.H, pl.hd, pl.NT
    KW, QH = D + H, QT * H
    SCALE = float(hd) ** -0.5
    with ExitStack() as ctx:
        def sb(n, s, d=F32):
            return ctx.enter_context(nc.sbuf_tensor("att_" + n, s, d))

        def ps(n):
            return ctx.enter_context(nc.psum_tensor("att_" + n, [P, 512], F32))

        def sem(n):
            return ctx.enter_context(nc.semaphore("att_" + n))
        wraw, wT, bias = sb("wo_raw", [P, C, D]), sb("woT", [P, C, D]), sb("bo", [P, D])
        rows = [sb(f"rows{u}", [P, QT, 2 * D]) for u in range(2)]
        ks = [sb(f"ksn{u}", [P, QT, KW]) for u in range(2)]
        xs = [sb(f"xs{u}", [P, QT, D]) for u in range(2)]
        vs = [sb(f"vs{u}", [P, QT, D]) for u in range(2)]
        hot = [sb(f"hot{u}", [P, QT, P]) for u in range(2)]
        lidx, ldst = sb("lidx", [P, 2, QT], I32), sb("ldst", [P, 2, QT])
        hotT = sb("hotT", [P, 2, P])
        prod, pv = sb("prod", [P, 2, D]), sb("pv", [P, 2, D])
        slot_sc = sb("slot_sc", [P, 3, QT, H])
        tsc = sb("tsc", [QH, 3, P])
        same, cut = sb("same", [QH, P + 1]), sb("cut", [QH, P + 1])
        top, fwd, bwd = sb("top", [QH, P]), sb("fwd", [QH, P]), sb("bwd", [QH, P])
        dif, ex, tot = sb("dif", [QH, 2, P]), sb("ex", [QH, 2, P]), sb("tot", [QH, P])
        tp = sb("tp", [QH, 3, P])
        pr = sb("pr", [P, QT, H])
        fin = sb("fin", [P, QT, 2 * H + 1])
        own = sb("own", [P, QT, 2 * H + 1])
        pself = sb("pself", [P, QT, H])
        vself = sb("vself", [P, QT, D])
        o, oT = sb("o", [P, 2, D]), sb("oT", [P, 2, D])
        x1 = [sb(f"x1_{u}", [P, QT, D]) for u in range(2)]
        ho = [sb(f"ho{u}", [P, QT, D]) for u in range(2)]
        st, mv = sb("st2", [P, QT, 6]), sb("mv2", [P, QT, 2])
        sd, rstd, nmr = sb("sd2", [P, QT]), sb("rstd2", [P, QT]), sb("nmr2", [P, QT])
        ps_hot, ps_k = ps("ps_hot"), [ps("ps_k0"), ps("ps_k1")]
        ps_sm, ps_g, ps_o, ps_p = ps("ps_sm"), [ps("ps_g0"), ps("ps_g1")], ps("ps_oT"), ps("ps_p")

        setup_in, bufs_clear, w_up, w_ready = sem("setup_in"), sem("bufs_clear"), sem("w_up"), sem("w_ready")
        table_ready, staged = sem("table_ready"), sem("staged")
        rows_in = [sem(f"rows_in{u}") for u in range(2)]
        ks_in, xs_in, vs_in = ([sem(f"{n}{u}") for u in range(2)] for n in ("ks_in", "xs_in", "vs_in"))
        hot_ready, hot_up, hotT_ready = sem("hot_ready"), sem("hot_up"), sem("hotT_ready")
        k_up, prod_ready, k_read = sem("k_up"), sem("prod_ready"), sem("k_read")
        score_ready, sc_up, tsc_ready = sem("score_ready"), sem("sc_up"), sem("tsc_ready")
        dif_ready, ex_ready, tp_ready, tp_up, pr_ready = (sem("dif_ready"), sem("ex_ready"), sem("tp_ready"),
                                                          sem("tp_up"), sem("pr_ready"))
        own_up, own_ready, pself_ready, vself_ready = (sem("own_up"), sem("own_ready"), sem("pself_ready"),
                                                       sem("vself_ready"))
        pv_ready, g_up, o_ready, o_up, oT_ready, p_up, x1_tile = (
            sem("pv_ready"), sem("g_up"), sem("o_ready"), sem("o_up"), sem("oT_ready"), sem("p_up"), sem("x1_tile"))
        soft, own_read = sem("soft"), sem("own_read")
        var, std, norm, h_ready = sem("var"), sem("std"), sem("norm"), sem("h_ready")
        vstep = sem("vstep")
        x1_out = [sem(f"x1_out{u}") for u in range(2)]
        h_out = [sem(f"h_out{u}") for u in range(2)]
        mask_out = sem("mask_out")
        passed = sem("passed")
        block = ctx.enter_context(nc.Block())
        last = pl.turns - 1

        @where(block.sync, con, True)
        def _(sp):
            for c in range(C):
                sp.dma_start(wraw[:, c, :], w_out[c * P:(c + 1) * P, :]).then_inc(setup_in, 16)
            sp.dma_start(bias[:], b_out.rearrange("(o d) -> o d", o=1).to_broadcast([P, D])).then_inc(setup_in, 16)
            sp.dma_start(con["links"][:], link_dram.rearrange("(p t) w -> p t w", p=P)).then_inc(setup_in, 16)
            sp.wait_ge(bufs_clear, 1)
            for u in range(2):
                sp.sem_inc(x1_out[u], 16)
                sp.sem_inc(h_out[u], 16)

            def load(i, u):
                q = 2 * i + u
                at = i * (BODY * P) + u * pl.QR
                sp.wait_ge(k_read, q * QT + QT)
                sp.dma_start(ks[u][:], quad_rows(ks_dram, at)).then_inc(ks_in[u], 16)
                sp.wait_ge(vself_ready, q + 1)
                sp.dma_start(vs[u][:], quad_rows(qv_dram, at, (D, 2 * D))).then_inc(vs_in[u], 16)
                sp.wait_ge(x1_tile, q * QT + QT)

            def load_x(i, u):
                sp.dma_start(xs[u][:], quad_rows(x, i * (BODY * P) + u * pl.QR)).then_inc(xs_in[u], 16)

            def store(i, u):
                q = 2 * i + u
                at = i * (BODY * P) + u * pl.QR
                sp.wait_ge(h_ready, q + 2)
                sp.dma_start(quad_rows(x1_dram, at), x1[u][:]).then_inc(x1_out[u], 16)
                sp.dma_start(quad_rows(h_dram, at), ho[u][:]).then_inc(h_out[u], 16)
            for u in range(2):
                load(0, u)
                load_x(0, u)
            with sp.Fori(0, last - 1) as i:
                for u in range(2):
                    load(i + 1, u)
                    load_x(i + 1, u)
                    store(i, u)
            load(last, 0)
            load_x(last, 0)
            store(last - 1, 0)
            load(last, 1)
            parts = ragged(x, last * BODY * P + pl.QR, pl.last_rows, xs[1])
            for dram, tile in parts[:-1]:
                sp.dma_start(tile, dram).then_inc(mask_out, 16)
            if len(parts) > 1:
                sp.wait_ge(mask_out, 16)
            sp.dma_start(parts[-1][1], parts[-1][0]).then_inc(xs_in[1], 16)
            store(last - 1, 1)
            store(last, 0)
            store(last, 1)
            for u in range(2):
                sp.wait_ge(x1_out[u], 16 * (pl.turns + 1))
                sp.wait_ge(h_out[u], 16 * (pl.turns + 1))
            sp.dma_start(h_dram[0:1, :], mask_embed.rearrange("(o d) -> o d", o=1)).then_inc(mask_out, 16)
            sp.wait_ge(mask_out, 16 * len(parts))

        @where(block.gpsimd, con, True)
        def _(pool):
            for u in range(2):
                nc.gpsimd.memset(rows[u][:], 0.0)
            nc.gpsimd.memset(xs[1][:], 0.0).then_inc(bufs_clear, 1)
            pool.wait_ge(setup_in, 16 * (C + 2))
            nc.gpsimd.tensor_copy(con["dloc"][:], con["links"][:, :, 1]).then_inc(table_ready, 1)
            pool.wait_ge(table_ready, 1)
            pool.wait_ge(bufs_clear, 1)
            pool.sem_inc(vself_ready, 2)
            bound = pool.to_reg(pl.NP - 1)

            def fetch(i, u):
                q = 2 * i + u
                pool.wait_ge(g_up, q * QT + QT)
                nc.gpsimd.tensor_copy(lidx[:, u, :], con["links"][:, bass.ds(i * BODY + u * QT, QT), 0])
                nc.gpsimd.tensor_copy(ldst[:, u, :], con["dloc"][:, bass.ds(i * BODY + u * QT, QT)]).then_inc(staged, 1)
                pool.wait_ge(staged, q + 1)
                pool.sem_inc(passed, 1)
                for t in range(QT):
                    nc.gpsimd.indirect_dma_start(
                        out=rows[u][:, t, :], out_offset=None, in_=qv_dram[:, :],
                        in_offset=bass.IndirectOffsetOnAxis(ap=lidx[:, u, t:t + 1], axis=0),
                        bounds_check=bound, oob_is_err=False).then_inc(rows_in[u], 16)
                for t in range(QT):
                    ins = nc.gpsimd.tensor_scalar(hot[u][:, t, :], con["iota"][:], ldst[:, u, t:t + 1], None, ALU.is_equal)
                ins.then_inc(hot_ready, 1)

            def weigh_own(i, u):
                q = 2 * i + u
                pool.wait_ge(vs_in[u], i * 16 + 16)
                pool.wait_ge(o_ready, q * QT + 2)
                pool.wait_ge(pself_ready, q + 1)
                nc.gpsimd.tensor_tensor(vself[:].rearrange("p t (h d) -> p (t h) d", h=H),
                                        vs[u][:].rearrange("p t (h d) -> p (t h) d", h=H),
                                        pself[:].rearrange("p t h -> p (t h)").to_broadcast([P, QH, hd]),
                                        ALU.mult).then_inc(vself_ready, 1)
            fetch(0, 0)

            def turn(i, end):
                fetch(i, 1)
                weigh_own(i, 0)
                if not end:
                    fetch(i + 1, 0)
                weigh_own(i, 1)
            with pool.Fori(0, last) as i:
                turn(i, False)
            turn(last, True)

        @where(block.tensor, con, True)
        def _(pe):
            pe.wait_ge(setup_in, 16 * (C + 2))
            for n in range(C * C):
                c, r = n // C, n % C
                if n:
                    pe.wait_ge(w_ready, n)
                nc.tensor.transpose(ps_hot[:, 0:P], wraw[:, c, r * P:(r + 1) * P], con["ident"][:]).then_inc(w_up, 1)
            pe.wait_ge(w_ready, C * C)
            pe.sem_inc(g_up, 2 * QT)

            def expand(i, u):
                q = 2 * i + u
                pe.wait_ge(hot_ready, q + 1)
                pe.wait_ge(ks_in[u], i * 16 + 16)
                for t in range(QT):
                    n = q * QT + t
                    pe.wait_ge(hotT_ready, n + 1)
                    nc.tensor.transpose(ps_hot[:, 0:P], hot[u][:, t, :], con["ident"][:]).then_inc(hot_up, 1)
                    pe.wait_ge(hotT_ready, n + 2)
                    pe.wait_ge(k_read, n + 7)
                    nc.tensor.matmul(ps_k[t % 2][:, 0:KW], hotT[:, t % 2, :], ks[u][:, t, :],
                                     start=True, stop=True).then_inc(k_up, 1)

            def turn_scores(i, u):
                q = 2 * i + u
                pe.wait_ge(score_ready, q + 1)
                pe.wait_ge(own_ready, q + 1)
                for a in range(3):
                    ins = nc.tensor.transpose(ps_sm[0:QH, a * P:(a + 1) * P],
                                              slot_sc[:, a, :, :].rearrange("p t h -> p (t h)"), con["ident"][:])
                ins.then_inc(sc_up, 1)
                pe.wait_ge(tp_ready, q + 1)
                pe.sem_inc(passed, 1)
                for a in range(3):
                    ins = nc.tensor.transpose(ps_sm[:, a * QH:(a + 1) * QH], tp[:, a, :], con["ident"][0:QH, 0:QH])
                ins.then_inc(tp_up, 1)

            def own_shares(i, u):
                q = 2 * i + u
                pe.wait_ge(pr_ready, q + 1)
                for t in range(QT):
                    ins = nc.tensor.matmul(ps_sm[:, t * 32:t * 32 + 2 * H + 1], hot[u][:, t, :], fin[:, t, :],
                                           start=True, stop=True)
                ins.then_inc(own_up, 1)

            def gather_up(i, u):
                q = 2 * i + u
                for t in range(QT):
                    n = q * QT + t
                    pe.wait_ge(pv_ready, n + 1)
                    pe.wait_ge(o_ready, n + 1)
                    nc.tensor.matmul(ps_g[t % 2][:, 0:D], hot[u][:, t, :], pv[:, t % 2, :],
                                     start=True, stop=True).then_inc(g_up, 1)
                    if t:
                        project_out(n - 1, t - 1)
                project_out(q * QT + QT - 1, QT - 1)

            def project_out(n, t):
                pe.wait_ge(o_ready, n + 3)
                pe.wait_ge(oT_ready, n + 1)
                for c in range(C):
                    ins = nc.tensor.transpose(ps_o[:, c * P:(c + 1) * P], o[:, t % 2, c * P:(c + 1) * P], con["ident"][:])
                ins.then_inc(o_up, 1)
                pe.wait_ge(oT_ready, n + 2)
                pe.wait_ge(x1_tile, n + 8)
                for c in range(C):
                    ins = nc.tensor.matmul(ps_p[:, 0:D], oT[:, t % 2, c * P:(c + 1) * P], wT[:, c, :],
                                           start=(c == 0), stop=(c == C - 1))
                ins.then_inc(p_up, 1)
            expand(0, 0)

            def turn(i, end):
                turn_scores(i, 0)
                expand(i, 1)
                own_shares(i, 0)
                gather_up(i, 0)
                turn_scores(i, 1)
                if not end:
                    expand(i + 1, 0)
                own_shares(i, 1)
                gather_up(i, 1)
            with pe.Fori(0, last) as i:
                turn(i, False)
            turn(last, True)

        @where(block.scalar, con, True)
        def _(act):
            for n in range(C * C):
                c, r = n // C, n % C
                act.wait_ge(w_up, n + 1)
                nc.scalar.copy(wT[:, r, c * P:(c + 1) * P], ps_hot[:, 0:P]).then_inc(w_ready, 1)
            act.sem_inc(hotT_ready, 1)
            act.sem_inc(oT_ready, 1)
            act.sem_inc(h_ready, 1)

            def keep_hot(i, u):
                q = 2 * i + u
                for t in range(QT):
                    n = q * QT + t
                    act.wait_ge(hot_up, n + 1)
                    act.wait_ge(k_up, n + 1)
                    nc.scalar.copy(hotT[:, t % 2, :], ps_hot[:, 0:P]).then_inc(hotT_ready, 1)

            def exponent(i, u):
                act.wait_ge(dif_ready, 2 * i + u + 1)
                nc.scalar.activation(ex[:], dif[:], ACT.Exp, scale=SCALE).then_inc(ex_ready, 1)

            def keep_o(i, u):
                q = 2 * i + u
                for t in range(QT):
                    n = q * QT + t
                    act.wait_ge(o_up, n + 1)
                    act.wait_ge(p_up, n + 1)
                    nc.scalar.copy(oT[:, t % 2, :], ps_o[:, 0:D]).then_inc(oT_ready, 1)

            def normalize(i, u):
                q = 2 * i + u
                act.wait_ge(var, q + 1)
                nc.scalar.activation(sd[:], mv[:, :, 1], ACT.Sqrt, bias=con["eps"][:, 0:1]).then_inc(std, 1)
                act.wait_ge(norm, q + 1)
                act.wait_ge(h_out[u], i * 16 + 16)
                for t in range(QT):
                    ins = nc.scalar.activation(ho[u][:, t, :], x1[u][:, t, :], ACT.Relu,
                                               bias=nmr[:, t:t + 1], scale=rstd[:, t:t + 1])
                ins.then_inc(h_ready, 1)
            keep_hot(0, 0)

            def turn(i, end):
                exponent(i, 0)
                keep_hot(i, 1)
                keep_o(i, 0)
                normalize(i, 0)
                exponent(i, 1)
                if not end:
                    keep_hot(i + 1, 0)
                keep_o(i, 1)
                normalize(i, 1)
            with act.Fori(0, last) as i:
                turn(i, False)
            turn(last, True)

        @where(block.vector, con, True)
        def _(dve):
            V = nc.vector
            dve.wait_ge(setup_in, 16 * (C + 2))
            V.memset(same[:, 0:1], 0.0)
            V.memset(same[:, P:P + 1], 0.0)
            V.memset(fin[:], 1.0).then_inc(vstep, 1)
            dve.sem_inc(k_read, 2 * QT)
            dve.sem_inc(k_up, 2)
            dve.sem_inc(own_ready, 1)
            dve.sem_inc(o_ready, 2)
            dve.sem_inc(p_up, 2)
            dve.sem_inc(x1_tile, 2 * QT)
            dve.wait_ge(vstep, 1)

            def scores(i, u):
                q = 2 * i + u
                dve.wait_ge(rows_in[u], i * (16 * QT) + 16 * QT)
                dve.wait_ge(staged, q + 1)
                dve.wait_ge(sc_up, q + 1)
                V.tensor_copy(slot_sc[:, 2, :, :], ldst[:, u, :].to_broadcast([P, QT, H]))
                for t in range(QT):
                    n = q * QT + t
                    dve.wait_ge(k_up, n + 3)
                    V.tensor_tensor(prod[:, t % 2, :], rows[u][:, t, 0:D], ps_k[t % 2][:, 0:D], ALU.mult).then_inc(prod_ready, 1)
                    V.tensor_copy(slot_sc[:, 1, t, :], ps_k[t % 2][:, D:KW]).then_inc(k_read, 1)
                    dve.wait_ge(prod_ready, n + 1)
                    ins = V.tensor_reduce(slot_sc[:, 0, t, :], prod[:, t % 2, :].rearrange("p (h d) -> p h d", h=H),
                                          AX.X, ALU.add)
                ins.then_inc(score_ready, 1)

            def softmax(i, u):
                q = 2 * i + u
                step = [0]
                STEPS = 11

                def then(ins):
                    step[0] += 1
                    ins.then_inc(soft, 1)
                    dve.wait_ge(soft, q * STEPS + step[0])
                dve.wait_ge(sc_up, q + 2)
                then(V.tensor_copy(tsc[:], ps_sm[0:QH, 0:3 * P].rearrange("p (a s) -> p a s", a=3)))
                V.tensor_tensor(top[:], tsc[:, 0, :], tsc[:, 1, :], ALU.max)
                then(V.tensor_tensor(same[:, 1:P], tsc[:, 2, 1:P], tsc[:, 2, 0:P - 1], ALU.is_equal))
                then(V.tensor_scalar(cut[:], same[:], -1.0, NEG, ALU.add, ALU.mult))
                V.tensor_tensor_scan(fwd[:], cut[:, 0:P], top[:], 0.0, ALU.add, ALU.max)
                then(V.tensor_tensor_scan(bwd[:, ::-1], cut[:, 1:P + 1][:, ::-1], top[:, ::-1], 0.0, ALU.add, ALU.max))
                then(V.tensor_tensor(fwd[:], fwd[:], bwd[:], ALU.max))
                V.tensor_tensor(dif[:, 0, :], tsc[:, 0, :], fwd[:], ALU.subtract)
                V.tensor_tensor(dif[:, 1, :], tsc[:, 1, :], fwd[:], ALU.subtract).then_inc(dif_ready, 1)
                dve.wait_ge(ex_ready, q + 1)
                V.tensor_tensor_scan(fwd[:], same[:, 0:P], ex[:, 0, :], 0.0, ALU.mult, ALU.add)
                V.tensor_tensor_scan(bwd[:, ::-1], same[:, 1:P + 1][:, ::-1], ex[:, 0, ::-1], 0.0, ALU.mult, ALU.add)
                then(V.tensor_tensor(tot[:], ex[:, 1, :], ex[:, 0, :], ALU.subtract))
                then(V.tensor_tensor(fwd[:], fwd[:], bwd[:], ALU.add))
                then(V.tensor_tensor(tot[:], tot[:], fwd[:], ALU.add))
                then(V.reciprocal(tot[:], tot[:]))
                V.tensor_scalar(tp[:, 2, :], same[:, 1:P + 1], -1.0, 1.0, ALU.mult, ALU.add)
                then(V.tensor_tensor(bwd[:], ex[:, 1, :], tot[:], ALU.mult))
                V.tensor_tensor(tp[:, 0, :], ex[:, 0, :], tot[:], ALU.mult)
                V.tensor_tensor(tp[:, 1, :], bwd[:], tp[:, 2, :], ALU.mult).then_inc(tp_ready, 1)
                dve.wait_ge(tp_up, q + 1)
                then(V.tensor_copy(pr[:].rearrange("p t h -> p (t h)"), ps_sm[:, 0:QH]))
                V.tensor_copy(fin[:, :, 0:H], ps_sm[:, QH:2 * QH].rearrange("p (t h) -> p t h", h=H))
                V.tensor_copy(fin[:, :, H:2 * H],
                              ps_sm[:, 2 * QH:3 * QH].rearrange("p (t h) -> p t h", h=H)).then_inc(pr_ready, 1)
                assert step[0] == STEPS, step

            def settle(i, u):
                q = 2 * i + u
                dve.wait_ge(own_up, q + 1)
                V.tensor_copy(own[:], ps_sm[:, 0:QT * 32].rearrange("p (t w) -> p t w", t=QT)[:, :, 0:2 * H + 1]
                              ).then_inc(own_read, 1)
                dve.wait_ge(own_read, q + 1)
                V.tensor_tensor(pself[:], own[:, :, 0:H], own[:, :, H:2 * H], ALU.subtract).then_inc(own_ready, 1)
                V.tensor_scalar(con["deg"][:, bass.ds(i * BODY + u * QT, QT)], own[:, :, 2 * H], 1.0, None, ALU.add)
                dve.wait_ge(own_ready, q + 2)
                V.tensor_scalar(pself[:], pself[:], 1.0, None, ALU.add).then_inc(pself_ready, 1)

            def combine(i, u):
                q = 2 * i + u

                def weigh(t):
                    n = q * QT + t
                    dve.wait_ge(g_up, n + 7)
                    V.tensor_tensor(pv[:, t % 2, :].rearrange("p (h d) -> p h d", h=H),
                                    rows[u][:, t, D:2 * D].rearrange("p (h d) -> p h d", h=H),
                                    pr[:, t, :].to_broadcast([P, H, hd]), ALU.mult).then_inc(pv_ready, 1)

                def finish(t):
                    n = q * QT + t
                    dve.wait_ge(p_up, n + 3)
                    V.tensor_tensor(x1[u][:, t, :], xs[u][:, t, :], ps_p[:, 0:D], ALU.add).then_inc(x1_tile, 1)
                dve.wait_ge(xs_in[u], i * 16 + 16)
                dve.wait_ge(x1_out[u], i * 16 + 16)
                for t in range(QT):
                    V.tensor_tensor(xs[u][:, t, :], xs[u][:, t, :], bias[:], ALU.add)
                weigh(0)
                for t in range(QT):
                    n = q * QT + t
                    if t < QT - 1:
                        weigh(t + 1)
                    if t == 0:
                        dve.wait_ge(vself_ready, q + 3)
                    dve.wait_ge(g_up, n + 9)
                    if t >= 2:
                        dve.wait_ge(o_up, q * QT + t - 1)
                    V.tensor_tensor(o[:, t % 2, :], ps_g[t % 2][:, 0:D], vself[:, t, :], ALU.add).then_inc(o_ready, 1)
                    if t:
                        finish(t - 1)
                finish(QT - 1)
                dve.wait_ge(x1_tile, q * QT + 3 * QT)
                for t in range(QT):
                    ins = V.bn_stats(st[:, t, :], x1[u][:, t, :])
                ins.then_inc(vstep, 1)
                dve.wait_ge(vstep, q * 3 + 2)
                dve.sem_inc(passed, 1)
                for t in range(QT):
                    ins = V.bn_aggr(mv[:, t, :], st[:, t, :])
                ins.then_inc(var, 1)
                dve.wait_ge(std, q + 1)
                dve.wait_ge(h_ready, q + 1)
                V.reciprocal(rstd[:], sd[:]).then_inc(vstep, 1)
                dve.wait_ge(vstep, q * 3 + 3)
                V.scalar_tensor_tensor(out=nmr[:], in0=mv[:, :, 0], scalar=-1.0, in1=rstd[:],
                                       op0=ALU.mult, op1=ALU.mult).then_inc(norm, 1)
                dve.sem_inc(vstep, 1)
            dve.sem_inc(sc_up, 1)
            scores(0, 0)

            def turn(i, end):
                softmax(i, 0)
                scores(i, 1)
                settle(i, 0)
                combine(i, 0)
                softmax(i, 1)
                if not end:
                    scores(i + 1, 0)
                settle(i, 1)
                combine(i, 1)
            with dve.Fori(0, last) as i:
                turn(i, False)
            turn(last, True)
            dve.wait_ge(own_ready, 2 * pl.turns + 1)
            V.reciprocal(con["inv_deg"][:], con["deg"][:])


def clear_signals(nc, signals):
    with nc.Block() as block:
        @block.gpsimd
        def _(pool):
            for s in signals:
                pool.sem_clear(s)


def edge_pass(nc, pl, con, signals, tag, kind, table, width, row_dram, ks_dram=None, top_dram=None, scores=None):
    D, H, hd, EC = pl.D, pl.H, pl.hd, pl.EC
    SCALE = float(hd) ** -0.5
    RW = row_dram.shape[1]
    with ExitStack() as ctx:
        def sb(n, s, d=F32):
            return ctx.enter_context(nc.sbuf_tensor(f"{tag}_{n}", s, d))

        def ps(n):
            return ctx.enter_context(nc.psum_tensor(f"{tag}_{n}", [P, 512], F32))
        isrc, idst, iput = sb("isrc", [P, 1], I32), sb("idst", [P, 1], I32), sb("iput", [P, 1], I32)
        rows, krow, old, new = sb("rows", [P, max(RW, width)]), sb("krow", [P, D + H]), sb("old", [P, width]), sb("new", [P, width])
        topr, val = sb("topr", [P, H]), sb("val", [P, width])
        dstf, wide, same, before = sb("dstf", [P, 1]), sb("wide", [P, P]), sb("same", [P, P]), sb("before", [P, P])
        tmp, cnt, fill = sb("tmp", [P, P]), sb("cnt", [P, 1]), sb("fill", [P, table.shape[1]])
        prod, s8, s8T = sb("prod", [P, D]), sb("s8", [P, H]), sb("s8T", [H, P])
        pick, big = sb("pick", [H, H, P]), sb("big", [P, H, P])
        p_d, p_a, p_b = ps("p_d"), ps("p_a"), ps("p_b")
        fetched, put = nc.alloc_semaphore(f"{tag}_fetched"), nc.alloc_semaphore(f"{tag}_put")
        for n in ("done", "dve_step", "filled", "built", "passed"):
            if n not in signals:
                signals[n] = nc.alloc_semaphore("general_" + n)
        done, dve_step, filled, built, passed = (signals[n] for n in ("done", "dve_step", "filled", "built", "passed"))
        steps = {"max": 11, "weigh": 11, "sum": 8}[kind]

        def reached(i, step):
            return i * steps + step + 1
        gathers = {"max": 3, "weigh": 3, "sum": 2}[kind]
        block = ctx.enter_context(nc.Block())

        @where(block.sync, con, False)
        def _(sp):
            sp.wait_ge(built, 2)
            with sp.Fori(0, pl.NT) as i:
                sp.dma_start(table[bass.ds(i * P, P), :], fill[:]).then_inc(filled, 16)
            sp.wait_ge(filled, 16 * pl.NT)
            sp.sem_inc(done, 1)

        @where(block.gpsimd, con, False)
        def _(pool):
            nc.gpsimd.memset(rows[:], 0.0)
            nc.gpsimd.memset(krow[:], 0.0)
            nc.gpsimd.memset(old[:], 0.0)
            nc.gpsimd.memset(topr[:], 0.0)
            nc.gpsimd.memset(before[:], 1.0)
            nc.gpsimd.memset(pick[:], 1.0).then_inc(passed, 1)
            pool.wait_ge(passed, 1)
            nc.gpsimd.affine_select(out=before[:], in_=before[:], compare_op=ALU.is_gt, fill=0.0, base=0,
                                    pattern=[[-1, P]], channel_multiplier=1)
            nc.gpsimd.affine_select(out=pick[:], in_=pick[:], compare_op=ALU.is_equal, fill=0.0, base=0,
                                    pattern=[[-1, H], [0, P]], channel_multiplier=1).then_inc(built, 1)
            bound = pool.to_reg(pl.NP - 1)

            def gather(out, table_in, idx):
                nc.gpsimd.indirect_dma_start(out=out, out_offset=None, in_=table_in[:, :],
                                             in_offset=bass.IndirectOffsetOnAxis(ap=idx[:, 0:1], axis=0),
                                             bounds_check=bound, oob_is_err=False).then_inc(fetched, 16)
            with pool.Fori(0, EC) as i:
                pool.wait_ge(done, reached(i, 0))
                nc.gpsimd.tensor_copy(isrc[:], con["edge_src"][:, bass.ds(i, 1)])
                nc.gpsimd.tensor_copy(idst[:], con["edge_dst"][:, bass.ds(i, 1)]).then_inc(done, 1)
                pool.wait_ge(done, reached(i, 1))
                pool.sem_inc(passed, 1)
                gather(rows[:, 0:RW], row_dram, isrc)
                gather(old[:], table, idst)
                if kind == "max":
                    gather(krow[:], ks_dram, idst)
                if kind == "weigh":
                    gather(topr[:], top_dram, idst)
                pool.wait_ge(fetched, i * (16 * gathers) + 16 * gathers)
                pool.sem_inc(done, 1)
                pool.wait_ge(done, reached(i, steps - 1))
                pool.sem_inc(passed, 1)
                nc.gpsimd.indirect_dma_start(out=table[:, :],
                                             out_offset=bass.IndirectOffsetOnAxis(ap=iput[:, 0:1], axis=0),
                                             in_=new[:], in_offset=None,
                                             bounds_check=bound, oob_is_err=False).then_inc(put, 16)
                pool.wait_ge(put, i * 16 + 16)
                pool.sem_inc(done, 1)

        @where(block.tensor, con, False)
        def _(pe):
            with pe.Fori(0, EC) as i:
                pe.wait_ge(done, reached(i, 3))
                nc.tensor.transpose(p_d[:, 0:P], wide[:], con["ident"][:]).then_inc(done, 1)
                if kind == "max":
                    pe.wait_ge(done, reached(i, 6))
                    nc.tensor.transpose(p_a[0:H, 0:P], s8[:], con["ident"][:]).then_inc(done, 1)
                    pe.wait_ge(done, reached(i, 8))
                    pe.sem_inc(passed, 1)
                    for h in range(H):
                        ins = nc.tensor.matmul((p_a if h < H // 2 else p_b)[:, (h % (H // 2)) * P:(h % (H // 2) + 1) * P],
                                               pick[:, h, :], s8T[:], start=True, stop=True)
                    ins.then_inc(done, 1)
                else:
                    pe.wait_ge(done, reached(i, 8 if kind == "weigh" else 5))
                    nc.tensor.matmul(p_a[:, 0:width], same[:], val[:] if kind == "weigh" else rows[:, 0:width],
                                     start=True, stop=True).then_inc(done, 1)

        @where(block.scalar, con, False)
        def _(act):
            if kind == "weigh":
                with act.Fori(0, EC) as i:
                    act.wait_ge(done, reached(i, 6))
                    nc.scalar.activation(s8[:], s8[:], ACT.Exp, scale=SCALE).then_inc(done, 1)

        @where(block.vector, con, False)
        def _(dve):
            V = nc.vector
            V.memset(val[:], 1.0)
            V.memset(fill[:], -NEG if kind == "max" else 0.0).then_inc(built, 1)
            heads = lambda v: v.rearrange("p (h d) -> p h d", h=H)
            n = [0]
            per = {"max": 9, "weigh": 6, "sum": 5}[kind]

            def body(i):
                n[0] = 0

                def then(ins):
                    n[0] += 1
                    ins.then_inc(dve_step, 1)
                    dve.wait_ge(dve_step, i * per + n[0])
                dve.wait_ge(done, reached(i, 2))
                then(V.tensor_copy(dstf[:], idst[:]))
                V.tensor_copy(wide[:], dstf[:].to_broadcast([P, P])).then_inc(done, 1)
                dve.wait_ge(done, reached(i, 4))
                then(V.tensor_scalar(same[:], p_d[:, 0:P], dstf[:, 0:1], None, ALU.is_equal))
                then(V.tensor_tensor(tmp[:], same[:], before[:], ALU.mult))
                then(V.tensor_reduce(cnt[:], tmp[:], AX.X, ALU.add))
                then(V.tensor_scalar(cnt[:], cnt[:], 0.5, float(SKIP), ALU.is_gt, ALU.mult))
                V.tensor_tensor(iput[:], cnt[:], dstf[:], ALU.add).then_inc(done, 1)
                if kind == "max":
                    dve.wait_ge(done, reached(i, 5))
                    then(V.tensor_tensor(prod[:], rows[:, 0:D], krow[:, 0:D], ALU.mult))
                    then(V.tensor_reduce(s8[:], heads(prod[:]), AX.X, ALU.add))
                    V.tensor_copy(scores[:, bass.ds(i * H, H)], s8[:])
                    V.tensor_scalar(tmp[:], same[:], -1.0, NEG, ALU.add, ALU.mult).then_inc(done, 1)
                    dve.wait_ge(done, reached(i, 7))
                    V.tensor_copy(s8T[:], p_a[0:H, 0:P]).then_inc(done, 1)
                    dve.wait_ge(done, reached(i, 9))
                    for j, bank in enumerate((p_a, p_b)):
                        for h in range(H // 2):
                            ins = V.tensor_tensor(big[:, j * (H // 2) + h, :], tmp[:], bank[:, h * P:(h + 1) * P], ALU.add)
                    then(ins)
                    then(V.tensor_reduce(new[:], big[:], AX.X, ALU.max))
                    V.tensor_tensor(new[:], new[:], old[:], ALU.max).then_inc(done, 1)
                elif kind == "weigh":
                    dve.wait_ge(done, reached(i, 5))
                    then(V.tensor_copy(s8[:], scores[:, bass.ds(i * H, H)]))
                    V.tensor_tensor(s8[:], s8[:], topr[:], ALU.subtract).then_inc(done, 1)
                    dve.wait_ge(done, reached(i, 7))
                    V.tensor_copy(val[:, D:D + H], s8[:])
                    V.tensor_tensor(heads(val[:, 0:D]), heads(rows[:, D:2 * D]), s8[:].to_broadcast([P, H, hd]),
                                    ALU.mult).then_inc(done, 1)
                    dve.wait_ge(done, reached(i, 9))
                    V.tensor_tensor(new[:], old[:], p_a[:, 0:width], ALU.add).then_inc(done, 1)
                else:
                    dve.wait_ge(done, reached(i, 6))
                    V.tensor_tensor(new[:], old[:], p_a[:, 0:width], ALU.add).then_inc(done, 1)
                return n[0]
            with dve.Fori(0, EC) as i:
                used = body(i)
            assert used == per, (kind, used)


def general_sums(nc, pl, con, signals, layer, h_in, acc):
    edge_pass(nc, pl, con, signals, f"esum{layer}", "sum", acc, acc.shape[1], h_in)
    clear_signals(nc, list(signals.values()))


def general_attend(nc, pl, con, signals, x, w_out, b_out, qv_dram, ks_dram, mask_embed, top, acc, x1_dram, h_dram):
    D, C, H, hd = pl.D, pl.C, pl.H, pl.hd
    W = acc.shape[1]
    with ExitStack() as ctx:
        scores = ctx.enter_context(nc.sbuf_tensor("edge_scores", [P, pl.EC * H], F32))
        edge_pass(nc, pl, con, signals, "emax", "max", top, H, qv_dram, ks_dram=ks_dram, scores=scores)
        clear_signals(nc, list(signals.values()))
        edge_pass(nc, pl, con, signals, "ewgh", "weigh", acc, W, qv_dram, top_dram=top, scores=scores)
        clear_signals(nc, list(signals.values()))
    with ExitStack() as ctx:
        def sb(n, s, d=F32):
            return ctx.enter_context(nc.sbuf_tensor("gen_" + n, s, d))

        def sem(n):
            if n not in signals:
                signals[n] = nc.alloc_semaphore("general_" + n)
            return signals[n]
        wraw, wT, bias = sb("wraw", [P, C, D]), sb("wT", [P, C, D]), sb("bias", [P, D])
        at, xt, r, o, oT = sb("at", [P, W]), sb("xt", [P, D]), sb("r", [P, H]), sb("o", [P, D]), sb("oT", [P, D])
        x1, h, zero = sb("x1", [P, D]), sb("h", [P, D]), sb("zero", [P, D])
        st, mv, sd, rstd, nmr = sb("st", [P, 6]), sb("mv", [P, 2]), sb("sd", [P, 1]), sb("rstd", [P, 1]), sb("nmr", [P, 1])
        ps_t = ctx.enter_context(nc.psum_tensor("gen_ps_t", [P, 512], F32))
        ps_p = ctx.enter_context(nc.psum_tensor("gen_ps_p", [P, 512], F32))
        setup_in, clear, w_up, w_ready = sem("setup_in"), sem("clear"), sem("w_up"), sem("w_ready")
        done, dve_step, loaded, stored, passed = sem("done"), sem("dve_step"), sem("loaded"), sem("stored"), sem("passed")
        STEPS, PER = 10, 6
        whole, rest = pl.N // P, pl.N % P

        def reached(i, step):
            return i * STEPS + step + 1
        block = ctx.enter_context(nc.Block())

        @where(block.sync, con, False)
        def _(sp):
            for c in range(C):
                sp.dma_start(wraw[:, c, :], w_out[c * P:(c + 1) * P, :]).then_inc(setup_in, 16)
            sp.dma_start(bias[:], b_out.rearrange("(o d) -> o d", o=1).to_broadcast([P, D])).then_inc(setup_in, 16)
            sp.wait_ge(clear, 1)

            def tile(i, rows):
                sp.wait_ge(done, reached(i, 0))
                sp.dma_start(at[:], acc[bass.ds(i * P, P), :]).then_inc(loaded, 16)
                sp.dma_start(xt[0:rows, :], x[bass.ds(i * P, rows), :]).then_inc(loaded, 16)
                sp.wait_ge(loaded, i * 32 + 32)
                sp.sem_inc(done, 1)
                sp.wait_ge(done, reached(i, 9))
                sp.dma_start(x1_dram[bass.ds(i * P, P), :], x1[:]).then_inc(stored, 16)
                sp.dma_start(h_dram[bass.ds(i * P, P), :], h[:]).then_inc(stored, 16)
                sp.wait_ge(stored, i * 32 + 32)
                sp.sem_inc(done, 1)
            with sp.Fori(0, whole) as i:
                tile(i, P)
            if rest:
                tile(whole, rest)
            tiles = whole + (rest > 0)
            for t in range(tiles, pl.NT):
                sp.dma_start(x1_dram[t * P:(t + 1) * P, :], zero[:]).then_inc(stored, 16)
                sp.dma_start(h_dram[t * P:(t + 1) * P, :], zero[:]).then_inc(stored, 16)
            sp.wait_ge(stored, 32 * pl.NT)
            sp.dma_start(h_dram[0:1, :], mask_embed.rearrange("(o d) -> o d", o=1)).then_inc(stored, 16)
            sp.wait_ge(stored, 32 * pl.NT + 16)

        @where(block.tensor, con, False)
        def _(pe):
            pe.wait_ge(setup_in, 16 * (C + 1))
            for n in range(C * C):
                c, rr = n // C, n % C
                if n:
                    pe.wait_ge(w_ready, n)
                nc.tensor.transpose(ps_t[:, 0:P], wraw[:, c, rr * P:(rr + 1) * P], con["ident"][:]).then_inc(w_up, 1)
            pe.wait_ge(w_ready, C * C)

            def tile(i):
                pe.wait_ge(done, reached(i, 2))
                for c in range(C):
                    ins = nc.tensor.transpose(ps_t[:, c * P:(c + 1) * P], o[:, c * P:(c + 1) * P], con["ident"][:])
                ins.then_inc(done, 1)
                pe.wait_ge(done, reached(i, 4))
                for c in range(C):
                    ins = nc.tensor.matmul(ps_p[:, 0:D], oT[:, c * P:(c + 1) * P], wT[:, c, :],
                                           start=(c == 0), stop=(c == C - 1))
                ins.then_inc(done, 1)
            with pe.Fori(0, whole) as i:
                tile(i)
            if rest:
                tile(whole)

        @where(block.scalar, con, False)
        def _(act):
            for n in range(C * C):
                c, rr = n // C, n % C
                act.wait_ge(w_up, n + 1)
                nc.scalar.copy(wT[:, rr, c * P:(c + 1) * P], ps_t[:, 0:P]).then_inc(w_ready, 1)

            def tile(i):
                act.wait_ge(done, reached(i, 6))
                nc.scalar.activation(sd[:], mv[:, 1:2], ACT.Sqrt, bias=con["eps"][:, 0:1]).then_inc(done, 1)
                act.wait_ge(done, reached(i, 8))
                nc.scalar.activation(h[:], x1[:], ACT.Relu, bias=nmr[:, 0:1], scale=rstd[:, 0:1]).then_inc(done, 1)
            with act.Fori(0, whole) as i:
                tile(i)
            if rest:
                tile(whole)

        @where(block.vector, con, False)
        def _(dve):
            V = nc.vector
            V.memset(zero[:], 0.0)
            V.memset(con["deg"][:], 1.0)
            V.memset(xt[:], 0.0).then_inc(clear, 1)
            dve.wait_ge(setup_in, 16 * (C + 1))
            dve.sem_inc(done, 1)

            def tile(i):
                n = [0]

                def then(ins):
                    n[0] += 1
                    ins.then_inc(dve_step, 1)
                    dve.wait_ge(dve_step, i * PER + n[0])
                dve.wait_ge(done, reached(i, 1))
                then(V.tensor_scalar(r[:], at[:, D:D + H], 0.0, None, ALU.is_equal))
                then(V.tensor_tensor(r[:], r[:], at[:, D:D + H], ALU.add))
                then(V.reciprocal(r[:], r[:]))
                V.tensor_scalar(con["deg"][:, bass.ds(i, 1)], at[:, D + H:D + H + 1], 1.0, None, ALU.max)
                V.tensor_tensor(o[:].rearrange("p (h d) -> p h d", h=H), at[:, 0:D].rearrange("p (h d) -> p h d", h=H),
                                r[:].to_broadcast([P, H, hd]), ALU.mult).then_inc(done, 1)
                dve.wait_ge(done, reached(i, 3))
                V.tensor_copy(oT[:], ps_t[:, 0:D]).then_inc(done, 1)
                dve.wait_ge(done, reached(i, 5))
                then(V.tensor_tensor(x1[:], xt[:], bias[:], ALU.add))
                then(V.tensor_tensor(x1[:], x1[:], ps_p[:, 0:D], ALU.add))
                V.bn_stats(st[:], x1[:]).then_inc(passed, 1)
                dve.wait_ge(passed, i * 2 + 1)
                dve.sem_inc(passed, 1)
                V.bn_aggr(mv[:], st[:]).then_inc(done, 1)
                dve.wait_ge(done, reached(i, 7))
                then(V.reciprocal(rstd[:], sd[:]))
                V.scalar_tensor_tensor(out=nmr[:], in0=mv[:, 0:1], scalar=-1.0, in1=rstd[:],
                                       op0=ALU.mult, op1=ALU.mult).then_inc(done, 1)
                assert n[0] == PER, n
            with dve.Fori(0, whole) as i:
                tile(i)
            if rest:
                tile(whole)
            tiles = whole + (rest > 0)
            dve.wait_ge(done, reached(tiles - 1, STEPS))
            V.reciprocal(con["inv_deg"][:], con["deg"][:])

    clear_signals(nc, list(signals.values()))


def aggregate(nc, pl, con, signals, layer, wl, wr, b, gamma, beta, rmean, rvar, h_in, h_next, x1_dram, sum_dram, out):
    D, C, NT = pl.D, pl.C, pl.NT
    final = out is not None
    with ExitStack() as ctx:
        def name(n):
            return f"{n}_l{layer}"

        def sb(n, s, d=F32):
            return ctx.enter_context(nc.sbuf_tensor(name(n), s, d))

        def ps(n):
            return ctx.enter_context(nc.psum_tensor(name(n), [P, 512], F32))

        def sem(n):
            if n.startswith("rows_in"):
                return nc.alloc_semaphore(f"agg_{name(n)}")
            if n not in signals:
                signals[n] = nc.alloc_semaphore("agg_" + n)
            return signals[n]
        wls, wrs = sb("wl", [P, C, D]), sb("wr", [P, C, D])
        par = sb("par", [P, 5, D])
        g, bias = sb("g", [P, D]), sb("bias", [P, D])
        hs = [sb(f"hs{u}", [P, QT, D]) for u in range(2)]
        xs = [sb(f"xs{u}", [P, QT, D]) for u in range(2)]
        rows = [sb(f"rows{u}", [P, QT, D]) for u in range(2)]
        hot = [sb(f"hot{u}", [P, QT, P]) for u in range(2)]
        res = [sb(f"res{u}", [P, QT, D]) for u in range(2)]
        lidx, ldst, ideg = sb("lidx", [P, 2, QT], I32), sb("ldst", [P, 2, QT]), sb("ideg", [P, 2, QT])
        hT, aT, z = sb("hT", [P, 2, D]), sb("aT", [P, 2, D]), sb("z", [P, 2, D])
        ps_h, ps_a, ps_z = [[ps(f"{n}{v}") for v in range(2)] for n in ("ps_h", "ps_a", "ps_z")]
        par_in, std_ready, fold, weights_ready = sem("par_in"), sem("std_ready"), sem("fold"), sem("weights_ready")
        bufs_clear, staged, hot_ready = sem("bufs_clear"), sem("staged"), sem("hot_ready")
        passed = sem("passed")
        hs_in, xs_in, rows_in, res_out = ([sem(f"{n}{u}") for u in range(2)] for n in ("hs_in", "xs_in", "rows_in", "res_out"))
        h_up, a_up, hT_ready, aT_ready, z_up, z_read, z_step, tile_done, ideg_ready, tail_io = (
            sem("h_up"), sem("a_up"), sem("hT_ready"), sem("aT_ready"), sem("z_up"), sem("z_read"), sem("z_step"),
            sem("tile_done"), sem("ideg_ready"), sem("tail_io"))
        block = ctx.enter_context(nc.Block())
        last = pl.turns - 1

        @block.sync
        def _(sp):
            for c in range(C):
                sp.dma_start(wls[:, c, :], wl[c * P:(c + 1) * P, :]).then_inc(par_in, 16)
                sp.dma_start(wrs[:, c, :], wr[c * P:(c + 1) * P, :]).then_inc(par_in, 16)
            for j, v in enumerate((b, gamma, beta, rmean, rvar)):
                sp.dma_start(par[:, j, :], v.to_broadcast([P, D])).then_inc(par_in, 16)
            for u in range(2):
                sp.sem_inc(res_out[u], 16)

            def load(i, u):
                sp.wait_ge(tile_done, (2 * i + u) * QT + QT)
                at = i * (BODY * P) + u * pl.QR
                sp.dma_start(hs[u][:], quad_rows(h_in, at)).then_inc(hs_in[u], 16)
                if final:
                    sp.dma_start(xs[u][:], quad_rows(x1_dram, at)).then_inc(xs_in[u], 16)

            def store(i, u):
                sp.wait_ge(tile_done, (2 * i + u) * QT + 3 * QT)
                sp.dma_start(quad_rows(out if final else h_next, i * (BODY * P) + u * pl.QR),
                             res[u][:]).then_inc(res_out[u], 16)
            load(0, 0)
            load(0, 1)
            with sp.Fori(0, last) as i:
                for u in range(2):
                    load(i + 1, u)
                    store(i, u)
            store(last, 0)
            if final:
                sp.wait_ge(tile_done, (2 * last + 1) * QT + 3 * QT)
                parts = ragged(out, last * BODY * P + pl.QR, pl.last_rows, res[1])
                for dram, tile in parts:
                    sp.dma_start(dram, tile).then_inc(tail_io, 16)
                sp.wait_ge(tail_io, 16 * len(parts))
            else:
                store(last, 1)
            sp.wait_ge(res_out[0], 16 * (pl.turns + 1))
            sp.wait_ge(res_out[1], 16 * (pl.turns + (0 if final else 1)))

        @block.gpsimd
        def _(pool):
            for u in range(2):
                ins = nc.gpsimd.memset(rows[u][:], 0.0)
            ins.then_inc(bufs_clear, 1)
            pool.wait_ge(bufs_clear, 1)
            bound = pool.to_reg(pl.NP - 1)

            def fetch(i, u):
                q = 2 * i + u
                pool.wait_ge(a_up, q * QT + QT)
                nc.gpsimd.tensor_copy(lidx[:, u, :], con["links"][:, bass.ds(i * BODY + u * QT, QT), 0])
                nc.gpsimd.tensor_copy(ldst[:, u, :], con["dloc"][:, bass.ds(i * BODY + u * QT, QT)]).then_inc(staged, 1)
                pool.wait_ge(staged, q + 1)
                pool.sem_inc(passed, 1)
                for t in range(QT):
                    nc.gpsimd.indirect_dma_start(
                        out=rows[u][:, t, :], out_offset=None, in_=h_in[:, :],
                        in_offset=bass.IndirectOffsetOnAxis(ap=lidx[:, u, t:t + 1], axis=0),
                        bounds_check=bound, oob_is_err=False).then_inc(rows_in[u], 16)
                for t in range(QT):
                    ins = nc.gpsimd.tensor_scalar(hot[u][:, t, :], con["iota"][:], ldst[:, u, t:t + 1], None, ALU.is_equal)
                ins.then_inc(hot_ready, 1)

            def fetch_sums(i, u):
                q = 2 * i + u
                pool.wait_ge(a_up, q * QT + QT)
                pool.sem_inc(passed, 1)
                for t in range(QT):
                    ins = nc.gpsimd.tensor_copy(hot[u][:, t, :], con["ident"][:])
                ins.then_inc(hot_ready, 1)
                nc.gpsimd.dma_start(rows[u][:], quad_rows(sum_dram, i * (BODY * P) + u * pl.QR)
                                    ).then_inc(rows_in[u], 16 * QT)
            flag = pool.value_load(con["flag"][0:1, 0:1], min_val=0, max_val=1)
            with pool.If(flag > 0):
                with pool.Fori(0, pl.turns) as i:
                    fetch(i, 0)
                    fetch(i, 1)
            with pool.Else():
                with pool.Fori(0, pl.turns) as i:
                    fetch_sums(i, 0)
                    fetch_sums(i, 1)

        @block.tensor
        def _(pe):
            pe.wait_ge(weights_ready, 1)
            pe.sem_inc(a_up, 2 * QT)

            def up(i, k):
                u, t, bb, n, q = k // QT, k % QT, k % 2, i * BODY + k, 2 * i + k // QT
                if t == 0:
                    pe.wait_ge(hs_in[u], i * 16 + 16)
                    pe.wait_ge(rows_in[u], i * (16 * QT) + 16 * QT)
                    pe.wait_ge(hot_ready, q + 1)
                pe.wait_ge(hT_ready, n + 1)
                for c in range(C):
                    ins = nc.tensor.transpose(ps_h[bb][:, c * P:(c + 1) * P], hs[u][:, t, c * P:(c + 1) * P], con["ident"][:])
                ins.then_inc(h_up, 1)
                pe.wait_ge(aT_ready, n + 1)
                for c in range(C):
                    ins = nc.tensor.matmul(ps_a[bb][:, c * P:(c + 1) * P], rows[u][:, t, c * P:(c + 1) * P],
                                           hot[u][:, t, :], start=True, stop=True)
                ins.then_inc(a_up, 1)

            def dense(i, k):
                n, bb = i * BODY + k, k % 2
                pe.wait_ge(hT_ready, n + 3)
                pe.wait_ge(z_read, n + 1)
                for c in range(C):
                    nc.tensor.matmul(ps_z[bb][:, D:2 * D], hT[:, bb, c * P:(c + 1) * P], wrs[:, c, :],
                                     start=(c == 0), stop=(c == C - 1))
                pe.wait_ge(aT_ready, n + 3)
                for c in range(C):
                    ins = nc.tensor.matmul(ps_z[bb][:, 0:D], aT[:, bb, c * P:(c + 1) * P], wls[:, c, :],
                                           start=(c == 0), stop=(c == C - 1))
                ins.then_inc(z_up, 1)
            up(0, 0)

            def turn(i, end):
                for k in range(BODY):
                    if k < BODY - 1:
                        up(i, k + 1)
                    elif not end:
                        up(i + 1, 0)
                    dense(i, k)
            with pe.Fori(0, last) as i:
                turn(i, False)
            turn(last, True)

        @block.scalar
        def _(act):
            act.wait_ge(par_in, 16 * (2 * C + 5))
            nc.scalar.activation(g[:], par[:, 4, :], ACT.Sqrt, bias=con["eps"][:, 0:1]).then_inc(std_ready, 1)
            act.sem_inc(hT_ready, 2)

            def keep(n, bb):
                act.wait_ge(h_up, n + 1)
                act.wait_ge(z_up, n + 1)
                nc.scalar.copy(hT[:, bb, :], ps_h[bb][:, 0:D]).then_inc(hT_ready, 1)
            with act.Fori(0, pl.turns) as i:
                for k in range(BODY):
                    keep(i * BODY + k, k % 2)

        @block.vector
        def _(dve):
            V = nc.vector
            dve.wait_ge(par_in, 16 * (2 * C + 5))
            dve.wait_ge(std_ready, 1)
            V.tensor_tensor(bias[:], par[:, 0, :], par[:, 3, :], ALU.subtract)
            V.reciprocal(g[:], g[:]).then_inc(fold, 1)
            dve.wait_ge(fold, 1)
            V.tensor_tensor(g[:], g[:], par[:, 1, :], ALU.mult).then_inc(fold, 1)
            dve.wait_ge(fold, 2)
            V.tensor_tensor(bias[:], bias[:], g[:], ALU.mult).then_inc(fold, 1)
            for w in (wls, wrs):
                for c in range(C):
                    V.tensor_tensor(w[:, c, :], w[:, c, :], g[:], ALU.mult)
            dve.wait_ge(fold, 3)
            V.tensor_tensor(bias[:], bias[:], par[:, 2, :], ALU.add).then_inc(weights_ready, 1)
            dve.wait_ge(weights_ready, 1)
            dve.sem_inc(aT_ready, 2)
            dve.sem_inc(z_up, 2)
            dve.sem_inc(z_read, 2)
            dve.sem_inc(tile_done, 2 * QT)

            def add_own(i, k, regular):
                n, bb = i * BODY + k, k % 2
                dve.wait_ge(a_up, n + 9)
                dve.wait_ge(hT_ready, n + 3)
                dve.wait_ge(z_up, n + 1)
                if regular:
                    V.tensor_tensor(aT[:, bb, :], hT[:, bb, :], ps_a[bb][:, 0:D], ALU.add).then_inc(aT_ready, 1)
                else:
                    V.tensor_copy(aT[:, bb, :], ps_a[bb][:, 0:D]).then_inc(aT_ready, 1)

            def close(i, k):
                u, t, bb, n, q = k // QT, k % QT, k % 2, i * BODY + k, 2 * i + k // QT
                if t == 0:
                    V.tensor_copy(ideg[:, u, :], con["inv_deg"][:, bass.ds(i * BODY + u * QT, QT)]).then_inc(ideg_ready, 1)
                    dve.wait_ge(ideg_ready, q + 1)
                    dve.wait_ge(res_out[u], i * 16 + 16)
                    if final:
                        dve.wait_ge(xs_in[u], i * 16 + 16)
                dve.wait_ge(z_up, n + 3)
                V.scalar_tensor_tensor(out=z[:, bb, :], in0=ps_z[bb][:, 0:D], scalar=ideg[:, u, t:t + 1], in1=bias[:],
                                       op0=ALU.mult, op1=ALU.add).then_inc(z_step, 1)
                dve.wait_ge(z_step, 2 * n + 1)
                V.tensor_tensor(z[:, bb, :], z[:, bb, :], ps_z[bb][:, D:2 * D], ALU.add).then_inc(z_read, 1)
                dve.wait_ge(z_read, n + 3)
                if final:
                    V.tensor_tensor(z[:, bb, :], z[:, bb, :], hs[u][:, t, :], ALU.add).then_inc(z_step, 1)
                    dve.wait_ge(z_step, 2 * n + 2)
                    V.tensor_tensor(res[u][:, t, :], z[:, bb, :], xs[u][:, t, :], ALU.add).then_inc(tile_done, 1)
                else:
                    V.scalar_tensor_tensor(out=res[u][:, t, :], in0=z[:, bb, :], scalar=0.0, in1=hs[u][:, t, :],
                                           op0=ALU.max, op1=ALU.add).then_inc(tile_done, 1)
                    dve.sem_inc(z_step, 1)

            def turn(i, end, regular):
                for k in range(BODY):
                    if k < BODY - 1:
                        add_own(i, k + 1, regular)
                    elif not end:
                        add_own(i + 1, 0, regular)
                    close(i, k)

            def run(regular):
                add_own(0, 0, regular)
                with dve.Fori(0, last) as i:
                    turn(i, False, regular)
                turn(last, True, regular)
            flag = dve.value_load(con["flag"][0:1, 0:1], min_val=0, max_val=1)
            with dve.If(flag > 0):
                run(True)
            with dve.Else():
                run(False)


def program(nc, x, src, dst, Wq, bq, Wk, bk, Wv, bv, Wo, bo, mask_embed, Wl, Wr, b, gamma, beta, rmean, rvar, out):
    N, D = x.shape
    pl = Plan(N, src.shape[0], D, 8)
    KW = D + pl.H
    qv = nc.dram_tensor("qv_rows", (pl.NP, 2 * D), F32, kind="Internal").ap()
    ks = nc.dram_tensor("k_rows", (pl.NP, KW), F32, kind="Internal").ap()
    links = nc.dram_tensor("link_table", (P * pl.NT, 2), I32, kind="Internal").ap()
    x1 = nc.dram_tensor("x1_rows", (pl.NP, D), F32, kind="Internal").ap()
    hbuf = [nc.dram_tensor(f"h_rows{j}", (pl.NP, D), F32, kind="Internal").ap() for j in range(2)]
    top = nc.dram_tensor("top_rows", (pl.NP, pl.H), F32, kind="Internal").ap()
    acc = nc.dram_tensor("sum_rows", (pl.NP, D + pl.H + 8), F32, kind="Internal").ap()
    with ExitStack() as ctx:
        con = constants(nc, ctx, pl)
        with ExitStack() as edges:
            idx = edges.enter_context(nc.sbuf_tensor("edge_rows", [P, pl.EB], I32))
            pay = edges.enter_context(nc.sbuf_tensor("edge_pay", [P, pl.EB, 2], I32))
            edge_tables(nc, pl, con, src, dst, links, idx, pay)
            project(nc, pl, con, x, (Wq, Wk, Wv), (bq, bk, bv), qv, ks, links, idx, pay)
        attend(nc, pl, con, x, Wo, bo, qv, ks, links, mask_embed, x1, hbuf[0])
        general = {}
        general_attend(nc, pl, con, general, x, Wo, bo, qv, ks, mask_embed, top, acc, x1, hbuf[0])
        L = Wl.shape[0]
        signals = {}
        for l in range(L):
            vec = [v[l:l + 1, :] for v in (b, gamma, beta, rmean, rvar)]
            if l:
                clear_signals(nc, list(signals.values()))
            general_sums(nc, pl, con, general, l, hbuf[l % 2], acc)
            aggregate(nc, pl, con, signals, l, Wl[l], Wr[l], *vec, hbuf[l % 2], hbuf[(l + 1) % 2], x1, acc[:, 0:D],
                      out if l == L - 1 else None)


INPUTS = ['x', 'src', 'dst', 'L0_gnn_Wq', 'L0_gnn_bq', 'L0_gnn_Wk', 'L0_gnn_bk', 'L0_gnn_Wv', 'L0_gnn_bv',
          'L0_gnn_Wo', 'L0_gnn_bo', 'L1_gnn_mask_embed', 'L1_gnn_Wl', 'L1_gnn_Wr', 'L1_gnn_b', 'L1_gnn_gamma',
          'L1_gnn_beta', 'L1_gnn_rmean', 'L1_gnn_rvar']


def kernel(**inputs):
    import concourse.bacc as bacc
    import numpy as np
    from concourse.bass_utils import run_bass_kernel_spmd

    nc = bacc.Bacc("TRN2", target_bir_lowering=False, num_devices=1)
    arrays, args = {}, []
    for name in INPUTS:
        a = np.ascontiguousarray(inputs[name])
        arrays[f"in_{name}"] = a
        args.append(nc.dram_tensor(f"in_{name}", a.shape, mybir.dt.from_np(a.dtype), kind="ExternalInput").ap())
    out = nc.dram_tensor("out_x", inputs["x"].shape, F32, kind="ExternalOutput").ap()
    program(nc, *args, out)
    r = run_bass_kernel_spmd(nc, [arrays], core_ids=[0])
    return r.results[0]["out_x"]
```

```python
from contextlib import ExitStack

import concourse.bass as bass
from concourse import mybir

F32 = mybir.dt.float32
F32R = mybir.dt.float32r
I32 = mybir.dt.int32
ALU = mybir.AluOpType
ACT = mybir.ActivationFunctionType
AX = mybir.AxisListType

P = 128
QT = 4
BODY = 2 * QT
SKIP = 1 << 20
NEG = 1.0e30
EPS = 1e-5


class Plan:

    def __init__(self, n, e, d, heads):
        self.N, self.E, self.D, self.H = n, e, d, heads
        self.hd = d // heads
        self.C = d // P
        self.turns = -(-n // (P * BODY))
        self.NT = self.turns * BODY
        self.NP = self.NT * P
        self.QR = QT * P
        self.last_rows = n - (self.turns - 1) * BODY * P - self.QR
        assert 0 < self.last_rows <= self.QR
        self.EC = -(-e // P)
        self.EB = -(-self.EC // 16) * 16
        self.e_tail = e - (P - 1) * self.EC
        assert 0 < self.e_tail <= self.EC


def quad_rows(t, base, cols=None):
    v = t[bass.ds(base, QT * P), :] if cols is None else t[bass.ds(base, QT * P), cols[0]:cols[1]]
    return v.rearrange("(t p) d -> p t d", p=P)


def ragged(table, base, rows, tile):
    full, rest = rows // P, rows % P
    out = []
    if rest:
        out.append((table[base + full * P:base + rows, :], tile[0:rest, full, :]))
    if full:
        out.append((table[base:base + full * P, :].rearrange("(t p) d -> p t d", p=P), tile[:, 0:full, :]))
    return out


def constants(nc, ctx, pl):
    c = {}
    for name, shape, dt in (("ident", [P, P], F32), ("ones", [P, P], F32), ("iota", [P, QT, P], F32),
                            ("eps", [P, 1], F32), ("links", [P, pl.NT, 2], I32), ("dloc", [P, pl.NT], F32),
                            ("flag", [1, 1], I32), ("edge_src", [P, pl.EC], I32), ("edge_dst", [P, pl.EC], I32),
                            ("deg", [P, pl.NT], F32), ("inv_deg", [P, pl.NT], F32)):
        c[name] = ctx.enter_context(nc.sbuf_tensor(name, shape, dt))
    return c


def where(attach, con, regular):
    def wrap(body):
        @attach
        def _(eng):
            flag = eng.value_load(con["flag"][0:1, 0:1], min_val=0, max_val=1)
            with eng.If(flag > 0 if regular else flag < 1):
                body(eng)
    return wrap


def edge_tables(nc, pl, con, src, dst, link_dram, idx_out, pay_out):
    EC, NT = pl.EC, pl.NT
    with ExitStack() as ctx:
        def sb(n, s, d=F32):
            return ctx.enter_context(nc.sbuf_tensor(n, s, d))

        def sem(n):
            return ctx.enter_context(nc.semaphore(n))
        dst_i, src_i = sb("dst_i", [P, EC + 2], I32), sb("src_i", [P, EC], I32)
        tb_i, e_i = sb("tb_i", [P, EC + 2], I32), sb("e_i", [P, EC], I32)
        iota_i = sb("iota_i", [P, P], I32)
        d, s, tb, e = sb("d_f", [P, EC + 2]), sb("s_f", [P, EC]), sb("tb_f", [P, EC + 2]), sb("e_f", [P, EC])
        first, start, slot = sb("first", [P, EC]), sb("start", [P, EC]), sb("slot", [P, EC])
        loop, link, tmp = sb("loop", [P, EC]), sb("link", [P, EC]), sb("tmp", [P, EC])
        row_in, row, carry = sb("row_in", [1, P]), sb("row", [1, P + 1]), sb("carry", [P, 1])
        sums, total, bad = sb("sums", [P, 3]), sb("total", [1, 3]), sb("bad", [1, 1])
        empty = sb("empty", [P, NT, 2], I32)
        ps_row = ctx.enter_context(nc.psum_tensor("ps_row", [P, 512], F32))
        ps_col = ctx.enter_context(nc.psum_tensor("ps_col", [P, 512], F32))
        padded, edges_in, pool_ready, step = sem("padded"), sem("edges_in"), sem("pool_ready"), sem("step")
        row_up, row_back, row_ready, empty_out, ident_clear = (
            sem("row_up"), sem("row_back"), sem("row_ready"), sem("empty_out"), sem("ident_clear"))
        start_ready, sums_ready, sums_up = sem("start_ready"), sem("sums_ready"), sem("sums_up")
        block = ctx.enter_context(nc.Block())

        @block.sync
        def _(sp):
            sp.wait_ge(padded, 1)
            flat = lambda a, n: a.rearrange("(p c) -> p c", c=n)
            sp.dma_start(dst_i[0:1, 1:EC + 2], flat(dst[0:EC + 1], EC + 1)).then_inc(edges_in, 16)
            mid = dst[EC - 1:EC - 1 + (P - 2) * EC]
            sp.dma_start(dst_i[1:P - 1, 0:EC], flat(mid, EC)).then_inc(edges_in, 16)
            with nc.allow_non_contiguous_dma("the two neighbours past a partition's edges"):
                tail = dst[2 * EC - 1:2 * EC - 1 + (P - 3) * EC].rearrange("(p c) -> p c", c=EC)
                sp.dma_start(dst_i[1:P - 2, EC:EC + 2], tail[:, 0:2]).then_inc(edges_in, 16)
                at = (P - 1) * EC - 1
                sp.dma_start(dst_i[P - 2:P - 1, EC:EC + 2], flat(dst[at:at + 2], 2)).then_inc(edges_in, 16)
            sp.dma_start(dst_i[P - 1:P, 0:pl.e_tail + 1],
                         flat(dst[(P - 1) * EC - 1:pl.E], pl.e_tail + 1)).then_inc(edges_in, 16)
            sp.dma_start(src_i[0:P - 1, :], flat(src[0:(P - 1) * EC], EC)).then_inc(edges_in, 16)
            sp.dma_start(src_i[P - 1:P, 0:pl.e_tail],
                         flat(src[(P - 1) * EC:pl.E], pl.e_tail)).then_inc(edges_in, 16)
            sp.wait_ge(padded, 2)
            sp.dma_start(link_dram.rearrange("(p t) w -> p (t w)", p=P),
                         empty[:].rearrange("p t w -> p (t w)")).then_inc(empty_out, 16)
            sp.wait_ge(empty_out, 16)

        @block.gpsimd
        def _(pool):
            nc.gpsimd.iota(iota_i[:], pattern=[[1, P]], base=0, channel_multiplier=0)
            nc.gpsimd.iota(e_i[:], pattern=[[1, EC]], base=0, channel_multiplier=EC).then_inc(pool_ready, 1)
            nc.gpsimd.memset(con["ones"][:], 1.0)
            nc.gpsimd.memset(con["eps"][:], EPS)
            nc.gpsimd.memset(con["ident"][:], 0.0).then_inc(ident_clear, 1)
            pool.wait_ge(ident_clear, 1)
            nc.gpsimd.affine_select(out=con["ident"][:], in_=con["ident"][:], compare_op=ALU.not_equal, fill=1.0,
                                    base=0, pattern=[[-1, P]], channel_multiplier=1).then_inc(pool_ready, 1)

        @block.tensor
        def _(pe):
            pe.wait_ge(pool_ready, 2)
            pe.wait_ge(start_ready, 1)
            nc.tensor.transpose(ps_row[0:1, 0:P], start[:, EC - 1:EC], con["ident"][:]).then_inc(row_up, 1)
            pe.wait_ge(row_ready, 1)
            nc.tensor.matmul(ps_col[:, 0:1], row[0:1, 0:P], con["ones"][0:1, 0:1],
                             start=True, stop=True).then_inc(row_back, 1)
            pe.wait_ge(sums_ready, 1)
            nc.tensor.matmul(ps_row[0:1, 0:3], con["ones"][:, 0:1], sums[:], start=True, stop=True).then_inc(sums_up, 1)

        @block.vector
        def _(dve):
            n = [0]

            def then(ins):
                n[0] += 1
                ins.then_inc(step, 1)
                dve.wait_ge(step, n[0])
            V = nc.vector
            V.memset(dst_i[:], pl.NP)
            then(V.memset(src_i[:], 0))
            V.memset(dst_i[0:1, 0:1], -1).then_inc(padded, 1)
            V.memset(empty[:, :, 0], SKIP)
            V.memset(empty[:, :, 1], -1).then_inc(padded, 1)
            V.memset(idx_out[:], SKIP)
            V.memset(pay_out[:], 0)
            V.memset(row[:], 0.0)
            dve.wait_ge(pool_ready, 1)
            for t in range(QT):
                V.tensor_copy(con["iota"][:, t, :], iota_i[:])
            V.tensor_copy(e[:], e_i[:])
            dve.wait_ge(edges_in, 7 * 16)
            V.tensor_copy(d[:], dst_i[:])
            V.tensor_copy(s[:], src_i[:])
            then(V.tensor_scalar(tb_i[:], dst_i[:], 7, 7, ALU.arith_shift_right, ALU.logical_shift_left))
            then(V.tensor_copy(tb[:], tb_i[:]))
            own, prev, nxt = slice(1, EC + 1), slice(0, EC), slice(2, EC + 2)
            then(V.tensor_tensor(first[:], tb[:, own], tb[:, prev], ALU.not_equal))
            then(V.tensor_tensor(first[:], first[:], e[:], ALU.mult))
            V.tensor_tensor_scan(start[:], first[:], first[:], 0.0, ALU.max, ALU.max).then_inc(start_ready, 1)
            dve.wait_ge(row_up, 1)
            then(V.tensor_copy(row_in[:], ps_row[0:1, 0:P]))
            V.tensor_tensor_scan(row[0:1, 1:P + 1], row_in[:], row_in[:], 0.0,
                                 ALU.max, ALU.max).then_inc(row_ready, 1)
            dve.wait_ge(row_back, 1)
            then(V.tensor_copy(carry[:], ps_col[:, 0:1]))
            then(V.tensor_scalar(start[:], start[:], carry[:, 0:1], None, ALU.max))
            then(V.tensor_tensor(slot[:], e[:], d[:, own], ALU.subtract))
            then(V.tensor_tensor(slot[:], slot[:], start[:], ALU.subtract))
            then(V.tensor_tensor(slot[:], slot[:], tb[:, own], ALU.add))
            then(V.tensor_tensor(loop[:], d[:, own], d[:, nxt], ALU.not_equal))
            then(V.tensor_tensor(tmp[:], d[:, own], s[:], ALU.is_equal))
            then(V.tensor_tensor(loop[:], loop[:], tmp[:], ALU.mult))
            then(V.tensor_scalar(link[:], e[:], float(pl.E), None, ALU.is_lt))
            then(V.tensor_tensor(link[:], link[:], loop[:], ALU.subtract))
            then(V.tensor_scalar(tmp[:], tb[:, own], 1.0 / P, float(SKIP), ALU.mult, ALU.add))
            then(V.scalar_tensor_tensor(out=tmp[:], in0=slot[:], scalar=float(NT), in1=tmp[:],
                                        op0=ALU.mult, op1=ALU.add))
            then(V.scalar_tensor_tensor(out=idx_out[:, 0:EC], in0=link[:], scalar=-float(SKIP), in1=tmp[:],
                                        op0=ALU.mult, op1=ALU.add))
            V.tensor_copy(pay_out[:, 0:EC, 0], src_i[:])
            V.tensor_copy(con["edge_src"][:], src_i[:])
            V.tensor_copy(con["edge_dst"][:], dst_i[:, own])
            then(V.tensor_tensor(pay_out[:, 0:EC, 1], d[:, own], tb[:, own], ALU.subtract))
            then(V.tensor_tensor(tmp[:], d[:, own], d[:, prev], ALU.is_lt))
            then(V.tensor_reduce(sums[:, 0:1], tmp[:], AX.X, ALU.add))
            then(V.tensor_scalar(tmp[:], slot[:], P - 0.5, None, ALU.is_gt))
            then(V.tensor_tensor(tmp[:], tmp[:], link[:], ALU.mult))
            then(V.tensor_reduce(sums[:, 1:2], tmp[:], AX.X, ALU.add))
            V.tensor_reduce(sums[:, 2:3], loop[:], AX.X, ALU.add).then_inc(sums_ready, 1)
            dve.wait_ge(sums_up, 1)
            then(V.tensor_copy(total[:], ps_row[0:1, 0:3]))
            then(V.tensor_scalar(total[0:1, 2:3], total[0:1, 2:3], float(pl.N), None, ALU.not_equal))
            then(V.tensor_reduce(bad[:], total[:], AX.X, ALU.add))
            then(V.tensor_scalar(con["flag"][:], bad[:], 0.5, None, ALU.is_lt))


def project(nc, pl, con, x, weights, biases, qv_dram, ks_dram, link_dram, idx, pay):
    D, C, H = pl.D, pl.C, pl.H
    KW = D + H
    with ExitStack() as ctx:
        def sb(n, s, d=F32):
            return ctx.enter_context(nc.sbuf_tensor("proj_" + n, s, d))

        def ps(n):
            return ctx.enter_context(nc.psum_tensor("proj_" + n, [P, 512], F32))

        def sem(n):
            return ctx.enter_context(nc.semaphore("proj_" + n))
        wraw = sb("wraw", [P, 3 * C, D])
        wT = sb("wT", [P, C, 3 * D])
        w_hi, w_lo = sb("w_hi", [P, C, 3 * D], F32R), sb("w_lo", [P, C, 3 * D], F32R)
        k_bias = sb("k_bias", [P, D])
        BR = 32
        bias, bias_hi = sb("bias", [2 * BR, 2 * D]), sb("bias_hi", [2 * BR, 2 * D], F32R)
        bias_rows, ones = sb("bias_rows", [2 * BR, 2 * D], F32R), sb("ones", [2 * BR, P], F32R)
        xq = [sb(f"xq{u}", [P, QT, D]) for u in range(2)]
        st, mv = sb("st", [P, 2, QT, 6]), sb("mv", [P, 2, QT, 2])
        sd, rstd, nmr = sb("sd", [P, 2, QT]), sb("rstd", [P, 2, QT]), sb("nmr", [P, 2, QT])
        h = sb("h", [P, 2, D])
        hT_hi, hT_lo = sb("hT_hi", [P, 2, D], F32R), sb("hT_lo", [P, 2, D], F32R)
        prod = sb("prod", [P, 2, D])
        qv = [sb(f"qv{u}", [P, QT, 2 * D]) for u in range(2)]
        ks = [sb(f"ks{u}", [P, QT, KW]) for u in range(2)]
        sidx, spay = sb("sidx", [P, 2, 8], I32), sb("spay", [P, 2, 16], I32)
        psT, psQV, psK = [ps(f"psT{b}") for b in range(2)], [ps(f"psQV{b}") for b in range(2)], [ps(f"psK{b}") for b in range(2)]
        w_in, w_up, w_ready, x_clear = sem("w_in"), sem("w_up"), sem("w_ready"), sem("x_clear")
        tail_in = sem("tail_in")
        x_in = [sem(f"x_in{u}") for u in range(2)]
        qv_out = [sem(f"qv_out{u}") for u in range(2)]
        h_free_of_x = sem("x_read")
        stats, var, std, rs, norm = sem("stats"), sem("var"), sem("std"), sem("rs"), sem("norm")
        h_ready, hT_up, hT_ready, qkv_up, k_read = (sem("h_ready"), sem("hT_up"), sem("hT_ready"),
                                                      sem("qkv_up"), sem("k_read"))
        prod_ready = sem("prod_ready")
        w_hi_ready, parts_ready, hT_hi_ready, qv_kept = sem("w_hi_ready"), sem("parts_ready"), sem("hT_hi_ready"), sem("qv_kept")
        qv_ready = sem("qv_ready")
        passed = sem("passed")
        staged, scattered = sem("staged"), [sem(f"scattered{b}") for b in range(2)]
        block = ctx.enter_context(nc.Block())
        last = pl.turns - 1

        @block.sync
        def _(sp):
            for m, w in enumerate(weights):
                for c in range(C):
                    sp.dma_start(wraw[:, m * C + c, :], w[c * P:(c + 1) * P, :]).then_inc(w_in, 16)
            sp.dma_start(k_bias[:], biases[2].rearrange("(o d) -> o d", o=1).to_broadcast([P, D])).then_inc(w_in, 16)
            sp.wait_ge(x_clear, 1)
            for m in range(2):
                for r in (0, BR):
                    sp.dma_start(bias[r:r + 1, m * D:(m + 1) * D],
                                 biases[m].rearrange("(o d) -> o d", o=1)).then_inc(w_in, 16)

            def load(i, u):
                sp.wait_ge(h_free_of_x, 2 * i + u + 1)
                sp.dma_start(xq[u][:], quad_rows(x, i * (BODY * P) + u * pl.QR)).then_inc(x_in[u], 16)

            def store(i, u):
                sp.wait_ge(qv_ready, 2 * i + u + 1)
                sp.wait_ge(qv_kept, (2 * i + u) * QT + QT + 2)
                at = i * (BODY * P) + u * pl.QR
                sp.dma_start(quad_rows(qv_dram, at), qv[u][:]).then_inc(qv_out[u], 16)
                sp.dma_start(quad_rows(ks_dram, at), ks[u][:]).then_inc(qv_out[u], 16)
            sp.sem_inc(qv_out[0], 32)
            sp.sem_inc(qv_out[1], 32)
            load(0, 0)
            load(0, 1)
            with sp.Fori(0, last - 1) as i:
                load(i + 1, 0)
                store(i, 0)
                load(i + 1, 1)
                store(i, 1)
            load(last, 0)
            store(last - 1, 0)
            sp.wait_ge(h_free_of_x, 2 * last + 2)
            parts = ragged(x, last * BODY * P + pl.QR, pl.last_rows, xq[1])
            for dram, tile in parts[:-1]:
                sp.dma_start(tile, dram).then_inc(tail_in, 16)
            if len(parts) > 1:
                sp.wait_ge(tail_in, 16)
            sp.dma_start(parts[-1][1], parts[-1][0]).then_inc(x_in[1], 16)
            store(last - 1, 1)
            store(last, 0)
            store(last, 1)
            for u in range(2):
                sp.wait_ge(qv_out[u], 32 * (pl.turns + 1))

        @where(block.gpsimd, con, True)
        def _(pool):
            bound = pool.to_reg(P * pl.NT - 1)

            def scatter(i, b, first):
                if not first:
                    pool.wait_ge(scattered[b], i * 128)
                nc.gpsimd.tensor_copy(sidx[:, b, :], idx[:, bass.ds(i * 16 + b * 8, 8)])
                nc.gpsimd.tensor_copy(spay[:, b, :],
                                      pay[:].rearrange("p e w -> p (e w)")[:, bass.ds(i * 32 + b * 16, 16)]
                                      ).then_inc(staged, 1)
                pool.wait_ge(staged, i * 2 + b + 1)
                pool.sem_inc(passed, 1)
                for c in range(8):
                    nc.gpsimd.indirect_dma_start(
                        out=link_dram[:, :], out_offset=bass.IndirectOffsetOnAxis(ap=sidx[:, b, c:c + 1], axis=0),
                        in_=spay[:, b, 2 * c:2 * c + 2], in_offset=None,
                        bounds_check=bound, oob_is_err=False).then_inc(scattered[b], 16)
            scatter(0, 0, True)
            scatter(0, 1, True)
            with pool.Fori(1, pl.EB // 16) as i:
                scatter(i, 0, False)
                scatter(i, 1, False)
            for b in range(2):
                pool.wait_ge(scattered[b], 128 * (pl.EB // 16))

        @block.tensor
        def _(pe):
            pe.wait_ge(w_in, 16 * (3 * C + 5))
            for m in range(3):
                for c in range(C):
                    for r in range(C):
                        n = (m * C + c) * C + r
                        if n >= 2:
                            pe.wait_ge(w_ready, n - 1)
                        nc.tensor.transpose(psT[n % 2][:, 0:P], wraw[:, m * C + c, r * P:(r + 1) * P],
                                            con["ident"][:]).then_inc(w_up, 1)
            pe.wait_ge(parts_ready, 1)
            pe.sem_inc(hT_up, 2)

            def up(n, b):
                pe.wait_ge(h_ready, n + 1)
                pe.wait_ge(hT_ready, n + 1)
                for c in range(C):
                    ins = nc.tensor.transpose(psT[b][:, c * P:(c + 1) * P], h[:, b, c * P:(c + 1) * P], con["ident"][:])
                ins.then_inc(hT_up, 1)

            def products(n, b):
                pe.wait_ge(hT_ready, n + 3)
                pe.wait_ge(k_read, n + 1)
                pe.wait_ge(qv_kept, n + 1)
                nc.tensor.matmul(psQV[b][:, :], ones[:], bias_rows[:], start=True, stop=False)
                for bank, cols in ((psQV[b][:, :], slice(0, 2 * D)), (psK[b][:, 0:D], slice(2 * D, 3 * D))):
                    for c in range(C):
                        part = slice(c * P, (c + 1) * P)
                        fresh = c == 0 and cols.start > 0
                        nc.tensor.matmul(bank, hT_hi[:, b, part], w_hi[:, c, cols], start=fresh, stop=False)
                        nc.tensor.matmul(bank, hT_hi[:, b, part], w_lo[:, c, cols], start=False, stop=False)
                        ins = nc.tensor.matmul(bank, hT_lo[:, b, part], w_hi[:, c, cols], start=False, stop=(c == C - 1))
                ins.then_inc(qkv_up, 1)
            up(0, 0)

            def turn(i, end):
                for k in range(BODY):
                    n = i * BODY + k
                    if not (end and k == BODY - 1):
                        up(n + 1, (k + 1) % 2)
                    products(n, k % 2)
            with pe.Fori(0, last) as i:
                turn(i, False)
            turn(last, True)

        @block.scalar
        def _(act):
            n = 0
            for m in range(3):
                for c in range(C):
                    for r in range(C):
                        act.wait_ge(w_up, n + 1)
                        nc.scalar.copy(wT[:, r, m * D + c * P:m * D + (c + 1) * P], psT[n % 2][:, 0:P]).then_inc(w_ready, 1)
                        n += 1
            act.wait_ge(w_ready, 3 * C * C)
            act.wait_ge(w_in, 16 * (3 * C + 5))
            nc.scalar.copy(w_hi[:], wT[:])
            nc.scalar.copy(ones[:], con["ones"][0:2 * BR, :])
            nc.scalar.copy(bias_rows[0:BR, :], bias[0:BR, :])
            nc.scalar.copy(bias_hi[:], bias[:]).then_inc(w_hi_ready, 1)
            act.sem_inc(h_free_of_x, 2)
            act.sem_inc(qv_kept, 2)

            def deviation(i, u):
                act.wait_ge(var, 2 * i + u + 1)
                nc.scalar.activation(sd[:, u, :], mv[:, u, :, 1], ACT.Sqrt, bias=con["eps"][:, 0:1]).then_inc(std, 1)

            def normalize(i, k):
                u, t, n = k // QT, k % QT, i * BODY + k
                if t == 0:
                    act.wait_ge(norm, 2 * i + u + 1)
                act.wait_ge(hT_up, n + 1)
                ins = nc.scalar.activation(h[:, k % 2, :], xq[u][:, t, :], ACT.Relu,
                                           bias=nmr[:, u, t:t + 1], scale=rstd[:, u, t:t + 1])
                ins.then_inc(h_ready, 1)
                if t == QT - 1:
                    act.wait_ge(h_ready, n + 1)
                    act.sem_inc(h_free_of_x, 1)

            def keep(i, k):
                n = i * BODY + k
                act.wait_ge(hT_up, n + 3)
                act.wait_ge(qkv_up, n + 1)
                nc.scalar.copy(hT_hi[:, k % 2, :], psT[k % 2][:, 0:D]).then_inc(hT_hi_ready, 1)

            def keep_qv(i, k):
                u, t, n = k // QT, k % QT, i * BODY + k
                if t == 0:
                    act.wait_ge(qv_out[u], i * 32 + 32)
                act.wait_ge(qkv_up, n + 3)
                nc.scalar.copy(qv[u][:, t, :], psQV[k % 2][:, :]).then_inc(qv_kept, 1)
            deviation(0, 0)

            def turn(i, first, end):
                for k in range(BODY):
                    normalize(i, k)
                    if k >= 2:
                        keep_qv(i, k - 2)
                    elif not first:
                        keep_qv(i - 1, BODY + k - 2)
                    if k == 3:
                        deviation(i, 1)
                    if k == QT + 3 and not end:
                        deviation(i + 1, 0)
                    keep(i, k)
            turn(0, True, False)
            with act.Fori(1, last) as i:
                turn(i, False, False)
            turn(last, False, True)
            keep_qv(last, BODY - 2)
            keep_qv(last, BODY - 1)

        @block.vector
        def _(dve):
            V = nc.vector
            V.memset(bias[:], 0.0)
            V.memset(xq[1][:], 0.0).then_inc(x_clear, 1)
            dve.sem_inc(k_read, 2)
            dve.wait_ge(w_in, 16 * (3 * C + 5))
            dve.wait_ge(w_hi_ready, 1)
            V.tensor_tensor(w_lo[:], wT[:], w_hi[:].bitcast(F32), ALU.subtract)
            V.tensor_tensor(bias_rows[BR:2 * BR, :], bias[BR:2 * BR, :], bias_hi[BR:2 * BR, :].bitcast(F32),
                            ALU.subtract).then_inc(parts_ready, 1)
            dve.sem_inc(hT_ready, 2)
            dve.sem_inc(qkv_up, 2)

            def statistics(i, u, part):
                q = 2 * i + u
                dve.wait_ge(x_in[u], i * 16 + 16)
                half = QT // 2
                for t in (range(half) if part == 0 else range(half, QT)):
                    ins = V.bn_stats(st[:, u, t, :], xq[u][:, t, :])
                if part == 0:
                    return
                ins.then_inc(stats, 1)
                dve.wait_ge(stats, q + 1)
                dve.sem_inc(passed, 1)
                for t in range(QT):
                    ins = V.bn_aggr(mv[:, u, t, :], st[:, u, t, :])
                ins.then_inc(var, 1)

            def shift(i, u):
                q = 2 * i + u
                dve.wait_ge(std, q + 1)
                V.reciprocal(rstd[:, u, :], sd[:, u, :]).then_inc(rs, 1)
                dve.wait_ge(rs, q + 1)
                V.scalar_tensor_tensor(out=nmr[:, u, :], in0=mv[:, u, :, 0], scalar=-1.0, in1=rstd[:, u, :],
                                       op0=ALU.mult, op1=ALU.mult).then_inc(norm, 1)

            def split(i, k):
                n, b = i * BODY + k, k % 2
                dve.wait_ge(hT_hi_ready, n + 1)
                V.tensor_tensor(hT_lo[:, b, :], psT[b][:, 0:D], hT_hi[:, b, :].bitcast(F32), ALU.subtract).then_inc(hT_ready, 1)

            def collect(i, k, first):
                u, t, n, b = k // QT, k % QT, i * BODY + k, k % 2
                dve.wait_ge(qkv_up, n + 3)
                if t == 0:
                    dve.wait_ge(qv_out[u], i * 32 + 32)
                V.tensor_tensor(ks[u][:, t, 0:D], psK[b][:, 0:D], k_bias[:], ALU.add).then_inc(k_read, 1)
                if not (first and k == 0):
                    loop_score(n - 1, (k - 1) % BODY)
                dve.wait_ge(k_read, n + 3)
                dve.wait_ge(qv_kept, n + 3)
                V.tensor_tensor(prod[:, b, :], qv[u][:, t, 0:D], ks[u][:, t, 0:D], ALU.mult).then_inc(prod_ready, 1)

            def loop_score(n, k):
                u, t, b = k // QT, k % QT, k % 2
                dve.wait_ge(prod_ready, n + 1)
                ins = V.tensor_reduce(ks[u][:, t, D:KW], prod[:, b, :].rearrange("p (h d) -> p h d", h=H), AX.X, ALU.add)
                if t == QT - 1:
                    ins.then_inc(qv_ready, 1)
            statistics(0, 0, 0)
            statistics(0, 0, 1)
            shift(0, 0)
            split(0, 0)

            def turn(i, first, end):
                for k in range(BODY):
                    following = (i, 1) if k < QT else None if end else (i + 1, 0)
                    if following and k % QT < 2:
                        statistics(*following, k % QT)
                    if k < BODY - 1:
                        split(i, k + 1)
                    elif not end:
                        split(i + 1, 0)
                    if following and k % QT == 2:
                        shift(*following)
                    collect(i, k, first)
            turn(0, True, False)
            with dve.Fori(1, last) as i:
                turn(i, False, False)
            turn(last, False, True)
            loop_score(last * BODY + BODY - 1, BODY - 1)


def attend(nc, pl, con, x, w_out, b_out, qv_dram, ks_dram, link_dram, mask_embed, x1_dram, h_dram):
    D, C, H, hd = pl.D, pl.C, pl.H, pl.hd
    KW, QH = D + H, QT * H
    SCALE = float(hd) ** -0.5
    PAIR = 2 * D
    with ExitStack() as ctx:
        def sb(n, s, d=F32):
            return ctx.enter_context(nc.sbuf_tensor("att_" + n, s, d))

        def ps(n):
            return ctx.enter_context(nc.psum_tensor("att_" + n, [P, 512], F32))

        def sem(n):
            return ctx.enter_context(nc.semaphore("att_" + n))
        wraw, wT, bias = sb("wo_raw", [P, C, D]), sb("woT", [P, C, D]), sb("bo", [P, QT, D])
        rows = [sb(f"rows{u}", [P, QT, 2 * D]) for u in range(2)]
        ks = [sb(f"ksn{u}", [P, QT, KW]) for u in range(2)]
        xs = [sb(f"xs{u}", [P, QT, D]) for u in range(2)]
        vs = [sb(f"vs{u}", [P, QT, D]) for u in range(2)]
        hot = [sb(f"hot{u}", [P, QT, P]) for u in range(2)]
        gap = [sb(f"gap{u}", [P, QT, P]) for u in range(2)]
        lidx, ldst = sb("lidx", [P, 2, QT], I32), sb("ldst", [P, 2, QT])
        hotT = sb("hotT", [P, QT, P])
        prod, pv = sb("prod", [P, QT, D]), sb("pv", [P, QT, D])
        slot_sc = sb("slot_sc", [P, 3, QT, H])
        tsc = sb("tsc", [QH, 3, P])
        same, cut = sb("same", [QH, P + 1]), sb("cut", [QH, P + 1])
        top, fwd, bwd = sb("top", [QH, P]), sb("fwd", [QH, P]), sb("bwd", [QH, P])
        dif, ex, tot = sb("dif", [QH, 2, P]), sb("ex", [QH, 2, P]), sb("tot", [QH, P])
        tp = sb("tp", [QH, 3, P])
        pr, inv = sb("pr", [P, QT, H]), sb("inv", [P, QT, H])
        fin = sb("fin", [P, QT, 2 * H + 1])
        own = sb("own", [P, QT, 2 * H + 1])
        pself = sb("pself", [P, QT, H])
        vself = sb("vself", [P, QT, D])
        o, oT = sb("o", [P, QT, D]), sb("oT", [P, QT, D])
        x1 = [sb(f"x1_{u}", [P, QT, D]) for u in range(2)]
        ho = [sb(f"ho{u}", [P, QT, D]) for u in range(2)]
        st, mv = sb("st2", [P, QT, 6]), sb("mv2", [P, 2, QT, 2])
        rstd, nmr, power = sb("rstd2", [P, 2, QT]), sb("nmr2", [P, 2, QT]), sb("power", [P, QT])
        ps_T, ps_k = ps("ps_T"), [ps("ps_k0"), ps("ps_k1")]
        ps_sm, ps_g, ps_p = ps("ps_sm"), [ps("ps_g0"), ps("ps_g1")], [ps("ps_p0"), ps("ps_p1")]

        setup_in, bufs_clear, w_up, w_ready = sem("setup_in"), sem("bufs_clear"), sem("w_up"), sem("w_ready")
        table_ready, staged = sem("table_ready"), sem("staged")
        rows_in = [sem(f"rows_in{u}") for u in range(2)]
        ks_in, xs_in, vs_in = ([sem(f"{n}{u}") for u in range(2)] for n in ("ks_in", "xs_in", "vs_in"))
        x1_out, h_out = ([sem(f"{n}{u}") for u in range(2)] for n in ("x1_out", "h_out"))
        gap_ready, square_ready = sem("gap_ready"), sem("square_ready")
        hot_ready, hot_up, hotT_ready, k_read, score_ready, sc_up, soft = (
            sem("hot_ready"), sem("hot_up"), sem("hotT_ready"), sem("k_read"), sem("score_ready"), sem("sc_up"), sem("soft"))
        dif_ready, ex_ready, tp_ready, pr_ready = sem("dif_ready"), sem("ex_ready"), sem("tp_ready"), sem("pr_ready")
        own_up, own_read, pself_half, pself_ready, vself_ready = (
            sem("own_up"), sem("own_read"), sem("pself_half"), sem("pself_ready"), sem("vself_ready"))
        bias_added, x1_ready, stats, var, rs, norm, h_ready = (
            sem("bias_added"), sem("x1_ready"), sem("stats"), sem("var"), sem("rs"), sem("norm"), sem("h_ready"))
        tp_up = sem("tp_up")
        tsc_ready, inv_ready = sem("tsc_ready"), sem("inv_ready")
        k_up, prod_ready, pv_ready, g_up, o_ready, o_up, oT_ready, p_up = (
            sem("k_up"), sem("prod_ready"), sem("pv_ready"), sem("g_up"), sem("o_ready"), sem("o_up"),
            sem("oT_ready"), sem("p_up"))
        mask_out = sem("mask_out")
        passed = sem("passed")
        block = ctx.enter_context(nc.Block())
        last = pl.turns - 1
        quads = 2 * pl.turns

        def later(count):
            return not isinstance(count, int) or count > 0

        def before(i, u):
            return (i, 0) if u else (i - 1, 1)

        def after(i, u):
            return (i + 1, 0) if u else (i, 1)

        def exists(i, u):
            return not isinstance(i, int) or 0 <= 2 * i + u < quads

        def steps(eng, body):
            body(0, 0)
            body(0, 1)
            with eng.Fori(1, last) as i:
                body(i, 0)
                body(i, 1)
            body(last, 0)
            body(last, 1)

        def pair(v, j):
            return v[:, 2 * j:2 * j + 2, :]

        def bank(b):
            return b[:, 0:PAIR].rearrange("p (t d) -> p t d", t=2)

        @where(block.sync, con, True)
        def _(sp):
            for c in range(C):
                sp.dma_start(wraw[:, c, :], w_out[c * P:(c + 1) * P, :]).then_inc(setup_in, 16)
            for t in range(QT):
                sp.dma_start(bias[:, t, :], b_out.rearrange("(o d) -> o d", o=1).to_broadcast([P, D])).then_inc(setup_in, 16)
            sp.dma_start(con["links"][:], link_dram.rearrange("(p t) w -> p t w", p=P)).then_inc(setup_in, 16)
            sp.wait_ge(bufs_clear, 1)
            for u in range(2):
                sp.sem_inc(x1_out[u], 16)
                sp.sem_inc(h_out[u], 16)

            def base(i, u):
                return i * (BODY * P) + u * pl.QR

            def load_k(i, u):
                q = 2 * i + u
                if later(q - 1):
                    sp.wait_ge(tp_up, q - 1)
                sp.dma_start(ks[u][:], quad_rows(ks_dram, base(i, u))).then_inc(ks_in[u], 16)

            def load_v(i, u):
                q = 2 * i + u
                if later(q - 1):
                    sp.wait_ge(vself_ready, q - 1)
                sp.dma_start(vs[u][:], quad_rows(qv_dram, base(i, u), (D, 2 * D))).then_inc(vs_in[u], 16)

            def load_x(i, u):
                q = 2 * i + u
                if later(q - 1):
                    sp.wait_ge(x1_ready, q - 1)
                if not exists(i + 1, u) and u == 1:
                    parts = ragged(x, last * BODY * P + pl.QR, pl.last_rows, xs[1])
                    for dram, tile in parts[:-1]:
                        sp.dma_start(tile, dram).then_inc(mask_out, 16)
                    if len(parts) > 1:
                        sp.wait_ge(mask_out, 16)
                    sp.dma_start(parts[-1][1], parts[-1][0]).then_inc(xs_in[1], 16)
                else:
                    sp.dma_start(xs[u][:], quad_rows(x, base(i, u))).then_inc(xs_in[u], 16)

            def store(i, u):
                sp.wait_ge(h_ready, 2 * i + u + 1)
                sp.dma_start(quad_rows(x1_dram, base(i, u)), x1[u][:]).then_inc(x1_out[u], 16)
                sp.dma_start(quad_rows(h_dram, base(i, u)), ho[u][:]).then_inc(h_out[u], 16)
            load_k(0, 0)
            load_k(0, 1)
            load_v(0, 0)
            load_x(0, 0)

            def step(i, u):
                if exists(i + 1, u):
                    load_k(i + 1, u)
                if exists(*after(i, u)):
                    load_v(*after(i, u))
                if exists(i - 1, u):
                    store(i - 1, u)
                if exists(*after(i, u)):
                    load_x(*after(i, u))
            steps(sp, step)
            store(last, 0)
            store(last, 1)
            for u in range(2):
                sp.wait_ge(x1_out[u], 16 * (pl.turns + 1))
                sp.wait_ge(h_out[u], 16 * (pl.turns + 1))
            sp.dma_start(h_dram[0:1, :], mask_embed.rearrange("(o d) -> o d", o=1)).then_inc(mask_out, 16)
            sp.wait_ge(mask_out, 16 * len(ragged(x, last * BODY * P + pl.QR, pl.last_rows, xs[1])))

        @where(block.gpsimd, con, True)
        def _(pool):
            for u in range(2):
                nc.gpsimd.memset(rows[u][:], 0.0)
            nc.gpsimd.memset(power[:], -0.5)
            nc.gpsimd.memset(xs[1][:], 0.0).then_inc(bufs_clear, 1)
            pool.wait_ge(setup_in, 16 * (C + QT + 1))
            nc.gpsimd.tensor_copy(con["dloc"][:], con["links"][:, :, 1]).then_inc(table_ready, 1)
            pool.wait_ge(table_ready, 1)
            pool.wait_ge(bufs_clear, 1)
            bound = pool.to_reg(pl.NP - 1)

            def mark(i, u):
                q = 2 * i + u
                if later(q - 1):
                    pool.wait_ge(hot_ready, q - 1)
                    pool.wait_ge(score_ready, q - 1)
                nc.gpsimd.tensor_copy(lidx[:, u, :], con["links"][:, bass.ds(i * BODY + u * QT, QT), 0])
                nc.gpsimd.tensor_copy(ldst[:, u, :], con["dloc"][:, bass.ds(i * BODY + u * QT, QT)]).then_inc(staged, 1)
                pool.wait_ge(staged, q + 1)
                nc.gpsimd.tensor_tensor(gap[u][:], con["iota"][:], ldst[:, u, :].to_broadcast([P, QT, P]),
                                        ALU.subtract).then_inc(gap_ready, 1)

            def gather(i, u):
                q = 2 * i + u
                for t in range(QT):
                    if t % 2 == 0 and later(2 * q - 3 + t // 2):
                        pool.wait_ge(pv_ready, 2 * q - 3 + t // 2)
                        pool.sem_inc(passed, 1)
                    nc.gpsimd.indirect_dma_start(
                        out=rows[u][:, t, :], out_offset=None, in_=qv_dram[:, :],
                        in_offset=bass.IndirectOffsetOnAxis(ap=lidx[:, u, t:t + 1], axis=0),
                        bounds_check=bound, oob_is_err=False).then_inc(rows_in[u], 16)

            def weigh_own(i, u):
                q = 2 * i + u
                pool.wait_ge(vs_in[u], i * 16 + 16)
                if later(2 * q):
                    pool.wait_ge(o_ready, 2 * q)
                pool.wait_ge(pself_ready, q + 1)
                nc.gpsimd.tensor_tensor(vself[:].rearrange("p t (h d) -> p (t h) d", h=H),
                                        vs[u][:].rearrange("p t (h d) -> p (t h) d", h=H),
                                        pself[:].rearrange("p t h -> p (t h)").to_broadcast([P, QH, hd]),
                                        ALU.mult).then_inc(vself_ready, 1)

            def shift(i, u):
                q = 2 * i + u
                pool.wait_ge(var, q + 1)
                pool.sem_inc(passed, 1)
                nc.gpsimd.tensor_scalar(rstd[:, u, :], mv[:, u, :, 1], EPS, 1.0, ALU.add, ALU.mult).then_inc(rs, 1)
                pool.wait_ge(rs, 3 * q + 1)
                nc.gpsimd.tensor_tensor(rstd[:, u, :], rstd[:, u, :], power[:], ALU.pow).then_inc(rs, 1)
                pool.wait_ge(rs, 3 * q + 2)
                nc.gpsimd.tensor_tensor(nmr[:, u, :], mv[:, u, :, 0], rstd[:, u, :], ALU.mult).then_inc(rs, 1)
                pool.wait_ge(rs, 3 * q + 3)
                pool.sem_inc(passed, 1)
                nc.gpsimd.tensor_scalar(nmr[:, u, :], nmr[:, u, :], -1.0, 0.0, ALU.mult, ALU.add).then_inc(norm, 1)

            def add_bias(i, u):
                pool.wait_ge(xs_in[u], i * 16 + 16)
                nc.gpsimd.tensor_tensor(xs[u][:], xs[u][:], bias[:], ALU.add).then_inc(bias_added, 1)
            for u in range(2):
                mark(0, u)
                gather(0, u)

            def step(i, u):
                if exists(i + 1, u):
                    mark(i + 1, u)
                add_bias(i, u)
                if exists(i + 1, u):
                    gather(i + 1, u)
                weigh_own(i, u)
                if exists(*before(i, u)):
                    shift(*before(i, u))
            steps(pool, step)
            shift(last, 1)

        @where(block.tensor, con, True)
        def _(pe):
            pe.wait_ge(setup_in, 16 * (C + QT + 1))
            for n in range(C * C):
                c, r = n // C, n % C
                if n:
                    pe.wait_ge(w_ready, n)
                nc.tensor.transpose(ps_T[:, 0:P], wraw[:, c, r * P:(r + 1) * P], con["ident"][:]).then_inc(w_up, 1)
            pe.wait_ge(w_ready, C * C)

            def expand(i, u):
                q = 2 * i + u
                pe.wait_ge(hot_ready, q + 1)
                if later(2 * q - 4):
                    pe.wait_ge(oT_ready, 2 * q - 4)
                for t in range(QT):
                    ins = nc.tensor.transpose(ps_T[:, t * P:(t + 1) * P], hot[u][:, t, :], con["ident"][:])
                ins.then_inc(hot_up, 1)
                pe.wait_ge(ks_in[u], i * 16 + 16)
                pe.wait_ge(hotT_ready, q + 1)
                if later(q):
                    pe.wait_ge(k_read, q)
                for t in range(QT):
                    ins = nc.tensor.matmul(ps_k[t // 2][:, (t % 2) * D:(t % 2 + 1) * D], hotT[:, t, :], ks[u][:, t, 0:D],
                                           start=True, stop=True)
                    if t % 2:
                        ins.then_inc(k_up, 1)

            def expand_loops(u):
                for t in range(QT):
                    ins = nc.tensor.matmul(ps_sm[:, 4 * QH + t * H:4 * QH + (t + 1) * H], hotT[:, t, :],
                                           ks[u][:, t, D:KW], start=True, stop=True)
                return ins

            def turn_scores(i, u):
                q = 2 * i + u
                pe.wait_ge(score_ready, q + 1)
                if later(q):
                    pe.wait_ge(own_read, q)
                for a in range(3):
                    ins = nc.tensor.transpose(ps_sm[0:QH, a * P:(a + 1) * P],
                                              slot_sc[:, a, :, :].rearrange("p t h -> p (t h)"), con["ident"][:])
                ins.then_inc(sc_up, 1)

            def turn_shares(i, u):
                q = 2 * i + u
                pe.wait_ge(tp_ready, q + 1)
                pe.sem_inc(passed, 1)
                for a, part in enumerate((ex[:, 0, :], tp[:, 0, :], tp[:, 1, :], tp[:, 2, :])):
                    ins = nc.tensor.transpose(ps_sm[:, a * QH:(a + 1) * QH], part, con["ident"][0:QH, 0:QH])
                if exists(*after(i, u)):
                    ins = expand_loops(1 - u)
                ins.then_inc(tp_up, 1)

            def own_shares(i, u):
                pe.wait_ge(pr_ready, 2 * i + u + 1)
                for t in range(QT):
                    ins = nc.tensor.matmul(ps_sm[:, t * 32:t * 32 + 2 * H + 1], hot[u][:, t, :], fin[:, t, :],
                                           start=True, stop=True)
                ins.then_inc(own_up, 1)

            def sum_links(i, u):
                q = 2 * i + u
                if later(2 * q):
                    pe.wait_ge(o_ready, 2 * q)
                for j in range(2):
                    pe.wait_ge(pv_ready, 2 * q + j + 1)
                    for t in (2 * j, 2 * j + 1):
                        ins = nc.tensor.matmul(ps_g[j][:, (t % 2) * D:(t % 2 + 1) * D], hot[u][:, t, :], pv[:, t, :],
                                               start=True, stop=True)
                    ins.then_inc(g_up, 1)

            def turn_o(i, u):
                q = 2 * i + u
                for j in range(2):
                    if j:
                        pe.wait_ge(oT_ready, 2 * q + 1)
                    pe.wait_ge(o_ready, 2 * q + j + 1)
                    for t in (2 * j, 2 * j + 1):
                        for c in range(C):
                            at = (t % 2) * D + c * P
                            ins = nc.tensor.transpose(ps_T[:, at:at + P], o[:, t, c * P:(c + 1) * P], con["ident"][:])
                    ins.then_inc(o_up, 1)

            def project_out(i, u, j):
                q = 2 * i + u
                if later(q):
                    pe.wait_ge(x1_ready, q)
                pe.wait_ge(oT_ready, 2 * q + j + 1)
                for t in (2 * j, 2 * j + 1):
                    for c in range(C):
                        ins = nc.tensor.matmul(ps_p[j][:, (t % 2) * D:(t % 2 + 1) * D], oT[:, t, c * P:(c + 1) * P],
                                               wT[:, c, :], start=(c == 0), stop=(c == C - 1))
                ins.then_inc(p_up, 1)
            expand(0, 0)
            expand_loops(0).then_inc(tp_up, 1)
            turn_scores(0, 0)
            expand(0, 1)

            def step(i, u):
                if exists(*before(i, u)):
                    turn_o(*before(i, u))
                    project_out(*before(i, u), 0)
                turn_shares(i, u)
                if exists(*before(i, u)):
                    project_out(*before(i, u), 1)
                own_shares(i, u)
                sum_links(i, u)
                if exists(*after(i, u)):
                    turn_scores(*after(i, u))
                if exists(i + 1, u):
                    expand(i + 1, u)
            steps(pe, step)
            turn_o(last, 1)
            project_out(last, 1, 0)
            project_out(last, 1, 1)

        @where(block.scalar, con, True)
        def _(act):
            for n in range(C * C):
                c, r = n // C, n % C
                act.wait_ge(w_up, n + 1)
                nc.scalar.copy(wT[:, r, c * P:(c + 1) * P], ps_T[:, 0:P]).then_inc(w_ready, 1)

            def flat(v):
                return v[:].rearrange("p t e -> p (t e)")

            def square(i, u):
                act.wait_ge(gap_ready, 2 * i + u + 1)
                nc.scalar.activation(flat(gap[u]), flat(gap[u]), ACT.Square).then_inc(square_ready, 1)

            def finish_hot(i, u):
                q = 2 * i + u
                act.wait_ge(square_ready, q + 1)
                if later(2 * q - 2):
                    act.wait_ge(g_up, 2 * q - 2)
                nc.scalar.activation(flat(hot[u]), flat(gap[u]), ACT.Relu, bias=con["ones"][:, 0:1], scale=-1.0
                                     ).then_inc(hot_ready, 1)

            def keep_hot(i, u):
                q = 2 * i + u
                act.wait_ge(hot_up, q + 1)
                if later(q):
                    act.wait_ge(tp_up, q)
                nc.scalar.copy(hotT[:].rearrange("p t e -> p (t e)"), ps_T[:, :]).then_inc(hotT_ready, 1)

            def keep_scores(i, u):
                q = 2 * i + u
                act.wait_ge(sc_up, q + 1)
                if later(q):
                    act.wait_ge(dif_ready, q)
                nc.scalar.copy(tsc[:].rearrange("p a s -> p (a s)"), ps_sm[0:QH, 0:3 * P]).then_inc(tsc_ready, 1)

            def exponent(i, u):
                act.wait_ge(dif_ready, 2 * i + u + 1)
                nc.scalar.activation(ex[:], dif[:], ACT.Exp, scale=SCALE).then_inc(ex_ready, 1)

            def keep_o(i, u):
                q = 2 * i + u
                if later(2 * q):
                    act.wait_ge(p_up, 2 * q)
                for j in range(2):
                    act.wait_ge(o_up, 2 * q + j + 1)
                    nc.scalar.copy(pair(oT, j).rearrange("p t d -> p (t d)"), ps_T[:, 0:PAIR]).then_inc(oT_ready, 1)

            def normalize(i, u):
                act.wait_ge(norm, 2 * i + u + 1)
                act.wait_ge(h_out[u], i * 16 + 16)
                for t in range(QT):
                    ins = nc.scalar.activation(ho[u][:, t, :], x1[u][:, t, :], ACT.Relu,
                                               bias=nmr[:, u, t:t + 1], scale=rstd[:, u, t:t + 1])
                ins.then_inc(h_ready, 1)
            square(0, 0)
            finish_hot(0, 0)
            keep_hot(0, 0)
            keep_scores(0, 0)
            square(0, 1)
            finish_hot(0, 1)
            keep_hot(0, 1)

            def step(i, u):
                exponent(i, u)
                if exists(*before(i, u)):
                    keep_o(*before(i, u))
                if exists(i - 1, u):
                    normalize(i - 1, u)
                if exists(i + 1, u):
                    square(i + 1, u)
                if exists(*after(i, u)):
                    keep_scores(*after(i, u))
                if exists(i + 1, u):
                    finish_hot(i + 1, u)
                    keep_hot(i + 1, u)
            steps(act, step)
            keep_o(last, 1)
            normalize(last, 0)
            normalize(last, 1)

        @where(block.vector, con, True)
        def _(dve):
            V = nc.vector
            dve.wait_ge(setup_in, 16 * (C + QT + 1))
            V.memset(same[:, 0:1], 0.0)
            V.memset(same[:, P:P + 1], 0.0)
            V.memset(fin[:], 1.0).then_inc(passed, 1)
            dve.wait_ge(passed, 1)
            STEPS = 6
            count = [0]

            def then(ins, q):
                count[0] += 1
                ins.then_inc(soft, 1)
                dve.wait_ge(soft, q * STEPS + count[0])

            def scores(i, u):
                q = 2 * i + u
                dve.wait_ge(rows_in[u], i * (16 * QT) + 16 * QT)
                dve.wait_ge(staged, q + 1)
                if later(q):
                    dve.wait_ge(sc_up, q)
                V.tensor_copy(slot_sc[:, 2, :, :], ldst[:, u, :].to_broadcast([P, QT, H]))
                for j in range(2):
                    dve.wait_ge(k_up, 2 * q + j + 1)
                    V.tensor_tensor(pair(prod, j), rows[u][:, 2 * j:2 * j + 2, 0:D], bank(ps_k[j]),
                                    ALU.mult).then_inc(prod_ready, 1)
                dve.wait_ge(prod_ready, 2 * q + 2)
                dve.sem_inc(k_read, 1)
                V.tensor_reduce(slot_sc[:, 0, :, :].rearrange("p t h -> p (t h)"),
                                prod[:].rearrange("p t (h d) -> p (t h) d", h=H), AX.X, ALU.add)

            def maxima(i, u):
                q = 2 * i + u
                count[0] = 0
                dve.wait_ge(tsc_ready, q + 1)
                V.tensor_tensor(top[:], tsc[:, 0, :], tsc[:, 1, :], ALU.max)
                then(V.tensor_tensor(same[:, 1:P], tsc[:, 2, 1:P], tsc[:, 2, 0:P - 1], ALU.is_equal), q)
                then(V.tensor_scalar(cut[:], same[:], -1.0, NEG, ALU.add, ALU.mult), q)
                V.tensor_tensor_scan(fwd[:], cut[:, 0:P], top[:], 0.0, ALU.add, ALU.max)
                then(V.tensor_tensor_scan(bwd[:, ::-1], cut[:, 1:P + 1][:, ::-1], top[:, ::-1], 0.0, ALU.add, ALU.max), q)
                then(V.tensor_tensor(fwd[:], fwd[:], bwd[:], ALU.max), q)
                V.tensor_tensor(dif[:, 0, :], tsc[:, 0, :], fwd[:], ALU.subtract)
                V.tensor_tensor(dif[:, 1, :], tsc[:, 1, :], fwd[:], ALU.subtract).then_inc(dif_ready, 1)

            def shares(i, u):
                q = 2 * i + u
                dve.wait_ge(ex_ready, q + 1)
                V.tensor_tensor_scan(fwd[:], same[:, 0:P], ex[:, 0, :], 0.0, ALU.mult, ALU.add)
                V.tensor_tensor_scan(bwd[:, ::-1], same[:, 1:P + 1][:, ::-1], ex[:, 0, ::-1], 0.0, ALU.mult, ALU.add)
                then(V.tensor_tensor(tot[:], ex[:, 1, :], ex[:, 0, :], ALU.subtract), q)
                V.tensor_tensor(fwd[:], fwd[:], bwd[:], ALU.add)
                then(V.tensor_scalar(tp[:, 1, :], same[:, 1:P + 1], -1.0, 1.0, ALU.mult, ALU.add), q)
                V.tensor_tensor(tp[:, 2, :], tot[:], fwd[:], ALU.add)
                V.tensor_tensor(tp[:, 0, :], ex[:, 1, :], tp[:, 1, :], ALU.mult).then_inc(tp_ready, 1)
                assert count[0] == STEPS, count

            def take_loops(q):
                V.tensor_copy(slot_sc[:, 1, :, :].rearrange("p t h -> p (t h)"),
                              ps_sm[:, 4 * QH:5 * QH]).then_inc(score_ready, 1)

            def back(i, u):
                q = 2 * i + u
                dve.wait_ge(tp_up, q + 2)
                V.reciprocal(inv[:].rearrange("p t h -> p (t h)"), ps_sm[:, 3 * QH:4 * QH]).then_inc(inv_ready, 1)
                V.tensor_copy(fin[:, :, H:2 * H], ps_sm[:, 2 * QH:3 * QH].rearrange("p (t h) -> p t h", h=H))
                dve.wait_ge(inv_ready, q + 1)
                V.tensor_tensor(pr[:].rearrange("p t h -> p (t h)"), ps_sm[:, 0:QH],
                                inv[:].rearrange("p t h -> p (t h)"), ALU.mult)
                if exists(*after(i, u)):
                    take_loops(q + 1)
                V.tensor_tensor(fin[:, :, 0:H], ps_sm[:, QH:2 * QH].rearrange("p (t h) -> p t h", h=H), inv[:],
                                ALU.mult).then_inc(pr_ready, 1)

            def weigh(i, u):
                q = 2 * i + u
                dve.wait_ge(pr_ready, q + 1)
                if later(2 * q):
                    dve.wait_ge(g_up, 2 * q)
                for t in range(QT):
                    ins = V.tensor_tensor(pv[:, t, :].rearrange("p (h d) -> p h d", h=H),
                                          rows[u][:, t, D:2 * D].rearrange("p (h d) -> p h d", h=H),
                                          pr[:, t, :].to_broadcast([P, H, hd]), ALU.mult)
                    if t % 2:
                        ins.then_inc(pv_ready, 1)

            def settle(i, u):
                q = 2 * i + u
                dve.wait_ge(own_up, q + 1)
                V.tensor_copy(own[:], ps_sm[:, 0:QT * 32].rearrange("p (t w) -> p t w", t=QT)[:, :, 0:2 * H + 1]
                              ).then_inc(own_read, 1)
                dve.wait_ge(own_read, q + 1)
                if later(q):
                    dve.wait_ge(vself_ready, q)
                V.tensor_tensor(pself[:], own[:, :, 0:H], own[:, :, H:2 * H], ALU.subtract).then_inc(pself_half, 1)
                V.tensor_scalar(con["deg"][:, bass.ds(i * BODY + u * QT, QT)], own[:, :, 2 * H], 1.0, None, ALU.add)
                dve.wait_ge(pself_half, q + 1)
                V.tensor_scalar(pself[:], pself[:], 1.0, None, ALU.add).then_inc(pself_ready, 1)

            def join(i, u):
                q = 2 * i + u
                dve.wait_ge(vself_ready, q + 1)
                if later(2 * q):
                    dve.wait_ge(o_up, 2 * q)
                for j in range(2):
                    dve.wait_ge(g_up, 2 * q + j + 1)
                    V.tensor_tensor(pair(o, j), bank(ps_g[j]), pair(vself, j), ALU.add).then_inc(o_ready, 1)

            def residual(i, u):
                q = 2 * i + u
                dve.wait_ge(bias_added, q + 1)
                dve.wait_ge(x1_out[u], i * 16 + 16)
                for j in range(2):
                    dve.wait_ge(p_up, 2 * q + j + 1)
                    ins = V.tensor_tensor(pair(x1[u], j), pair(xs[u], j), bank(ps_p[j]), ALU.add)
                ins.then_inc(x1_ready, 1)

            def layer_norm(i, u):
                q = 2 * i + u
                dve.wait_ge(x1_ready, q + 1)
                for t in range(QT):
                    ins = V.bn_stats(st[:, t, :], x1[u][:, t, :])
                ins.then_inc(stats, 1)
                dve.wait_ge(stats, q + 1)
                dve.sem_inc(passed, 1)
                for t in range(QT):
                    ins = V.bn_aggr(mv[:, u, t, :], st[:, t, :])
                ins.then_inc(var, 1)

            scores(0, 0)
            dve.wait_ge(tp_up, 1)
            take_loops(0)

            def step(i, u):
                maxima(i, u)
                if exists(*before(i, u)):
                    join(*before(i, u))
                shares(i, u)
                if exists(*after(i, u)):
                    scores(*after(i, u))
                back(i, u)
                weigh(i, u)
                if exists(*before(i, u)):
                    residual(*before(i, u))
                settle(i, u)
                if exists(*before(i, u)):
                    layer_norm(*before(i, u))
            steps(dve, step)
            join(last, 1)
            residual(last, 1)
            layer_norm(last, 1)
            dve.wait_ge(pself_ready, quads)
            V.reciprocal(con["inv_deg"][:], con["deg"][:])


def clear_signals(nc, signals):
    with nc.Block() as block:
        @block.gpsimd
        def _(pool):
            for s in signals:
                pool.sem_clear(s)


def lend(nc, signals, taken):
    if len(taken) == len(signals):
        signals.append(nc.alloc_semaphore(f"shared_{len(signals)}"))
    taken.append(signals[len(taken)])
    return taken[-1]


def edge_pass(nc, pl, con, signals, tag, kind, table, width, row_dram, ks_dram=None, top_dram=None, scores=None):
    D, H, hd, EC = pl.D, pl.H, pl.hd, pl.EC
    SCALE = float(hd) ** -0.5
    RW = row_dram.shape[1]
    with ExitStack() as ctx:
        def sb(n, s, d=F32):
            return ctx.enter_context(nc.sbuf_tensor(f"{tag}_{n}", s, d))

        def ps(n):
            return ctx.enter_context(nc.psum_tensor(f"{tag}_{n}", [P, 512], F32))
        isrc, idst, iput = sb("isrc", [P, 1], I32), sb("idst", [P, 1], I32), sb("iput", [P, 1], I32)
        rows, krow, old, new = sb("rows", [P, max(RW, width)]), sb("krow", [P, D + H]), sb("old", [P, width]), sb("new", [P, width])
        topr, val = sb("topr", [P, H]), sb("val", [P, width])
        dstf, wide, same, before = sb("dstf", [P, 1]), sb("wide", [P, P]), sb("same", [P, P]), sb("before", [P, P])
        tmp, cnt, fill = sb("tmp", [P, P]), sb("cnt", [P, 1]), sb("fill", [P, table.shape[1]])
        prod, s8, s8T = sb("prod", [P, D]), sb("s8", [P, H]), sb("s8T", [H, P])
        pick, big = sb("pick", [H, H, P]), sb("big", [P, H, P])
        p_d, p_a, p_b = ps("p_d"), ps("p_a"), ps("p_b")
        fetched, put = nc.alloc_semaphore(f"{tag}_fetched"), nc.alloc_semaphore(f"{tag}_put")
        taken = []
        done, dve_step, filled, built, passed = (lend(nc, signals, taken) for _ in range(5))
        steps = {"max": 11, "weigh": 11, "sum": 8}[kind]

        def reached(i, step):
            return i * steps + step + 1
        gathers = {"max": 3, "weigh": 3, "sum": 2}[kind]
        block = ctx.enter_context(nc.Block())

        @where(block.sync, con, False)
        def _(sp):
            sp.wait_ge(built, 2)
            with sp.Fori(0, pl.NT) as i:
                sp.dma_start(table[bass.ds(i * P, P), :], fill[:]).then_inc(filled, 16)
            sp.wait_ge(filled, 16 * pl.NT)
            sp.sem_inc(done, 1)

        @where(block.gpsimd, con, False)
        def _(pool):
            nc.gpsimd.memset(rows[:], 0.0)
            nc.gpsimd.memset(krow[:], 0.0)
            nc.gpsimd.memset(old[:], 0.0)
            nc.gpsimd.memset(topr[:], 0.0)
            nc.gpsimd.memset(before[:], 1.0)
            nc.gpsimd.memset(pick[:], 1.0).then_inc(passed, 1)
            pool.wait_ge(passed, 1)
            nc.gpsimd.affine_select(out=before[:], in_=before[:], compare_op=ALU.is_gt, fill=0.0, base=0,
                                    pattern=[[-1, P]], channel_multiplier=1)
            nc.gpsimd.affine_select(out=pick[:], in_=pick[:], compare_op=ALU.is_equal, fill=0.0, base=0,
                                    pattern=[[-1, H], [0, P]], channel_multiplier=1).then_inc(built, 1)
            bound = pool.to_reg(pl.NP - 1)

            def gather(out, table_in, idx):
                nc.gpsimd.indirect_dma_start(out=out, out_offset=None, in_=table_in[:, :],
                                             in_offset=bass.IndirectOffsetOnAxis(ap=idx[:, 0:1], axis=0),
                                             bounds_check=bound, oob_is_err=False).then_inc(fetched, 16)
            with pool.Fori(0, EC) as i:
                pool.wait_ge(done, reached(i, 0))
                nc.gpsimd.tensor_copy(isrc[:], con["edge_src"][:, bass.ds(i, 1)])
                nc.gpsimd.tensor_copy(idst[:], con["edge_dst"][:, bass.ds(i, 1)]).then_inc(done, 1)
                pool.wait_ge(done, reached(i, 1))
                pool.sem_inc(passed, 1)
                gather(rows[:, 0:RW], row_dram, isrc)
                gather(old[:], table, idst)
                if kind == "max":
                    gather(krow[:], ks_dram, idst)
                if kind == "weigh":
                    gather(topr[:], top_dram, idst)
                pool.wait_ge(fetched, i * (16 * gathers) + 16 * gathers)
                pool.sem_inc(done, 1)
                pool.wait_ge(done, reached(i, steps - 1))
                pool.sem_inc(passed, 1)
                nc.gpsimd.indirect_dma_start(out=table[:, :],
                                             out_offset=bass.IndirectOffsetOnAxis(ap=iput[:, 0:1], axis=0),
                                             in_=new[:], in_offset=None,
                                             bounds_check=bound, oob_is_err=False).then_inc(put, 16)
                pool.wait_ge(put, i * 16 + 16)
                pool.sem_inc(done, 1)

        @where(block.tensor, con, False)
        def _(pe):
            with pe.Fori(0, EC) as i:
                pe.wait_ge(done, reached(i, 3))
                nc.tensor.transpose(p_d[:, 0:P], wide[:], con["ident"][:]).then_inc(done, 1)
                if kind == "max":
                    pe.wait_ge(done, reached(i, 6))
                    nc.tensor.transpose(p_a[0:H, 0:P], s8[:], con["ident"][:]).then_inc(done, 1)
                    pe.wait_ge(done, reached(i, 8))
                    pe.sem_inc(passed, 1)
                    for h in range(H):
                        ins = nc.tensor.matmul((p_a if h < H // 2 else p_b)[:, (h % (H // 2)) * P:(h % (H // 2) + 1) * P],
                                               pick[:, h, :], s8T[:], start=True, stop=True)
                    ins.then_inc(done, 1)
                else:
                    pe.wait_ge(done, reached(i, 8 if kind == "weigh" else 5))
                    nc.tensor.matmul(p_a[:, 0:width], same[:], val[:] if kind == "weigh" else rows[:, 0:width],
                                     start=True, stop=True).then_inc(done, 1)

        @where(block.scalar, con, False)
        def _(act):
            if kind == "weigh":
                with act.Fori(0, EC) as i:
                    act.wait_ge(done, reached(i, 6))
                    nc.scalar.activation(s8[:], s8[:], ACT.Exp, scale=SCALE).then_inc(done, 1)

        @where(block.vector, con, False)
        def _(dve):
            V = nc.vector
            V.memset(val[:], 1.0)
            V.memset(fill[:], -NEG if kind == "max" else 0.0).then_inc(built, 1)
            heads = lambda v: v.rearrange("p (h d) -> p h d", h=H)
            n = [0]
            per = {"max": 9, "weigh": 6, "sum": 5}[kind]

            def body(i):
                n[0] = 0

                def then(ins):
                    n[0] += 1
                    ins.then_inc(dve_step, 1)
                    dve.wait_ge(dve_step, i * per + n[0])
                dve.wait_ge(done, reached(i, 2))
                then(V.tensor_copy(dstf[:], idst[:]))
                V.tensor_copy(wide[:], dstf[:].to_broadcast([P, P])).then_inc(done, 1)
                dve.wait_ge(done, reached(i, 4))
                then(V.tensor_scalar(same[:], p_d[:, 0:P], dstf[:, 0:1], None, ALU.is_equal))
                then(V.tensor_tensor(tmp[:], same[:], before[:], ALU.mult))
                then(V.tensor_reduce(cnt[:], tmp[:], AX.X, ALU.add))
                then(V.tensor_scalar(cnt[:], cnt[:], 0.5, float(SKIP), ALU.is_gt, ALU.mult))
                V.tensor_tensor(iput[:], cnt[:], dstf[:], ALU.add).then_inc(done, 1)
                if kind == "max":
                    dve.wait_ge(done, reached(i, 5))
                    then(V.tensor_tensor(prod[:], rows[:, 0:D], krow[:, 0:D], ALU.mult))
                    then(V.tensor_reduce(s8[:], heads(prod[:]), AX.X, ALU.add))
                    V.tensor_copy(scores[:, bass.ds(i * H, H)], s8[:])
                    V.tensor_scalar(tmp[:], same[:], -1.0, NEG, ALU.add, ALU.mult).then_inc(done, 1)
                    dve.wait_ge(done, reached(i, 7))
                    V.tensor_copy(s8T[:], p_a[0:H, 0:P]).then_inc(done, 1)
                    dve.wait_ge(done, reached(i, 9))
                    for j, bank in enumerate((p_a, p_b)):
                        for h in range(H // 2):
                            ins = V.tensor_tensor(big[:, j * (H // 2) + h, :], tmp[:], bank[:, h * P:(h + 1) * P], ALU.add)
                    then(ins)
                    then(V.tensor_reduce(new[:], big[:], AX.X, ALU.max))
                    V.tensor_tensor(new[:], new[:], old[:], ALU.max).then_inc(done, 1)
                elif kind == "weigh":
                    dve.wait_ge(done, reached(i, 5))
                    then(V.tensor_copy(s8[:], scores[:, bass.ds(i * H, H)]))
                    V.tensor_tensor(s8[:], s8[:], topr[:], ALU.subtract).then_inc(done, 1)
                    dve.wait_ge(done, reached(i, 7))
                    V.tensor_copy(val[:, D:D + H], s8[:])
                    V.tensor_tensor(heads(val[:, 0:D]), heads(rows[:, D:2 * D]), s8[:].to_broadcast([P, H, hd]),
                                    ALU.mult).then_inc(done, 1)
                    dve.wait_ge(done, reached(i, 9))
                    V.tensor_tensor(new[:], old[:], p_a[:, 0:width], ALU.add).then_inc(done, 1)
                else:
                    dve.wait_ge(done, reached(i, 6))
                    V.tensor_tensor(new[:], old[:], p_a[:, 0:width], ALU.add).then_inc(done, 1)
                return n[0]
            with dve.Fori(0, EC) as i:
                used = body(i)
            assert used == per, (kind, used)


def general_sums(nc, pl, con, signals, layer, h_in, acc):
    edge_pass(nc, pl, con, signals, f"esum{layer}", "sum", acc, acc.shape[1], h_in)
    clear_signals(nc, signals)


def general_attend(nc, pl, con, signals, x, w_out, b_out, qv_dram, ks_dram, mask_embed, top, acc, x1_dram, h_dram):
    D, C, H, hd = pl.D, pl.C, pl.H, pl.hd
    W = acc.shape[1]
    with ExitStack() as ctx:
        scores = ctx.enter_context(nc.sbuf_tensor("edge_scores", [P, pl.EC * H], F32))
        edge_pass(nc, pl, con, signals, "emax", "max", top, H, qv_dram, ks_dram=ks_dram, scores=scores)
        clear_signals(nc, signals)
        edge_pass(nc, pl, con, signals, "ewgh", "weigh", acc, W, qv_dram, top_dram=top, scores=scores)
        clear_signals(nc, signals)
    with ExitStack() as ctx:
        def sb(n, s, d=F32):
            return ctx.enter_context(nc.sbuf_tensor("gen_" + n, s, d))

        taken = []

        def sem(n):
            return lend(nc, signals, taken)
        wraw, wT, bias = sb("wraw", [P, C, D]), sb("wT", [P, C, D]), sb("bias", [P, D])
        at, xt, r, o, oT = sb("at", [P, W]), sb("xt", [P, D]), sb("r", [P, H]), sb("o", [P, D]), sb("oT", [P, D])
        x1, h, zero = sb("x1", [P, D]), sb("h", [P, D]), sb("zero", [P, D])
        st, mv, sd, rstd, nmr = sb("st", [P, 6]), sb("mv", [P, 2]), sb("sd", [P, 1]), sb("rstd", [P, 1]), sb("nmr", [P, 1])
        ps_t = ctx.enter_context(nc.psum_tensor("gen_ps_t", [P, 512], F32))
        ps_p = ctx.enter_context(nc.psum_tensor("gen_ps_p", [P, 512], F32))
        setup_in, clear, w_up, w_ready = sem("setup_in"), sem("clear"), sem("w_up"), sem("w_ready")
        done, dve_step, loaded, stored, passed = sem("done"), sem("dve_step"), sem("loaded"), sem("stored"), sem("passed")
        STEPS, PER = 10, 6
        whole, rest = pl.N // P, pl.N % P

        def reached(i, step):
            return i * STEPS + step + 1
        block = ctx.enter_context(nc.Block())

        @where(block.sync, con, False)
        def _(sp):
            for c in range(C):
                sp.dma_start(wraw[:, c, :], w_out[c * P:(c + 1) * P, :]).then_inc(setup_in, 16)
            sp.dma_start(bias[:], b_out.rearrange("(o d) -> o d", o=1).to_broadcast([P, D])).then_inc(setup_in, 16)
            sp.wait_ge(clear, 1)

            def tile(i, rows):
                sp.wait_ge(done, reached(i, 0))
                sp.dma_start(at[:], acc[bass.ds(i * P, P), :]).then_inc(loaded, 16)
                sp.dma_start(xt[0:rows, :], x[bass.ds(i * P, rows), :]).then_inc(loaded, 16)
                sp.wait_ge(loaded, i * 32 + 32)
                sp.sem_inc(done, 1)
                sp.wait_ge(done, reached(i, 9))
                sp.dma_start(x1_dram[bass.ds(i * P, P), :], x1[:]).then_inc(stored, 16)
                sp.dma_start(h_dram[bass.ds(i * P, P), :], h[:]).then_inc(stored, 16)
                sp.wait_ge(stored, i * 32 + 32)
                sp.sem_inc(done, 1)
            with sp.Fori(0, whole) as i:
                tile(i, P)
            if rest:
                tile(whole, rest)
            tiles = whole + (rest > 0)
            for t in range(tiles, pl.NT):
                sp.dma_start(x1_dram[t * P:(t + 1) * P, :], zero[:]).then_inc(stored, 16)
                sp.dma_start(h_dram[t * P:(t + 1) * P, :], zero[:]).then_inc(stored, 16)
            sp.wait_ge(stored, 32 * pl.NT)
            sp.dma_start(h_dram[0:1, :], mask_embed.rearrange("(o d) -> o d", o=1)).then_inc(stored, 16)
            sp.wait_ge(stored, 32 * pl.NT + 16)

        @where(block.tensor, con, False)
        def _(pe):
            pe.wait_ge(setup_in, 16 * (C + 1))
            for n in range(C * C):
                c, rr = n // C, n % C
                if n:
                    pe.wait_ge(w_ready, n)
                nc.tensor.transpose(ps_t[:, 0:P], wraw[:, c, rr * P:(rr + 1) * P], con["ident"][:]).then_inc(w_up, 1)
            pe.wait_ge(w_ready, C * C)

            def tile(i):
                pe.wait_ge(done, reached(i, 2))
                for c in range(C):
                    ins = nc.tensor.transpose(ps_t[:, c * P:(c + 1) * P], o[:, c * P:(c + 1) * P], con["ident"][:])
                ins.then_inc(done, 1)
                pe.wait_ge(done, reached(i, 4))
                for c in range(C):
                    ins = nc.tensor.matmul(ps_p[:, 0:D], oT[:, c * P:(c + 1) * P], wT[:, c, :],
                                           start=(c == 0), stop=(c == C - 1))
                ins.then_inc(done, 1)
            with pe.Fori(0, whole) as i:
                tile(i)
            if rest:
                tile(whole)

        @where(block.scalar, con, False)
        def _(act):
            for n in range(C * C):
                c, rr = n // C, n % C
                act.wait_ge(w_up, n + 1)
                nc.scalar.copy(wT[:, rr, c * P:(c + 1) * P], ps_t[:, 0:P]).then_inc(w_ready, 1)

            def tile(i):
                act.wait_ge(done, reached(i, 6))
                nc.scalar.activation(sd[:], mv[:, 1:2], ACT.Sqrt, bias=con["eps"][:, 0:1]).then_inc(done, 1)
                act.wait_ge(done, reached(i, 8))
                nc.scalar.activation(h[:], x1[:], ACT.Relu, bias=nmr[:, 0:1], scale=rstd[:, 0:1]).then_inc(done, 1)
            with act.Fori(0, whole) as i:
                tile(i)
            if rest:
                tile(whole)

        @where(block.vector, con, False)
        def _(dve):
            V = nc.vector
            V.memset(zero[:], 0.0)
            V.memset(con["deg"][:], 1.0)
            V.memset(xt[:], 0.0).then_inc(clear, 1)
            dve.wait_ge(setup_in, 16 * (C + 1))
            dve.sem_inc(done, 1)

            def tile(i):
                n = [0]

                def then(ins):
                    n[0] += 1
                    ins.then_inc(dve_step, 1)
                    dve.wait_ge(dve_step, i * PER + n[0])
                dve.wait_ge(done, reached(i, 1))
                then(V.tensor_scalar(r[:], at[:, D:D + H], 0.0, None, ALU.is_equal))
                then(V.tensor_tensor(r[:], r[:], at[:, D:D + H], ALU.add))
                then(V.reciprocal(r[:], r[:]))
                V.tensor_scalar(con["deg"][:, bass.ds(i, 1)], at[:, D + H:D + H + 1], 1.0, None, ALU.max)
                V.tensor_tensor(o[:].rearrange("p (h d) -> p h d", h=H), at[:, 0:D].rearrange("p (h d) -> p h d", h=H),
                                r[:].to_broadcast([P, H, hd]), ALU.mult).then_inc(done, 1)
                dve.wait_ge(done, reached(i, 3))
                V.tensor_copy(oT[:], ps_t[:, 0:D]).then_inc(done, 1)
                dve.wait_ge(done, reached(i, 5))
                then(V.tensor_tensor(x1[:], xt[:], bias[:], ALU.add))
                then(V.tensor_tensor(x1[:], x1[:], ps_p[:, 0:D], ALU.add))
                V.bn_stats(st[:], x1[:]).then_inc(passed, 1)
                dve.wait_ge(passed, i * 2 + 1)
                dve.sem_inc(passed, 1)
                V.bn_aggr(mv[:], st[:]).then_inc(done, 1)
                dve.wait_ge(done, reached(i, 7))
                then(V.reciprocal(rstd[:], sd[:]))
                V.scalar_tensor_tensor(out=nmr[:], in0=mv[:, 0:1], scalar=-1.0, in1=rstd[:],
                                       op0=ALU.mult, op1=ALU.mult).then_inc(done, 1)
                assert n[0] == PER, n
            with dve.Fori(0, whole) as i:
                tile(i)
            if rest:
                tile(whole)
            tiles = whole + (rest > 0)
            dve.wait_ge(done, reached(tiles - 1, STEPS))
            V.reciprocal(con["inv_deg"][:], con["deg"][:])

    clear_signals(nc, signals)


def aggregate(nc, pl, con, signals, layer, wl, wr, b, gamma, beta, rmean, rvar, h_in, h_next, x1_dram, sum_dram, out):
    D, C = pl.D, pl.C
    final = out is not None
    with ExitStack() as ctx:
        taken = []

        def name(n):
            return f"{n}_l{layer}"

        def sb(n, s, d=F32):
            return ctx.enter_context(nc.sbuf_tensor(name(n), s, d))

        def ps(n):
            return ctx.enter_context(nc.psum_tensor(name(n), [P, 512], F32))

        def sem(n):
            if n.startswith("rows_in"):
                return nc.alloc_semaphore(f"agg_{name(n)}")
            return lend(nc, signals, taken)
        wls, wrs = sb("wl", [P, C, D]), sb("wr", [P, C, D])
        wl_hi, wl_lo, wr_hi, wr_lo = (sb(n, [P, C, D], F32R) for n in ("wl_hi", "wl_lo", "wr_hi", "wr_lo"))
        par = sb("par", [P, 5, D])
        g, bias = sb("g", [P, D]), sb("bias", [P, D])
        hs = [sb(f"hs{u}", [P, QT, D]) for u in range(2)]
        xs = [sb(f"xs{u}", [P, QT, D]) for u in range(2)]
        rows = [sb(f"rows{u}", [P, QT, D]) for u in range(2)]
        hot = [sb(f"hot{u}", [P, QT, P]) for u in range(2)]
        res = [sb(f"res{u}", [P, QT, D]) for u in range(2)]
        lidx, ldst, ideg = sb("lidx", [P, 2, QT], I32), sb("ldst", [P, 2, QT]), sb("ideg", [P, 2, QT])
        hT_hi, hT_lo, aT_hi, aT_lo = (sb(n, [P, 2, 2 * D], F32R) for n in ("hT_hi", "hT_lo", "aT_hi", "aT_lo"))
        hT, aT, z = sb("hT", [P, 2, 2 * D]), sb("aT", [P, 2, 2 * D]), sb("z", [P, 2, 2, D])
        ps_h, ps_a, ps_zl, ps_zr = [[ps(f"{n}{v}") for v in range(2)] for n in ("ps_h", "ps_a", "ps_zl", "ps_zr")]
        par_in, std_ready, fold, weights_ready = sem("par_in"), sem("std_ready"), sem("fold"), sem("weights_ready")
        bufs_clear, staged, hot_ready = sem("bufs_clear"), sem("staged"), sem("hot_ready")
        gap_ready, square_ready = sem("gap_ready"), sem("square_ready")
        passed = sem("passed")
        rows_in, res_out = ([sem(f"{n}{u}") for u in range(2)] for n in ("rows_in", "res_out"))
        hs_in, xs_in = ([sem(f"{n}{j}") for j in range(BODY // 2)] for n in ("hs_in", "xs_in"))
        folded, hi_ready = sem("folded"), sem("hi_ready")
        h_up, a_up, hT_hi_ready, hT_ready, sum_ready, aT_hi_ready, aT_ready = (
            sem("h_up"), sem("a_up"), sem("hT_hi_ready"), sem("hT_ready"), sem("sum_ready"), sem("aT_hi_ready"), sem("aT_ready"))
        z_up, z_scaled, z_read, z_own, pair_done = sem("z_up"), sem("z_scaled"), sem("z_read"), sem("z_own"), sem("pair_done")
        ideg_ready, tail_io = sem("ideg_ready"), sem("tail_io")
        PAIRS = BODY // 2
        block = ctx.enter_context(nc.Block())
        last = pl.turns - 1

        @block.sync
        def _(sp):
            for c in range(C):
                sp.dma_start(wls[:, c, :], wl[c * P:(c + 1) * P, :]).then_inc(par_in, 16)
                sp.dma_start(wrs[:, c, :], wr[c * P:(c + 1) * P, :]).then_inc(par_in, 16)
            for j, v in enumerate((b, gamma, beta, rmean, rvar)):
                sp.dma_start(par[:, j, :], v.to_broadcast([P, D])).then_inc(par_in, 16)
            for u in range(2):
                sp.sem_inc(res_out[u], 16)

            def load(i, j):
                sp.wait_ge(pair_done, i * PAIRS + j + 1)
                at, mine = i * (BODY * P) + j * (2 * P), slice(2 * (j % 2), 2 * (j % 2) + 2)
                sp.dma_start(hs[j // 2][:, mine, :], h_in[bass.ds(at, 2 * P), :].rearrange("(t p) d -> p t d", p=P)
                             ).then_inc(hs_in[j], 16)
                if final:
                    sp.dma_start(xs[j // 2][:, mine, :],
                                 x1_dram[bass.ds(at, 2 * P), :].rearrange("(t p) d -> p t d", p=P)).then_inc(xs_in[j], 16)

            def store(i, u):
                sp.wait_ge(pair_done, 2 * (2 * i + u) + 6)
                sp.dma_start(quad_rows(out if final else h_next, i * (BODY * P) + u * pl.QR),
                             res[u][:]).then_inc(res_out[u], 16)
            for j in range(PAIRS):
                load(0, j)
            with sp.Fori(0, last) as i:
                for j in range(PAIRS):
                    load(i + 1, j)
                    if j % 2:
                        store(i, j // 2)
            store(last, 0)
            if final:
                sp.wait_ge(pair_done, 2 * (2 * last + 1) + 6)
                parts = ragged(out, last * BODY * P + pl.QR, pl.last_rows, res[1])
                for dram, tile in parts:
                    sp.dma_start(dram, tile).then_inc(tail_io, 16)
                sp.wait_ge(tail_io, 16 * len(parts))
            else:
                store(last, 1)
            sp.wait_ge(res_out[0], 16 * (pl.turns + 1))
            sp.wait_ge(res_out[1], 16 * (pl.turns + (0 if final else 1)))

        @block.gpsimd
        def _(pool):
            for u in range(2):
                ins = nc.gpsimd.memset(rows[u][:], 0.0)
            ins.then_inc(bufs_clear, 1)
            pool.wait_ge(bufs_clear, 1)
            bound = pool.to_reg(pl.NP - 1)

            def fetch(i, u):
                q = 2 * i + u
                pool.wait_ge(a_up, 2 * q + 2)
                nc.gpsimd.tensor_copy(lidx[:, u, :], con["links"][:, bass.ds(i * BODY + u * QT, QT), 0])
                nc.gpsimd.tensor_copy(ldst[:, u, :], con["dloc"][:, bass.ds(i * BODY + u * QT, QT)]).then_inc(staged, 1)
                pool.wait_ge(staged, q + 1)
                nc.gpsimd.tensor_tensor(hot[u][:], con["iota"][:], ldst[:, u, :].to_broadcast([P, QT, P]),
                                        ALU.subtract).then_inc(gap_ready, 1)
                for t in range(QT):
                    nc.gpsimd.indirect_dma_start(
                        out=rows[u][:, t, :], out_offset=None, in_=h_in[:, :],
                        in_offset=bass.IndirectOffsetOnAxis(ap=lidx[:, u, t:t + 1], axis=0),
                        bounds_check=bound, oob_is_err=False).then_inc(rows_in[u], 16)

            def fetch_sums(i, u):
                q = 2 * i + u
                pool.wait_ge(a_up, 2 * q + 2)
                pool.sem_inc(passed, 1)
                for t in range(QT):
                    ins = nc.gpsimd.tensor_scalar(hot[u][:, t, :], con["ident"][:], -1.0, 1.0, ALU.mult, ALU.add)
                ins.then_inc(gap_ready, 1)
                nc.gpsimd.dma_start(rows[u][:], quad_rows(sum_dram, i * (BODY * P) + u * pl.QR)
                                    ).then_inc(rows_in[u], 16 * QT)
            flag = pool.value_load(con["flag"][0:1, 0:1], min_val=0, max_val=1)
            with pool.If(flag > 0):
                with pool.Fori(0, pl.turns) as i:
                    fetch(i, 0)
                    fetch(i, 1)
            with pool.Else():
                with pool.Fori(0, pl.turns) as i:
                    fetch_sums(i, 0)
                    fetch_sums(i, 1)

        @block.tensor
        def _(pe):
            pe.wait_ge(weights_ready, 1)
            pe.sem_inc(a_up, 4)

            def up(i, j):
                u, m, q = j // 2, i * PAIRS + j, 2 * i + j // 2
                pe.wait_ge(hs_in[j], i * 16 + 16)
                pe.wait_ge(sum_ready, m + 1)
                for t in range(2):
                    for c in range(C):
                        at = t * D + c * P
                        ins = nc.tensor.transpose(ps_h[j % 2][:, at:at + P], hs[u][:, 2 * (j % 2) + t, c * P:(c + 1) * P],
                                                  con["ident"][:])
                ins.then_inc(h_up, 1)
                if j % 2 == 0:
                    pe.wait_ge(hot_ready, q + 1)
                    pe.wait_ge(rows_in[u], i * (16 * QT) + 16 * QT)
                for t in range(2):
                    for c in range(C):
                        at = t * D + c * P
                        ins = nc.tensor.matmul(ps_a[j % 2][:, at:at + P], rows[u][:, 2 * (j % 2) + t, c * P:(c + 1) * P],
                                               hot[u][:, 2 * (j % 2) + t, :], start=True, stop=True)
                ins.then_inc(a_up, 1)

            def product(bank, b, hi, lo, w_hi, w_lo):
                for t in range(2):
                    for c in range(C):
                        part = slice(t * D + c * P, t * D + (c + 1) * P)
                        region = bank[:, t * D:(t + 1) * D]
                        nc.tensor.matmul(region, hi[:, b, part], w_hi[:, c, :], start=(c == 0), stop=False)
                        nc.tensor.matmul(region, hi[:, b, part], w_lo[:, c, :], start=False, stop=False)
                        ins = nc.tensor.matmul(region, lo[:, b, part], w_hi[:, c, :], start=False, stop=(c == C - 1))
                return ins

            def dense(i, j):
                m, b = i * PAIRS + j, j % 2
                pe.wait_ge(hT_ready, m + 1)
                pe.wait_ge(z_read, m + 1)
                product(ps_zr[b], b, hT_hi, hT_lo, wr_hi, wr_lo)
                pe.wait_ge(aT_ready, m + 1)
                product(ps_zl[b], b, aT_hi, aT_lo, wl_hi, wl_lo).then_inc(z_up, 1)
            up(0, 0)

            def turn(i, end):
                for j in range(PAIRS):
                    if j < PAIRS - 1:
                        up(i, j + 1)
                    elif not end:
                        up(i + 1, 0)
                    dense(i, j)
            with pe.Fori(0, last) as i:
                turn(i, False)
            turn(last, True)

        @block.scalar
        def _(act):
            act.wait_ge(par_in, 16 * (2 * C + 5))
            nc.scalar.activation(g[:], par[:, 4, :], ACT.Sqrt, bias=con["eps"][:, 0:1]).then_inc(std_ready, 1)
            act.wait_ge(folded, 1)
            nc.scalar.copy(wl_hi[:], wls[:])
            nc.scalar.copy(wr_hi[:], wrs[:]).then_inc(hi_ready, 1)

            def keep(i, j):
                m, b = i * PAIRS + j, j % 2
                act.wait_ge(h_up, m + 1)
                act.wait_ge(z_up, m + 1)
                nc.scalar.copy(hT_hi[:, b, :], ps_h[b][:, :])
                nc.scalar.copy(hT[:, b, :], ps_h[b][:, :]).then_inc(hT_hi_ready, 1)
                act.wait_ge(sum_ready, m + 3)
                nc.scalar.copy(aT_hi[:, b, :], aT[:, b, :]).then_inc(aT_hi_ready, 1)

            def finish_hot(i, u):
                q = 2 * i + u
                gap = hot[u][:].rearrange("p t e -> p (t e)")
                act.wait_ge(gap_ready, q + 1)
                nc.scalar.activation(gap, gap, ACT.Square).then_inc(square_ready, 1)
                act.wait_ge(square_ready, q + 1)
                nc.scalar.activation(gap, gap, ACT.Relu, bias=con["ones"][:, 0:1], scale=-1.0).then_inc(hot_ready, 1)

            def turn(i, end):
                for j in range(PAIRS):
                    if j == 0:
                        finish_hot(i, 1)
                    keep(i, j)
                    if j == 2 and not end:
                        finish_hot(i + 1, 0)
            finish_hot(0, 0)
            with act.Fori(0, last) as i:
                turn(i, False)
            turn(last, True)

        @block.vector
        def _(dve):
            V = nc.vector
            dve.wait_ge(par_in, 16 * (2 * C + 5))
            dve.wait_ge(std_ready, 1)
            V.tensor_tensor(bias[:], par[:, 0, :], par[:, 3, :], ALU.subtract)
            V.reciprocal(g[:], g[:]).then_inc(fold, 1)
            dve.wait_ge(fold, 1)
            V.tensor_tensor(g[:], g[:], par[:, 1, :], ALU.mult).then_inc(fold, 1)
            dve.wait_ge(fold, 2)
            V.tensor_tensor(bias[:], bias[:], g[:], ALU.mult).then_inc(fold, 1)
            for w in (wls, wrs):
                for c in range(C):
                    ins = V.tensor_tensor(w[:, c, :], w[:, c, :], g[:], ALU.mult)
            ins.then_inc(folded, 1)
            dve.wait_ge(fold, 3)
            V.tensor_tensor(bias[:], bias[:], par[:, 2, :], ALU.add).then_inc(fold, 1)
            dve.wait_ge(hi_ready, 1)
            V.tensor_tensor(wl_lo[:], wls[:], wl_hi[:].bitcast(F32), ALU.subtract)
            V.tensor_tensor(wr_lo[:], wrs[:], wr_hi[:].bitcast(F32), ALU.subtract).then_inc(weights_ready, 1)
            dve.wait_ge(fold, 4)
            dve.sem_inc(sum_ready, 2)
            dve.sem_inc(z_up, 2)
            dve.sem_inc(z_read, 2)
            dve.sem_inc(pair_done, 4)

            def split_h(i, j):
                m, b = i * PAIRS + j, j % 2
                dve.wait_ge(hT_hi_ready, m + 1)
                V.tensor_tensor(hT_lo[:, b, :], hT[:, b, :], hT_hi[:, b, :].bitcast(F32), ALU.subtract).then_inc(hT_ready, 1)

            def add_own(i, j, regular):
                m, b = i * PAIRS + j, j % 2
                dve.wait_ge(a_up, m + 5)
                if regular:
                    V.tensor_tensor(aT[:, b, :], hT[:, b, :], ps_a[b][:, :], ALU.add).then_inc(sum_ready, 1)
                else:
                    V.tensor_copy(aT[:, b, :], ps_a[b][:, :]).then_inc(sum_ready, 1)

            def split_sum(i, j):
                m, b = i * PAIRS + j, j % 2
                dve.wait_ge(aT_hi_ready, m + 1)
                V.tensor_tensor(aT_lo[:, b, :], aT[:, b, :], aT_hi[:, b, :].bitcast(F32), ALU.subtract).then_inc(aT_ready, 1)

            def combine(i, j):
                u, b, m, q = j // 2, j % 2, i * PAIRS + j, 2 * i + j // 2
                if b == 0:
                    V.tensor_copy(ideg[:, u, :], con["inv_deg"][:, bass.ds(i * BODY + u * QT, QT)]).then_inc(ideg_ready, 1)
                    dve.wait_ge(ideg_ready, q + 1)
                dve.wait_ge(z_up, m + 3)
                for t in range(2):
                    ins = V.scalar_tensor_tensor(out=z[:, b, t, :], in0=ps_zl[b][:, t * D:(t + 1) * D],
                                                 scalar=ideg[:, u, 2 * b + t:2 * b + t + 1], in1=bias[:],
                                                 op0=ALU.mult, op1=ALU.add)
                ins.then_inc(z_scaled, 1)
                dve.wait_ge(z_scaled, m + 1)
                V.tensor_tensor(z[:, b, :, :], z[:, b, :, :], ps_zr[b][:, :].rearrange("p (t d) -> p t d", t=2),
                                ALU.add).then_inc(z_read, 1)

            def close(i, j):
                u, b, m = j // 2, j % 2, i * PAIRS + j
                if b == 0:
                    dve.wait_ge(res_out[u], i * 16 + 16)
                if final:
                    dve.wait_ge(xs_in[j], i * 16 + 16)
                dve.wait_ge(z_read, m + 3)
                mine, result = hs[u][:, 2 * b:2 * b + 2, :], res[u][:, 2 * b:2 * b + 2, :]
                if final:
                    V.tensor_tensor(z[:, b, :, :], z[:, b, :, :], mine, ALU.add).then_inc(z_own, 1)
                    dve.wait_ge(z_own, m + 1)
                    V.tensor_tensor(result, z[:, b, :, :], xs[u][:, 2 * b:2 * b + 2, :], ALU.add).then_inc(pair_done, 1)
                else:
                    V.scalar_tensor_tensor(out=result, in0=z[:, b, :, :], scalar=0.0, in1=mine,
                                           op0=ALU.max, op1=ALU.add).then_inc(pair_done, 1)

            def turn(i, end, regular):
                for j in range(PAIRS):
                    following = (i, j + 1) if j < PAIRS - 1 else None if end else (i + 1, 0)
                    if following:
                        split_h(*following)
                        add_own(*following, regular)
                    combine(i, j)
                    if following:
                        split_sum(*following)
                    close(i, j)

            def run(regular):
                split_h(0, 0)
                add_own(0, 0, regular)
                split_sum(0, 0)
                with dve.Fori(0, last) as i:
                    turn(i, False, regular)
                turn(last, True, regular)
            flag = dve.value_load(con["flag"][0:1, 0:1], min_val=0, max_val=1)
            with dve.If(flag > 0):
                run(True)
            with dve.Else():
                run(False)


def program(nc, x, src, dst, Wq, bq, Wk, bk, Wv, bv, Wo, bo, mask_embed, Wl, Wr, b, gamma, beta, rmean, rvar, out):
    N, D = x.shape
    pl = Plan(N, src.shape[0], D, 8)
    KW = D + pl.H
    qv = nc.dram_tensor("qv_rows", (pl.NP, 2 * D), F32, kind="Internal").ap()
    ks = nc.dram_tensor("k_rows", (pl.NP, KW), F32, kind="Internal").ap()
    links = nc.dram_tensor("link_table", (P * pl.NT, 2), I32, kind="Internal").ap()
    x1 = nc.dram_tensor("x1_rows", (pl.NP, D), F32, kind="Internal").ap()
    hbuf = [nc.dram_tensor(f"h_rows{j}", (pl.NP, D), F32, kind="Internal").ap() for j in range(2)]
    top = nc.dram_tensor("top_rows", (pl.NP, pl.H), F32, kind="Internal").ap()
    acc = nc.dram_tensor("sum_rows", (pl.NP, D + pl.H + 8), F32, kind="Internal").ap()
    with ExitStack() as ctx:
        con = constants(nc, ctx, pl)
        with ExitStack() as edges:
            idx = edges.enter_context(nc.sbuf_tensor("edge_rows", [P, pl.EB], I32))
            pay = edges.enter_context(nc.sbuf_tensor("edge_pay", [P, pl.EB, 2], I32))
            edge_tables(nc, pl, con, src, dst, links, idx, pay)
            project(nc, pl, con, x, (Wq, Wv, Wk), (bq, bv, bk), qv, ks, links, idx, pay)
        attend(nc, pl, con, x, Wo, bo, qv, ks, links, mask_embed, x1, hbuf[0])
        signals = []
        general_attend(nc, pl, con, signals, x, Wo, bo, qv, ks, mask_embed, top, acc, x1, hbuf[0])
        L = Wl.shape[0]
        for l in range(L):
            vec = [v[l:l + 1, :] for v in (b, gamma, beta, rmean, rvar)]
            if l:
                clear_signals(nc, signals)
            general_sums(nc, pl, con, signals, l, hbuf[l % 2], acc)
            aggregate(nc, pl, con, signals, l, Wl[l], Wr[l], *vec, hbuf[l % 2], hbuf[(l + 1) % 2], x1, acc[:, 0:D],
                      out if l == L - 1 else None)


INPUTS = ['x', 'src', 'dst', 'L0_gnn_Wq', 'L0_gnn_bq', 'L0_gnn_Wk', 'L0_gnn_bk', 'L0_gnn_Wv', 'L0_gnn_bv',
          'L0_gnn_Wo', 'L0_gnn_bo', 'L1_gnn_mask_embed', 'L1_gnn_Wl', 'L1_gnn_Wr', 'L1_gnn_b', 'L1_gnn_gamma',
          'L1_gnn_beta', 'L1_gnn_rmean', 'L1_gnn_rvar']


def kernel(**inputs):
    import concourse.bacc as bacc
    import numpy as np
    from concourse.bass_utils import run_bass_kernel_spmd

    nc = bacc.Bacc("TRN2", target_bir_lowering=False, num_devices=1)
    arrays, args = {}, []
    for name in INPUTS:
        a = np.ascontiguousarray(inputs[name])
        arrays[f"in_{name}"] = a
        args.append(nc.dram_tensor(f"in_{name}", a.shape, mybir.dt.from_np(a.dtype), kind="ExternalInput").ap())
    out = nc.dram_tensor("out_x", inputs["x"].shape, F32, kind="ExternalOutput").ap()
    program(nc, *args, out)
    r = run_bass_kernel_spmd(nc, [arrays], core_ids=[0])
    return r.results[0]["out_x"]
```
